# Optimizing a Trainium2 kernel written in Bass

```python
import numpy as np
import jax
import jax.numpy as jnp

def _softmax(x, axis=-1):
    return jax.nn.softmax(x, axis=axis)

def _gelu(x):
    return jax.nn.gelu(x, approximate=True)

def _silu(x):
    return jax.nn.silu(x)

def _sigmoid(x):
    return jax.nn.sigmoid(x)

def _layernorm(x, axis=-1, eps=1e-05):
    m = jnp.mean(x, axis=axis, keepdims=True)
    v = jnp.var(x, axis=axis, keepdims=True)
    return (x - m) / jnp.sqrt(v + eps)

def _scatter_add(tgt, idx, src, axis=0):
    return tgt.at[idx].add(src)

def _segment_sum(src, seg, n):
    return jax.ops.segment_sum(src, seg, n)
kernel_name = 'mk_xattn_ffn_d2_seqx_r8_daf3b9'

def setup_inputs(seed: int=0):
    np.random.seed(seed)
    _w = jnp.asarray

    def _rec_inputs():
        import jax
        import jax.numpy as jnp
        _rk = jax.random.key(seed)
        x = -0.0005207 + 1.001 * jax.random.normal(jax.random.fold_in(_rk, 1), (16, 64, 512), jnp.float32)
        _lenS = 64 - jax.random.randint(jax.random.fold_in(_rk, 7), (16,), 0, max(1, 64 // 4) + 1, jnp.int32)
        _lenS2 = 64 - jax.random.randint(jax.random.fold_in(_rk, 8), (16,), 0, max(1, 64 // 4) + 1, jnp.int32)
        _ctx_4096P = jax.random.normal(jax.random.fold_in(_rk, 11), (16, 16, 512), jnp.float32)
        _ctx_4096c = jax.random.dirichlet(jax.random.fold_in(_rk, 511), 0.3 * jnp.ones((16,), jnp.float32), (16, 64))
        _ctx_4096t = jnp.einsum('bsk,bkd->bsd', _ctx_4096c, _ctx_4096P)
        _ctx_4096t = _ctx_4096t * jax.lax.rsqrt(jnp.mean(jnp.square(_ctx_4096t)) + 1e-12) * 0.953939
        ctx_4096 = -0.00010331 + 0.999899 * (_ctx_4096t + 0.3 * jax.random.normal(jax.random.fold_in(_rk, 611), (16, 64, 512), jnp.float32))
        return (x, ctx_4096)
    x, ctx_4096 = _rec_inputs()

    def _L0_xattn_setup():
        import jax, jax.numpy as jnp
        import numpy as np
        HEADS = 32
        KV_HEADS = 8
        HEAD_DIM = 128
        EPS = 1e-06

        def rms_norm(x, w):
            var = jnp.mean(jnp.square(x.astype(jnp.float32)), axis=-1, keepdims=True)
            return (x.astype(jnp.float32) * jax.lax.rsqrt(var + EPS)).astype(x.dtype) * w
        key = jax.random.key(seed)
        ks = jax.random.split(key, 6)
        bsz, n_lat, seq, hidden = (8, 64, 512, 512)
        return {'latents': jax.random.normal(ks[0], (bsz, n_lat, hidden), jnp.float32), 'context': jax.random.normal(ks[1], (bsz, seq, hidden), jnp.float32), 'Wq': jax.random.normal(ks[2], (hidden, HEADS * HEAD_DIM), jnp.float32) * 0.02, 'Wk': jax.random.normal(ks[3], (hidden, KV_HEADS * HEAD_DIM), jnp.float32) * 0.02, 'Wv': jax.random.normal(ks[4], (hidden, KV_HEADS * HEAD_DIM), jnp.float32) * 0.02, 'Wo': jax.random.normal(ks[5], (HEADS * HEAD_DIM, hidden), jnp.float32) * 0.02, 'q_norm_w': jnp.ones((HEAD_DIM,), jnp.float32), 'k_norm_w': jnp.ones((HEAD_DIM,), jnp.float32)}
    _L0_xattn_all = _L0_xattn_setup()
    _L0_xattn_in = {k: v for k, v in _L0_xattn_all.items() if k in ('Wq', 'Wk', 'Wv', 'Wo', 'q_norm_w', 'k_norm_w')}
    del _L0_xattn_all

    def _L0_ffn_setup():
        import jax, jax.numpy as jnp
        import numpy as np
        HID = 512
        INTER = 1376
        BITS = 4
        PACK = 8
        MAXQ = 15
        GROUP = 128

        def _dequant(qweight, scales, qzeros, g_idx):
            shifts = jnp.arange(PACK, dtype=jnp.uint32) * BITS
            qw = qweight.astype(jnp.uint32)
            w = (qw[:, None, :] >> shifts[None, :, None] & MAXQ).reshape(-1, qweight.shape[1])
            qz = qzeros.astype(jnp.uint32)
            z = ((qz[:, :, None] >> shifts[None, None, :] & MAXQ) + 1).reshape(qzeros.shape[0], -1)
            s = scales[g_idx]
            return (w.astype(scales.dtype) - z[g_idx].astype(scales.dtype)) * s
        key = jax.random.key(seed)
        ks = jax.random.split(key, 16)

        def qw(k, K, N):
            return jax.random.randint(k, (K // PACK, N), 0, 2147483647, dtype=jnp.int32)

        def qz(k, G, N):
            return jax.random.randint(k, (G, N // PACK), 0, 2147483647, dtype=jnp.int32)

        def sc(k, G, N):
            return jax.random.uniform(k, (G, N), jnp.float32, 0.001, 0.01)
        Gk = HID // GROUP
        Gd = INTER // GROUP
        return {'x': jax.random.normal(ks[0], (4, 256, HID), jnp.float32), 'gate_qweight': qw(ks[1], HID, INTER), 'gate_scales': sc(ks[2], Gk, INTER), 'gate_qzeros': qz(ks[3], Gk, INTER), 'gate_g_idx': (jnp.arange(HID) // GROUP).astype(jnp.int32), 'up_qweight': qw(ks[4], HID, INTER), 'up_scales': sc(ks[5], Gk, INTER), 'up_qzeros': qz(ks[6], Gk, INTER), 'up_g_idx': (jnp.arange(HID) // GROUP).astype(jnp.int32), 'down_qweight': qw(ks[7], INTER, HID), 'down_scales': sc(ks[8], Gd, HID), 'down_qzeros': qz(ks[9], Gd, HID), 'down_g_idx': (jnp.arange(INTER) // GROUP).astype(jnp.int32)}
    _L0_ffn_all = _L0_ffn_setup()
    _L0_ffn_in = {k: v for k, v in _L0_ffn_all.items() if k in ('gate_qweight', 'gate_scales', 'gate_qzeros', 'gate_g_idx', 'up_qweight', 'up_scales', 'up_qzeros', 'up_g_idx', 'down_qweight', 'down_scales', 'down_qzeros', 'down_g_idx')}
    del _L0_ffn_all

    def _L1_xattn_setup():
        import jax, jax.numpy as jnp
        import numpy as np
        B, C, N = (8, 64, 512)
        key = jax.random.key(seed)
        k1, k2, k3 = jax.random.split(key, 3)
        k = jax.random.normal(k1, (B, C, N), dtype=jnp.float32)
        q = jax.random.normal(k2, (B, C, N), dtype=jnp.float32)
        v = jax.random.normal(k3, (B, C, N), dtype=jnpp.float32) if False else jax.random.normal(k3, (B, C, N), dtype=jnp.float32)
        return {'k': k, 'q': q, 'v': v}
    _L1_xattn_all = _L1_xattn_setup()
    _L1_xattn_in = {k: v for k, v in _L1_xattn_all.items() if k in ()}
    del _L1_xattn_all

    def _L1_ffn_setup():
        import jax, jax.numpy as jnp
        import numpy as np
        import math
        B, S, IN, OUT = (4, 256, 512, 512)
        E, R, K = (8, 64, 128)
        SCALE = 64.0 / 64.0
        MULTIPLIER = 1.0
        key = jax.random.key(seed)
        ks = jax.random.split(key, 6)
        return {'x': jax.random.normal(ks[0], (B, S, IN), jnp.float32), 'W_org': jax.random.normal(ks[1], (OUT, IN), jnp.float32) * 0.02, 'lora_down': jax.random.normal(ks[2], (E, IN, R), jnp.float32) * 0.02, 'lora_up': jax.random.normal(ks[3], (E, R, OUT), jnp.float32) * 0.02, 'lora_keys': jax.random.normal(ks[4], (E, K), jnp.float32), 'Wq': jax.random.normal(ks[5], (K, IN), jnp.float32) * 0.02}
    _L1_ffn_all = _L1_ffn_setup()
    _L1_ffn_in = {k: v for k, v in _L1_ffn_all.items() if k in ('W_org', 'lora_down', 'lora_up', 'lora_keys', 'Wq')}
    del _L1_ffn_all
    return {'x': x, 'ctx_4096': ctx_4096, 'L0_xattn_Wq': _L0_xattn_in['Wq'], 'L0_xattn_Wk': _L0_xattn_in['Wk'], 'L0_xattn_Wv': _L0_xattn_in['Wv'], 'L0_xattn_Wo': _L0_xattn_in['Wo'], 'L0_xattn_q_norm_w': _L0_xattn_in['q_norm_w'], 'L0_xattn_k_norm_w': _L0_xattn_in['k_norm_w'], 'L0_ffn_gate_qweight': _L0_ffn_in['gate_qweight'], 'L0_ffn_gate_scales': _L0_ffn_in['gate_scales'], 'L0_ffn_gate_qzeros': _L0_ffn_in['gate_qzeros'], 'L0_ffn_gate_g_idx': _L0_ffn_in['gate_g_idx'], 'L0_ffn_up_qweight': _L0_ffn_in['up_qweight'], 'L0_ffn_up_scales': _L0_ffn_in['up_scales'], 'L0_ffn_up_qzeros': _L0_ffn_in['up_qzeros'], 'L0_ffn_up_g_idx': _L0_ffn_in['up_g_idx'], 'L0_ffn_down_qweight': _L0_ffn_in['down_qweight'], 'L0_ffn_down_scales': _L0_ffn_in['down_scales'], 'L0_ffn_down_qzeros': _L0_ffn_in['down_qzeros'], 'L0_ffn_down_g_idx': _L0_ffn_in['down_g_idx'], 'L1_ffn_W_org': _L1_ffn_in['W_org'], 'L1_ffn_lora_down': _L1_ffn_in['lora_down'], 'L1_ffn_lora_up': _L1_ffn_in['lora_up'], 'L1_ffn_lora_keys': _L1_ffn_in['lora_keys'], 'L1_ffn_Wq': _L1_ffn_in['Wq']}

def reference(x, ctx_4096, L0_xattn_Wq, L0_xattn_Wk, L0_xattn_Wv, L0_xattn_Wo, L0_xattn_q_norm_w, L0_xattn_k_norm_w, L0_ffn_gate_qweight, L0_ffn_gate_scales, L0_ffn_gate_qzeros, L0_ffn_gate_g_idx, L0_ffn_up_qweight, L0_ffn_up_scales, L0_ffn_up_qzeros, L0_ffn_up_g_idx, L0_ffn_down_qweight, L0_ffn_down_scales, L0_ffn_down_qzeros, L0_ffn_down_g_idx, L1_ffn_W_org, L1_ffn_lora_down, L1_ffn_lora_up, L1_ffn_lora_keys, L1_ffn_Wq):
    import jax
    import jax.numpy as jnp

    def _L0_xattn_ref(latents, context, Wq, Wk, Wv, Wo, q_norm_w, k_norm_w):
        import jax, jax.numpy as jnp
        import numpy as np
        HEADS = 32
        KV_HEADS = 8
        HEAD_DIM = 128
        EPS = 1e-06

        def rms_norm(x, w):
            var = jnp.mean(jnp.square(x.astype(jnp.float32)), axis=-1, keepdims=True)
            return (x.astype(jnp.float32) * jax.lax.rsqrt(var + EPS)).astype(x.dtype) * w
        bsz, q_len, hidden = latents.shape
        kv = jnp.concatenate([context, latents], axis=1)
        kv_len = kv.shape[1]
        groups = HEADS // KV_HEADS
        q = (latents @ Wq).reshape(bsz, q_len, HEADS, HEAD_DIM).transpose(0, 2, 1, 3)
        k = (kv @ Wk).reshape(bsz, kv_len, KV_HEADS, HEAD_DIM).transpose(0, 2, 1, 3)
        v = (kv @ Wv).reshape(bsz, kv_len, KV_HEADS, HEAD_DIM).transpose(0, 2, 1, 3)
        q = rms_norm(q, q_norm_w)
        k = rms_norm(k, k_norm_w)
        qg = q.reshape(bsz, KV_HEADS, groups, q_len, HEAD_DIM)
        scale = 1.0 / np.sqrt(HEAD_DIM)
        scores = jnp.einsum('bhgqd,bhkd->bhgqk', qg, k) * scale
        probs = jax.nn.softmax(scores.astype(jnp.float32), axis=-1).astype(q.dtype)
        out = jnp.einsum('bhgqk,bhkd->bhgqd', probs, v)
        out = out.reshape(bsz, HEADS, q_len, HEAD_DIM).transpose(0, 2, 1, 3)
        out = out.reshape(bsz, q_len, HEADS * HEAD_DIM)
        return out @ Wo

    def _L0_ffn_ref(x, gate_qweight, gate_scales, gate_qzeros, gate_g_idx, up_qweight, up_scales, up_qzeros, up_g_idx, down_qweight, down_scales, down_qzeros, down_g_idx):
        import jax, jax.numpy as jnp
        import numpy as np
        HID = 512
        INTER = 1376
        BITS = 4
        PACK = 8
        MAXQ = 15
        GROUP = 128

        def _dequant(qweight, scales, qzeros, g_idx):
            shifts = jnp.arange(PACK, dtype=jnp.uint32) * BITS
            qw = qweight.astype(jnp.uint32)
            w = (qw[:, None, :] >> shifts[None, :, None] & MAXQ).reshape(-1, qweight.shape[1])
            qz = qzeros.astype(jnp.uint32)
            z = ((qz[:, :, None] >> shifts[None, None, :] & MAXQ) + 1).reshape(qzeros.shape[0], -1)
            s = scales[g_idx]
            return (w.astype(scales.dtype) - z[g_idx].astype(scales.dtype)) * s
        Wg = _dequant(gate_qweight, gate_scales, gate_qzeros, gate_g_idx)
        Wu = _dequant(up_qweight, up_scales, up_qzeros, up_g_idx)
        Wd = _dequant(down_qweight, down_scales, down_qzeros, down_g_idx)
        xf = x.reshape(-1, x.shape[-1])
        h = jax.nn.silu(xf @ Wg) * (xf @ Wu)
        out = h @ Wd
        return out.reshape(x.shape[:-1] + (Wd.shape[1],))

    def _L1_xattn_ref(k, q, v):
        import jax, jax.numpy as jnp
        import numpy as np
        B, C, N = (8, 64, 512)
        input_dim = k.shape[1]
        scores = jnp.einsum('bcn,bcm->bnm', k, q) / jnp.sqrt(jnp.float32(input_dim))
        attn = jax.nn.softmax(scores, axis=-1)
        out = jnp.einsum('bnm,bcm->bcn', attn, v)
        return out

    def _L1_ffn_ref(x, W_org, lora_down, lora_up, lora_keys, Wq):
        import jax, jax.numpy as jnp
        import numpy as np
        import math
        B, S, IN, OUT = (4, 256, 512, 512)
        E, R, K = (8, 64, 128)
        SCALE = 64.0 / 64.0
        MULTIPLIER = 1.0
        base = jnp.einsum('bsi,oi->bso', x, W_org)
        q = jnp.einsum('bi,ki->bk', x.mean(axis=1), Wq)
        scores = jnp.einsum('bk,ek->be', q, lora_keys) / math.sqrt(K)
        coeffs = jax.nn.softmax(scores, axis=-1)
        h = jnp.einsum('bsi,eir->bser', x, lora_down)
        delta = jnp.einsum('be,bser,ero->bso', coeffs, h, lora_up)
        return base + delta * (SCALE * MULTIPLIER)
    x = x + _L0_xattn_ref(_layernorm(x, axis=-1), ctx_4096, L0_xattn_Wq, L0_xattn_Wk, L0_xattn_Wv, L0_xattn_Wo, L0_xattn_q_norm_w, L0_xattn_k_norm_w)
    x = x + _L0_ffn_ref(_layernorm(x, axis=-1), L0_ffn_gate_qweight, L0_ffn_gate_scales, L0_ffn_gate_qzeros, L0_ffn_gate_g_idx, L0_ffn_up_qweight, L0_ffn_up_scales, L0_ffn_up_qzeros, L0_ffn_up_g_idx, L0_ffn_down_qweight, L0_ffn_down_scales, L0_ffn_down_qzeros, L0_ffn_down_g_idx)
    x = x + _L1_xattn_ref(ctx_4096, _layernorm(x, axis=-1), ctx_4096)
    x = x + _L1_ffn_ref(_layernorm(x, axis=-1), L1_ffn_W_org, L1_ffn_lora_down, L1_ffn_lora_up, L1_ffn_lora_keys, L1_ffn_Wq)
    return x

_drawn_inputs = setup_inputs


def setup_inputs(seed=0):
    import zlib

    import numpy as np

    out = dict(_drawn_inputs(seed))
    spreads = {'L0_xattn_q_norm_w': (1.0, 0.6), 'L0_xattn_k_norm_w': (1.0, 0.6)}
    factors = {'L1_ffn_lora_down': 3.131,
     'L1_ffn_lora_up': 3.094,
     'L1_ffn_lora_keys': 8.0,
     'L1_ffn_Wq': 8.0}
    for name, (base, spread) in spreads.items():
        noise = np.random.default_rng([zlib.crc32(name.encode()), seed]).standard_normal(out[name].shape)
        drawn = base * np.exp(spread * noise) if base else spread * noise
        out[name] = jnp.asarray(drawn.astype(out[name].dtype))
    for name, factor in factors.items():
        out[name] = (out[name] * factor).astype(out[name].dtype)
    return out
```

```python
from contextlib import ExitStack

import concourse.bass as bass
from concourse import mybir

F32 = mybir.dt.float32
F32R = mybir.dt.float32r
BF16 = mybir.dt.bfloat16
I32 = mybir.dt.int32
ALU = mybir.AluOpType
ACT = mybir.ActivationFunctionType
AX = mybir.AxisListType.X

P = 128
HI, LO = 0, 1
PASSES = ((HI, HI), (HI, LO), (LO, HI))


class Step:

    def __init__(self, i, j, period):
        self.i, self.j, self.period = i, j, period

    def done(self, lag=0, per=1):
        return per * self.period * self.i + per * (self.j - lag + 1)

    def has(self, lag, units):
        return not isinstance(self.i, int) or 0 <= self.j - lag < units


def wait(eng, sem, value):
    if not isinstance(value, int) or value > 0:
        eng.wait_ge(sem, value)


def run_steps(eng, step, head, period, rounds, total):
    for j in range(head):
        step(Step(0, j, period))
    with eng.Fori(0, rounds) as i:
        for j in range(head, head + period):
            step(Step(i, j, period))
    for j in range(head + period * rounds, total):
        step(Step(0, j, period))


def block_kernel(nc, a, out, stop=None):
    x, ctx_in = a["x"], a["ctx_4096"]
    Wq, Wk, Wv, Wo = (a[f"L0_xattn_{n}"] for n in ("Wq", "Wk", "Wv", "Wo"))
    B, T, D = x.shape
    HD = a["L0_xattn_q_norm_w"].shape[0]
    KVH = Wk.shape[1] // HD
    G = Wq.shape[1] // HD // KVH
    KT = D // P
    PAIRS = B * T // P
    UNITS = KVH * PAIRS
    QW = G * HD
    QKV = QW + 2 * HD
    RMS_EPS, LN_EPS = 1e-6, 1e-5
    F = a["L0_ffn_gate_qweight"].shape[1]
    GG = a["L0_ffn_gate_scales"].shape[0]
    GD = a["L0_ffn_down_scales"].shape[0]
    FT = -(-F // P)
    HALF = B * T // 2
    EXP = a["L1_ffn_lora_down"].shape[0]
    RANK = a["L1_ffn_lora_down"].shape[2]
    KD = a["L1_ffn_Wq"].shape[0]
    assert (T, D, HD, G, PAIRS, KVH, QW, EXP * RANK) == (64, 512, 128, 4, 8, 8, 512, 512)

    x_t = x.rearrange("(q b) t d -> q (b t) d", b=2)
    ctx_t = ctx_in.rearrange("(q b) t d -> q (b t) d", b=2)
    out_t = out.rearrange("(q b) t d -> q (b t) d", b=2)

    root = ExitStack()
    with root:
        def sb(name, shape, dt, scope=root):
            return scope.enter_context(nc.sbuf_tensor(name, shape, dt))

        def sem(name):
            return root.enter_context(nc.semaphore(name))

        def sems(name, n):
            return [sem(f"{name}{k}") for k in range(n)]

        bank = [root.enter_context(nc.psum_tensor(f"bank{k}", [P, 512], F32)) for k in range(8)]

        acc = sb("acc", [P, PAIRS, D], F32)
        ident = sb("ident", [P, P], F32)
        half_neg = sb("half_neg", [P, 8], F32)
        inv_sqrt_t = sb("inv_sqrt_t", [P, 1], F32)
        stat = sb("stat", [P, 16, 6], F32)
        mv = sb("mv", [P, 4, PAIRS, 2], F32)
        rstd = sb("rstd", [P, 4, PAIRS], F32)

        s0 = ExitStack()
        kvT = sb("kvT", [P, 2, KT, PAIRS, 4, T], F32R, s0)
        wqkv = sb("wqkv", [P, 2, 2, KT, QKV], F32R, s0)
        wo = sb("wo", [P, 2, 2, G, D], F32R, s0)
        wqkv_raw = sb("wqkv_raw", [P, 2, QKV], F32, s0)
        wo_raw = sb("wo_raw", [P, 2, D], F32, s0)
        wqk = sb("wqk", [P, 4], F32, s0)
        s0a = ExitStack()
        ctx_raw = sb("ctx_raw", [P, 4, D], F32, s0a)
        xn0 = sb("xn0", [P, 2, D], F32, s0a)
        s0a.close()
        s0b = ExitStack()
        qsq = sb("qsq", [P, G, HD], F32, s0b)
        ksq = sb("ksq", [P, 2, HD], F32, s0b)
        qn = sb("qn", [P, G, HD], F32, s0b)
        kn = sb("kn", [P, 2, HD], F32, s0b)
        qT = sb("qT", [P, 2, G, T], F32, s0b)
        kT = sb("kT", [P, 2, P], F32, s0b)
        vv = sb("vv", [P, 2, 2, 2, HD], F32R, s0b)
        prob = sb("prob", [P, 2 * 2, P], F32, s0b)
        pT = sb("pT", [P, 2, 2, G * T], F32R, s0b)
        aoT = sb("aoT", [P, 2, G, 2, T], F32R, s0b)
        ssq = sb("ssq", [P, 6], F32, s0b)
        msq = sb("msq", [P, 6], F32, s0b)
        rms = sb("rms", [P, 6], F32, s0b)
        nmax = sb("nmax", [P, 4], F32, s0b)
        psum_row = sb("psum_row", [P, 4], F32, s0b)
        rsum = sb("rsum", [P, 4], F32, s0b)
        s0b.close()
        s0.close()

        GATE, UP, DOWN = 0, F, 2 * F
        ZS = 2 * F + D
        s1 = ExitStack()
        zs = sb("zs", [P, 2, ZS], BF16, s1)
        oh_gu = sb("oh_gu", [P, 2, D], BF16, s1)
        oh_d = sb("oh_d", [P, F], BF16, s1)
        shift = sb("shift", [P, 1], I32, s1)
        s1a = ExitStack()
        pid = sb("pid", [P, 1], I32, s1a)
        grp_i = sb("grp_i", [P, 1], I32, s1a)
        grp = sb("grp", [P, 1], F32, s1a)
        idx_raw = sb("idx_raw", [P, 2 * D + F], I32, s1a)
        idx_f = sb("idx_f", [P, 2 * D + F], F32, s1a)
        idx_n = sb("idx_n", [P, 2 * D + F], F32, s1a)
        s_raw = sb("s_raw", [P, ZS], F32, s1a)
        z_raw = sb("z_raw", [32, ZS // 8], I32, s1a)
        z_int = sb("z_int", [32, ZS // 8, 8], I32, s1a)
        s1a.close()
        s1b = ExitStack()
        wgu = sb("wgu", [P, FT, 2, 2, KT, P], F32R, s1b)
        wd = sb("wd", [P, FT, 2, D], F32R, s1b)
        x2T = sb("x2T", [P, 2, KT, HALF], F32R, s1b)
        hT = sb("hT", [P, 2, HALF], F32R, s1b)
        packed = sb("packed", [P, 3, 512], I32, s1b)
        nib = sb("nib", [P, 256], I32, s1b)
        wint = sb("wint", [P, 256], F32, s1b)
        wtmp = sb("wtmp", [P, 2, 256], F32, s1b)
        xn2 = sb("xn2", [P, 2, D], F32, s1b)
        gact = sb("gact", [P, HALF], F32, s1b)
        hval = sb("hval", [P, HALF], F32, s1b)
        s1b.close()
        s1.close()

        s2 = ExitStack()
        cx = sb("cx", [P, 2, D], F32, s2)
        cR = sb("cR", [P, 2, 2, D], F32R, s2)
        vTz = sb("vTz", [P, 2, KT, 2, 3 * T], F32R, s2)
        xn3 = sb("xn3", [P, 2, D], F32, s2)
        qR = sb("qR", [P, 2, 2, D], F32R, s2)
        pr = sb("pr", [P, 4, KT, D], F32, s2)
        pmT = sb("pmT", [P, 4, 2, D], F32R, s2)
        st3 = sb("st3", [P, 6], F32, s2)
        mv3 = sb("mv3", [P, 2, 2], F32, s2)
        rs3 = sb("rs3", [P, 2, 2], F32, s2)
        nm1 = sb("nm1", [P, 4], F32, s2)
        sm1 = sb("sm1", [P, 4], F32, s2)
        rc1 = sb("rc1", [P, 4], F32, s2)
        s2.close()

        s3 = ExitStack()
        x4T = sb("x4T", [P, 2, KT, B * T], F32R, s3)
        woT = sb("woT", [P, 2, KT, D], F32R, s3)
        dn = sb("dn", [P, 2, KT, EXP * RANK], F32R, s3)
        up = sb("up", [P, 2, KT, D], F32R, s3)
        hs = sb("hs", [P, 2, KT, B * T], F32R, s3)
        worg = sb("worg", [P, KT, D], F32, s3)
        draw = sb("draw", [P, KT, EXP * RANK], F32, s3)
        uraw = sb("uraw", [P, KT, D], F32, s3)
        wq1 = sb("wq1", [P, D], F32, s3)
        wq1T = sb("wq1T", [P, KT, KD], F32, s3)
        keys = sb("keys", [EXP, KD], F32, s3)
        keysT = sb("keysT", [P, EXP], F32, s3)
        xn4 = sb("xn4", [P, 2, D], F32, s3)
        meanT = sb("meanT", [P, KT, B], F32, s3)
        q1T = sb("q1T", [P, B], F32, s3)
        lg = sb("lg", [B, EXP], F32, s3)
        cf = sb("cf", [B, EXP], F32, s3)
        cstat = sb("cstat", [B, 4], F32, s3)
        cexp = sb("cexp", [B, EXP, RANK], F32, s3)
        cT = sb("cT", [P, KT, B], F32, s3)
        hval4 = sb("hval4", [P, 2, 512], F32, s3)
        s3.close()

        s_const = sem("s_const")
        s_stat, s_rstd, s_xn = sem("s_stat"), sem("s_rstd"), sem("s_xn")
        sx, sc = sems("s_x", PAIRS), sems("s_ctx", PAIRS)

        block = root.enter_context(nc.Block())

        s_nw = sem("s_nw")
        s_wqk = sem("s_wqk")
        s_wqkv_in, s_wo_in = sems("s_wqkv_in", 2), sems("s_wo_in", 2)
        s_wqkv_hi, s_wqkv = sem("s_wqkv_hi"), sem("s_wqkv")
        s_wo_hi, s_wo = sem("s_wo_hi"), sem("s_wo")
        s_tc, s_tx = sem("s_tc"), sem("s_tx")
        s_chi, s_clo, s_xhi, s_xlo = sem("s_chi"), sem("s_clo"), sem("s_xhi"), sem("s_xlo")
        s_q, s_kv, s_t, s_s, s_pt, s_pv, s_o = (sem(f"s_{n}") for n in ("q", "kv", "t", "s", "pt", "pv", "o"))
        s_qsq, s_ksq, s_qT, s_kT, s_vhi, s_exp, s_phi, s_aohi = (
            sem(f"s_{n}") for n in ("qsq", "ksq", "qT", "kT", "vhi", "exp", "phi", "aohi"))
        s_qms, s_kms, s_qn, s_kn, s_vlo, s_max, s_plo, s_pn, s_aolo, s_acc = (
            sem(f"s_{n}") for n in ("qms", "kms", "qn", "kn", "vlo", "max", "plo", "pn", "aolo", "acc"))
        s_red = sem("s_red")
        s_rq, s_rk = sem("s_rq"), sem("s_rk")
        s_rec = sem("s_rec")
        b_q, b_kv, b_tq, b_tk, b_s, b_pt, b_pv, b_o = bank

        HEAD, PERIOD = 8, 2 * PAIRS
        ROUNDS = (UNITS - HEAD) // PERIOD
        STEPS0 = UNITS + 4

        def unit(st, lag):
            u = st.j - lag
            return u % PAIRS, u // PAIRS % 2, u % 2

        def ln_load(sp):
            for p in range(PAIRS):
                sp.dma_start(acc[:, p, :], x_t[p]).then_inc(sx[p], 16)

        def sp_first(sp):
            sp.dma_start(wqk[:, 0:1], a["L0_xattn_q_norm_w"].rearrange("(d o) -> d o", o=1)).then_inc(s_nw, 16)
            sp.dma_start(wqk[:, 1:2], a["L0_xattn_k_norm_w"].rearrange("(d o) -> d o", o=1)).then_inc(s_nw, 16)

            def qkv_piece(g, kt, freed):
                wait(sp, s_wqkv, freed)
                rows, slot = slice(kt * P, (kt + 1) * P), kt % 2
                sp.dma_start(wqkv_raw[:, slot, 0:QW], Wq[rows, bass.ds(g * QW, QW)]).then_inc(s_wqkv_in[slot], 16)
                sp.dma_start(wqkv_raw[:, slot, QW:QW + HD], Wk[rows, bass.ds(g * HD, HD)]).then_inc(s_wqkv_in[slot], 16)
                sp.dma_start(wqkv_raw[:, slot, QW + HD:QKV], Wv[rows, bass.ds(g * HD, HD)]).then_inc(s_wqkv_in[slot], 16)

            def wo_piece(g, h, freed):
                wait(sp, s_wo, freed)
                sp.dma_start(wo_raw[:, h % 2, :], Wo[bass.ds(g * QW + h * HD, HD), :]).then_inc(s_wo_in[h % 2], 16)

            def group(g, first):
                def freed(piece):
                    return piece - 1 if first else 4 * g + piece - 1
                qkv_piece(g, 0, freed(0))
                if not first:
                    wo_piece(g - 1, 3, 4 * g - 2)
                qkv_piece(g, 1, freed(1))
                wo_piece(g, 0, freed(0))
                qkv_piece(g, 2, freed(2))
                wo_piece(g, 1, freed(1))
                qkv_piece(g, 3, freed(3))
                wo_piece(g, 2, freed(2))

            for p in range(2):
                sp.dma_start(acc[:, p, :], x_t[p]).then_inc(sx[p], 16)
                sp.dma_start(ctx_raw[:, p, :], ctx_t[p]).then_inc(sc[p], 16)
            group_zero = True
            qkv_piece(0, 0, 0)
            qkv_piece(0, 1, 0)
            for p in range(2, 4):
                sp.dma_start(acc[:, p, :], x_t[p]).then_inc(sx[p], 16)
                sp.dma_start(ctx_raw[:, p, :], ctx_t[p]).then_inc(sc[p], 16)
            wo_piece(0, 0, 0)
            qkv_piece(0, 2, 1)
            wo_piece(0, 1, 0)
            for p in range(4, PAIRS):
                sp.dma_start(acc[:, p, :], x_t[p]).then_inc(sx[p], 16)
                sp.wait_ge(s_clo, p - 3)
                sp.dma_start(ctx_raw[:, p % 4, :], ctx_t[p]).then_inc(sc[p], 16)
            qkv_piece(0, 3, 2)
            wo_piece(0, 2, 1)
            with sp.Fori(1, KVH) as g:
                group(g, False)
            wo_piece(KVH - 1, 3, 4 * KVH - 2)

        def split_qkv_hi(act, value, par, kt, n_in):
            act.wait_ge(s_wqkv_in[kt % 2], n_in)
            act.activation(wqkv[:, par, HI, kt, :], wqkv_raw[:, kt % 2, :], ACT.Copy).then_inc(s_wqkv_hi, 1)

        def pe_first(pe):
            pe.wait_ge(s_const, 4)
            for p in range(PAIRS + 1):
                if p < PAIRS:
                    b = bank[p % 2]
                    pe.wait_ge(sc[p], 16)
                    if p >= 2:
                        pe.wait_ge(s_clo, p - 1)
                    for kt in range(KT):
                        mm = pe.transpose(b[:, kt * P:(kt + 1) * P], ctx_raw[:, p % 4, kt * P:(kt + 1) * P], ident[:, :])
                    mm.then_inc(s_tc, 1)
                if p >= 1:
                    b = bank[2 + p % 2]
                    pe.wait_ge(s_xn, p)
                    if p >= 3:
                        pe.wait_ge(s_xlo, p - 2)
                    for kt in range(KT):
                        mm = pe.transpose(b[:, kt * P:(kt + 1) * P], xn0[:, (p - 1) % 2, kt * P:(kt + 1) * P], ident[:, :])
                    mm.then_inc(s_tx, 1)
            pe.wait_ge(s_clo, PAIRS)
            pe.wait_ge(s_xlo, PAIRS)
            run_steps(pe, pe_step0, HEAD, PERIOD, ROUNDS, STEPS0)

        def group_count(st, lag):
            return 4 * ((st.j - lag) // PAIRS + 1) + st.i * 4 * (PERIOD // PAIRS)

        def pe_step0(st):
            pe = nc.tensor
            if st.has(0, UNITS):
                p, par, _ = unit(st, 0)
                if p == 0:
                    pe.wait_ge(s_wqkv, group_count(st, 0))
                wait(pe, s_qn, st.done(1))
                for kt in range(KT):
                    for n, (l, r) in enumerate(PASSES):
                        mm = pe.matmul(b_q[:, :], kvT[:, l, kt, p, 1:3, :], wqkv[:, par, r, kt, 0:QW],
                                       start=(kt == 0 and n == 0), stop=(kt == KT - 1 and n == 2))
                mm.then_inc(s_q, 1)
            if st.has(1, UNITS):
                pe.wait_ge(s_qn, st.done(1))
                wait(pe, s_qT, st.done(2))
                wait(pe, s_kT, st.done(2))
                for h in range(G):
                    pe.transpose(b_tq[:, h * P:(h + 1) * P], qn[:, h, :], ident[:, :])
                pe.wait_ge(s_kn, st.done(1))
                for b in range(2):
                    mm = pe.transpose(b_tk[:, b * P:(b + 1) * P], kn[:, b, :], ident[:, :])
                mm.then_inc(s_t, 1)
            if st.has(0, UNITS):
                p, par, _ = unit(st, 0)
                wait(pe, s_vlo, st.done(1))
                wait(pe, s_kn, st.done(1))
                for b in range(2):
                    for kt in range(KT):
                        for n, (l, r) in enumerate(PASSES):
                            mm = pe.matmul(b_kv[:, b * 256:(b + 1) * 256], kvT[:, l, kt, p, 2 * b:2 * b + 2, :],
                                           wqkv[:, par, r, kt, QW:QKV],
                                           start=(kt == 0 and n == 0), stop=(kt == KT - 1 and n == 2))
                mm.then_inc(s_kv, 1)
            if st.has(1, UNITS):
                pe.wait_ge(s_qT, st.done(1))
                pe.wait_ge(s_kT, st.done(1))
                wait(pe, s_exp, st.done(2, 4))
                for b in range(2):
                    for hp in range(2):
                        n = b * 2 + hp
                        mm = pe.matmul(b_s[:, n * P:(n + 1) * P], qT[:, b, 2 * hp:2 * hp + 2, :], kT[:, b, :],
                                       start=True, stop=True)
                mm.then_inc(s_s, 1)
            if st.has(2, UNITS):
                pe.wait_ge(s_pn, st.done(2))
                wait(pe, s_plo, st.done(3))
                for n in range(4):
                    mm = pe.transpose(b_pt[:, n * P:(n + 1) * P], prob[:, n, :], ident[:, :])
                mm.then_inc(s_pt, 1)
            if st.has(3, UNITS):
                p, par, _ = unit(st, 3)
                if p == 0:
                    pe.wait_ge(s_wo, group_count(st, 3))
                pe.wait_ge(s_aolo, st.done(3))
                wait(pe, s_acc, st.done(4))
                for h in range(G):
                    for n, (l, r) in enumerate(PASSES):
                        mm = pe.matmul(b_o[:, :], aoT[:, l, h, :, :], wo[:, par, r, h, :],
                                       start=(h == 0 and n == 0), stop=(h == G - 1 and n == 2))
                mm.then_inc(s_o, 1)
            if st.has(2, UNITS):
                _, _, par = unit(st, 2)
                pe.wait_ge(s_plo, st.done(2))
                pe.wait_ge(s_vlo, st.done(2))
                wait(pe, s_aolo, st.done(3))
                for b in range(2):
                    for n, (l, r) in enumerate(PASSES):
                        mm = pe.matmul(b_pv[:, b * 256:(b + 1) * 256], vv[:, par, l, b, :], pT[:, r, b, :],
                                       start=(n == 0), stop=(n == 2))
                mm.then_inc(s_pv, 1)

        def weight_piece(st):
            j = st.j % PAIRS
            return {0: ("qkv", 0, 1), 1: ("wo", 3, 0), 2: ("qkv", 1, 1), 3: ("wo", 0, 1),
                    4: ("qkv", 2, 1), 5: ("wo", 1, 1), 6: ("qkv", 3, 1), 7: ("wo", 2, 1)}[j]

        def piece_of(st):
            kind, n, ahead = weight_piece(st)
            gj = st.j // PAIRS + ahead
            exists = not isinstance(st.i, int) or gj < KVH
            g = gj + st.i * (PERIOD // PAIRS)
            return kind, n, g, gj, exists

        def hi_piece(act, st):
            kind, n, g, gj, exists = piece_of(st)
            if not exists:
                return
            par = gj % 2
            if kind == "qkv":
                act.wait_ge(s_wqkv_in[n % 2], 48 * (2 * g + n // 2 + 1))
                wait(act, s_kv, (8 * (g - 1)) if gj >= 2 else 0)
                act.activation(wqkv[:, par, HI, n, :], wqkv_raw[:, n % 2, :], ACT.Copy).then_inc(s_wqkv_hi, 1)
            else:
                act.wait_ge(s_wo_in[n % 2], 16 * (2 * g + n // 2 + 1))
                wait(act, s_o, (8 * (g - 1)) if gj >= 2 else 0)
                act.activation(wo[:, par, HI, n, :], wo_raw[:, n % 2, :], ACT.Copy).then_inc(s_wo_hi, 1)

        def lo_piece(pool, st):
            kind, n, g, gj, exists = piece_of(st)
            if not exists:
                return
            par = gj % 2
            if kind == "qkv":
                pool.wait_ge(s_wqkv_hi, 4 * g + n + 1)
                pool.tensor_tensor(wqkv[:, par, LO, n, :], wqkv_raw[:, n % 2, :],
                                   wqkv[:, par, HI, n, :].bitcast(F32), ALU.subtract).then_inc(s_wqkv, 1)
            else:
                pool.wait_ge(s_wo_hi, 4 * g + n + 1)
                pool.tensor_tensor(wo[:, par, LO, n, :], wo_raw[:, n % 2, :],
                                   wo[:, par, HI, n, :].bitcast(F32), ALU.subtract).then_inc(s_wo, 1)

        def kv_context(part, p):
            return kvT[:, part, :, p, 0::3, :]

        def kv_latents(part, p):
            return kvT[:, part, :, p, 1:3, :]

        def by_batch(b):
            return b[:, :].rearrange("p (k b t) -> p k b t", k=KT, b=2)

        def act_first(act):
            for p in range(PAIRS + 1):
                if p < PAIRS:
                    act.wait_ge(s_tc, p + 1)
                    act.activation(kv_context(HI, p), by_batch(bank[p % 2]), ACT.Copy).then_inc(s_chi, 1)
                if p >= 1:
                    act.wait_ge(s_tx, p)
                    act.activation(kv_latents(HI, p - 1), by_batch(bank[2 + p % 2]), ACT.Copy).then_inc(s_xhi, 1)
                if 1 <= p <= 4:
                    kt = p - 1
                    act.wait_ge(s_wqkv_in[kt % 2], 48 * (kt // 2 + 1))
                    act.activation(wqkv[:, 0, HI, kt, :], wqkv_raw[:, kt % 2, :], ACT.Copy).then_inc(s_wqkv_hi, 1)
                if 5 <= p <= 7:
                    h = p - 5
                    act.wait_ge(s_wo_in[h % 2], 16 * (h // 2 + 1))
                    act.activation(wo[:, 0, HI, h, :], wo_raw[:, h % 2, :], ACT.Copy).then_inc(s_wo_hi, 1)
            act.wait_ge(s_clo, PAIRS)
            act.wait_ge(s_tx, PAIRS)
            act.wait_ge(s_wqk, 2)
            run_steps(act, act_step0, HEAD, PERIOD, ROUNDS, STEPS0)

        def act_step0(st):
            act = nc.scalar
            if st.has(3, UNITS):
                act.wait_ge(s_pv, st.done(3))
                wait(act, s_o, st.done(4))
                act.activation(aoT[:, HI, :, :, :], b_pv[:, :].rearrange("p (b h t) -> p h b t", b=2, h=G),
                               ACT.Copy).then_inc(s_aohi, 1)
            if st.has(1, UNITS):
                _, _, par = unit(st, 1)
                act.wait_ge(s_kn, st.done(1))
                wait(act, s_pv, st.done(3))
                act.activation(vv[:, par, HI, :, :], b_kv[:, :].rearrange("p (b c) -> p b c", b=2)[:, :, HD:2 * HD],
                               ACT.Copy).then_inc(s_vhi, 1)
            if st.has(0, UNITS):
                act.wait_ge(s_q, st.done(0))
                wait(act, s_qms, st.done(1))
                act.activation(qsq[:, :, :], b_q[:, :].rearrange("p (h d) -> p h d", h=G), ACT.Square).then_inc(s_qsq, 1)
            if st.has(1, UNITS):
                act.wait_ge(s_t, st.done(1))
                wait(act, s_s, st.done(2))
                act.activation(qT[:, :, :, :].rearrange("p b h t -> p h b t"),
                               b_tq[:, :].rearrange("p (h b t) -> p h b t", h=G, b=2), ACT.Copy).then_inc(s_qT, 1)
                act.activation(kT[:, :, :], b_tk[:, 0:2 * P].rearrange("p (b k) -> p b k", b=2), ACT.Copy,
                               scale=wqk[:, 3:4]).then_inc(s_kT, 1)
            if st.has(0, UNITS):
                act.wait_ge(s_kv, st.done(0))
                wait(act, s_kms, st.done(1))
                act.activation(ksq[:, :, :], b_kv[:, :].rearrange("p (b c) -> p b c", b=2)[:, :, 0:HD],
                               ACT.Square).then_inc(s_ksq, 1)
            if st.has(2, UNITS):
                act.wait_ge(s_pt, st.done(2))
                wait(act, s_pv, st.done(3))
                act.activation(pT[:, HI, :, :], b_pt[:, :].rearrange("p (b q) -> p b q", b=2), ACT.Copy).then_inc(s_phi, 1)
            if st.has(1, UNITS):
                act.wait_ge(s_max, st.done(1))
                wait(act, s_pt, st.done(2))
                wait(act, s_rec, st.done(2))
                for n in range(4):
                    act.activation(prob[:, n, :], b_s[:, n * P:(n + 1) * P], ACT.Exp, bias=nmax[:, n:n + 1],
                                   accum_out=psum_row[:, n:n + 1]).then_inc(s_exp, 1)
            hi_piece(act, st)

        def dve_step0(st):
            dve = nc.vector
            if st.has(3, UNITS):
                dve.wait_ge(s_aohi, st.done(3))
                dve.tensor_tensor(aoT[:, LO, :, :, :], b_pv[:, :].rearrange("p (b h t) -> p h b t", b=2, h=G),
                                  aoT[:, HI, :, :, :].bitcast(F32), ALU.subtract).then_inc(s_aolo, 1)
            if st.has(4, UNITS):
                p, _, _ = unit(st, 4)
                dve.wait_ge(s_o, st.done(4))
                dve.tensor_tensor(acc[:, p, :], b_o[:, :], acc[:, p, :], ALU.add).then_inc(s_acc, 1)
            if st.has(1, UNITS):
                _, _, par = unit(st, 1)
                dve.wait_ge(s_vhi, st.done(1))
                dve.tensor_tensor(vv[:, par, LO, :, :], b_kv[:, :].rearrange("p (b c) -> p b c", b=2)[:, :, HD:2 * HD],
                                  vv[:, par, HI, :, :].bitcast(F32), ALU.subtract).then_inc(s_vlo, 1)
            if st.has(0, UNITS):
                dve.wait_ge(s_qsq, st.done(0))
                wait(dve, s_rq, st.done(1))
                dve.tensor_reduce(ssq[:, 0:4], qsq[:, :, :], AX, ALU.add).then_inc(s_red, 1)
                dve.wait_ge(s_red, st.done(0, 2) - 1)
                dve.tensor_scalar(msq[:, 0:4], ssq[:, 0:4], 1.0 / HD, RMS_EPS, ALU.mult, ALU.add).then_inc(s_qms, 1)
                dve.wait_ge(s_rq, st.done(0))
                wait(dve, s_t, st.done(1))
                dve.tensor_tensor(qn[:, :, :], b_q[:, :].rearrange("p (h d) -> p h d", h=G),
                                  rms[:, 0:4].unsqueeze(2).to_broadcast([P, G, HD]), ALU.mult).then_inc(s_qn, 1)
                dve.wait_ge(s_ksq, st.done(0))
                wait(dve, s_rk, st.done(1))
                dve.tensor_reduce(ssq[:, 4:6], ksq[:, :, :], AX, ALU.add).then_inc(s_red, 1)
                dve.wait_ge(s_red, st.done(0, 2))
                dve.tensor_scalar(msq[:, 4:6], ssq[:, 4:6], 1.0 / HD, RMS_EPS, ALU.mult, ALU.add).then_inc(s_kms, 1)
            if st.has(1, UNITS):
                dve.wait_ge(s_s, st.done(1))
                wait(dve, s_exp, st.done(2, 4))
                dve.tensor_reduce(nmax[:, :], b_s[:, :].rearrange("p (n k) -> p n k", n=4), AX, ALU.max,
                                  negate=True).then_inc(s_max, 1)
            if st.has(2, UNITS):
                dve.wait_ge(s_phi, st.done(2))
                dve.tensor_tensor(pT[:, LO, :, :].rearrange("p b q -> p (b q)"), b_pt[:, :],
                                  pT[:, HI, :, :].rearrange("p b q -> p (b q)").bitcast(F32),
                                  ALU.subtract).then_inc(s_plo, 1)
            if st.has(0, UNITS):
                dve.wait_ge(s_rk, st.done(0))
                wait(dve, s_t, st.done(1))
                dve.tensor_tensor(kn[:, :, :], b_kv[:, :].rearrange("p (b c) -> p b c", b=2)[:, :, 0:HD],
                                  rms[:, 4:6].unsqueeze(2).to_broadcast([P, 2, HD]), ALU.mult).then_inc(s_kn, 1)
            if st.has(1, UNITS):
                dve.wait_ge(s_exp, st.done(1, 4))
                wait(dve, s_pn, st.done(2))
                dve.reciprocal(rsum[:, :], psum_row[:, :]).then_inc(s_rec, 1)
                dve.wait_ge(s_rec, st.done(1))
                dve.tensor_tensor(prob[:, :, :], prob[:, :, :], rsum[:, :].unsqueeze(2).to_broadcast([P, 4, P]),
                                  ALU.mult).then_inc(s_pn, 1)

        def dve_first(dve):
            dve.wait_ge(s_nw, 32)
            dve.tensor_tensor(wqk[:, 2:3], wqk[:, 0:1], wqk[:, 1:2], ALU.mult).then_inc(s_wqk, 1)
            dve.wait_ge(s_wqk, 1)
            dve.tensor_scalar(wqk[:, 3:4], wqk[:, 2:3], float(HD) ** -0.5, None, ALU.mult).then_inc(s_wqk, 1)
            for p in range(PAIRS + 2):
                if p < PAIRS:
                    dve.wait_ge(sx[p], 16)
                    ln_stats(dve, 0, p)
                if 1 <= p <= PAIRS:
                    if p >= 3:
                        dve.wait_ge(s_tx, p - 2)
                    ln_apply(dve, 0, p - 1, xn0[:, (p - 1) % 2, :], p)
                if p < PAIRS:
                    dve.wait_ge(s_chi, p + 1)
                    dve.tensor_tensor(kv_context(LO, p), by_batch(bank[p % 2]), kv_context(HI, p).bitcast(F32),
                                      ALU.subtract).then_inc(s_clo, 1)
                if p >= 2:
                    dve.wait_ge(s_xhi, p - 1)
                    dve.tensor_tensor(kv_latents(LO, p - 2), by_batch(bank[2 + (p - 1) % 2]),
                                      kv_latents(HI, p - 2).bitcast(F32), ALU.subtract).then_inc(s_xlo, 1)
            run_steps(dve, dve_step0, HEAD, PERIOD, ROUNDS, STEPS0)

        def pool_first(pool):
            for p in range(PAIRS):
                ln_power(pool, 0, p)
                if p < 4:
                    pool.wait_ge(s_wqkv_hi, p + 1)
                    pool.tensor_tensor(wqkv[:, 0, LO, p, :], wqkv_raw[:, p % 2, :], wqkv[:, 0, HI, p, :].bitcast(F32),
                                       ALU.subtract).then_inc(s_wqkv, 1)
                if 4 <= p < 7:
                    h = p - 4
                    pool.wait_ge(s_wo_hi, h + 1)
                    pool.tensor_tensor(wo[:, 0, LO, h, :], wo_raw[:, h % 2, :], wo[:, 0, HI, h, :].bitcast(F32),
                                       ALU.subtract).then_inc(s_wo, 1)
            pool.wait_ge(s_clo, PAIRS)
            pool.wait_ge(s_tx, PAIRS)
            run_steps(pool, pool_step0, HEAD, PERIOD, ROUNDS, STEPS0)

        def pool_step0(st):
            pool = nc.gpsimd
            if st.has(0, UNITS):
                pool.wait_ge(s_qms, st.done(0))
                wait(pool, s_qn, st.done(1))
                pool.tensor_tensor(rms[:, 0:4], msq[:, 0:4], half_neg[:, 0:4], ALU.pow).then_inc(s_rq, 1)
                pool.wait_ge(s_kms, st.done(0))
                wait(pool, s_kn, st.done(1))
                pool.tensor_tensor(rms[:, 4:6], msq[:, 4:6], half_neg[:, 4:6], ALU.pow).then_inc(s_rk, 1)
            lo_piece(pool, st)

        s_bn = sem("s_bn")

        def ln_stats(dve, which, p):
            n = which * PAIRS + p
            dve.bn_stats(stat[:, n % 16, :], acc[:, p, :]).then_inc(s_bn, 1)
            dve.wait_ge(s_bn, 2 * n + 1)
            dve.bn_aggr(mv[:, which, p, :], stat[:, n % 16, :]).then_inc(s_bn, 1)
            dve.wait_ge(s_bn, 2 * n + 2)
            dve.tensor_scalar(mv[:, which, p, 1:2], mv[:, which, p, 1:2], LN_EPS, None, ALU.add).then_inc(s_stat, 1)

        def ln_power(pool, which, p):
            pool.wait_ge(s_stat, which * PAIRS + p + 1)
            pool.tensor_tensor(rstd[:, which, p:p + 1], mv[:, which, p, 1:2], half_neg[:, 0:1], ALU.pow).then_inc(s_rstd, 1)

        def ln_apply(dve, which, p, to, count):
            dve.wait_ge(s_rstd, which * PAIRS + p + 1)
            dve.tensor_scalar(to, acc[:, p, :], mv[:, which, p, 0:1], rstd[:, which, p:p + 1],
                              ALU.subtract, ALU.mult).then_inc(s_xn, 1)

        s_pid, s_col, s_zero = sem("s_pid"), sem("s_col"), sem("s_zero")
        s_idx, s_sraw, s_zraw = sem("s_idx"), sem("s_sraw"), sem("s_zraw")
        s_idx_v, s_scale_v, s_zero_v = sem("s_idx_v"), sem("s_scale_v"), sem("s_zero_v")
        s_packed = sems("s_packed", 3)
        s_nib, s_zs, s_wt, s_whi, s_wlo = sem("s_nib"), sem("s_zs"), sem("s_wt"), sem("s_whi"), sem("s_wlo")
        s_tx2, s_x2hi, s_x2lo = sem("s_tx2"), sem("s_x2hi"), sem("s_x2lo")
        s_g, s_u, s_d, s_gact, s_hval, s_hhi, s_hlo, s_y2 = (
            sem(f"s_{n}") for n in ("g", "u", "d", "gact", "hval", "hhi", "hlo", "y2"))
        f_g, f_u = bank[0], bank[1]
        f_z = bank[2:4]
        f_d = bank[4:8]
        SCALE_ROWS = (0, 64, 96)
        TABLES = (("gate", GATE, F, GG), ("up", UP, F, GG), ("down", DOWN, D, GD))
        CHUNKS = 6
        HP = PAIRS // 2
        X2 = 1

        def width(f):
            return min(P, F - f * P)

        def sp_ffn(sp):
            sp.wait_ge(s_acc, UNITS)
            for n, (m, count) in enumerate((("gate", D), ("up", D), ("down", F))):
                sp.dma_start(idx_raw[:, n * D:n * D + count],
                             a[f"L0_ffn_{m}_g_idx"].rearrange("(o k) -> o k", o=1).to_broadcast([P, count])).then_inc(s_idx, 16)
            for m, at, n, g in TABLES:
                sp.dma_start(z_raw[0:g, at // 8:(at + n) // 8], a[f"L0_ffn_{m}_qzeros"]).then_inc(s_zraw, 16)
            sp.wait_ge(s_zero, 1)
            for m, at, n, g in TABLES:
                for row in SCALE_ROWS:
                    sp.dma_start(s_raw[row:row + g, at:at + n], a[f"L0_ffn_{m}_scales"]).then_inc(s_sraw, 16)
            sp.wait_ge(s_scale_v, 5)
            sp.wait_ge(s_idx_v, 7)
            sp.wait_ge(s_zero_v, 18)
            for f in range(FT):
                w = width(f)
                for k, m in enumerate(("gate", "up")):
                    if f >= 1:
                        sp.wait_ge(s_nib, 2 * (CHUNKS * (f - 1) + 2 * k + 2) - 1)
                    rows = a[f"L0_ffn_{m}_qweight"].rearrange("(t r) n -> t r n", t=KT)
                    for kt in range(KT):
                        sp.dma_start(packed[:, k, kt * P:kt * P + w],
                                     rows[kt, :, f * P:f * P + w].unsqueeze(1).to_broadcast([P // 8, 8, w])
                                     ).then_inc(s_packed[k], 16)
                if f >= 1:
                    sp.wait_ge(s_nib, 2 * CHUNKS * f - 1)
                sp.dma_start(packed[0:w, 2, :],
                             a["L0_ffn_down_qweight"][f * P // 8:(f * P + w) // 8, :].unsqueeze(1)
                             .to_broadcast([w // 8, 8, D])).then_inc(s_packed[2], 16)

        def pool_ffn(pool):
            pool.wait_ge(s_acc, UNITS)
            pool.iota(pid[:, :], pattern=[[0, 1]], base=0, channel_multiplier=1).then_inc(s_pid, 1)
            pool.memset(s_raw[:, :], 0.0).then_inc(s_zero, 1)
            pool.memset(zs[:, 0, :], 0.0).then_inc(s_zero, 1)
            for p in range(PAIRS):
                ln_power(pool, X2, p)
            for f in range(FT):
                for k in range(CHUNKS):
                    c = CHUNKS * f + k
                    dst, rows = weight_chunk(f, k, LO)
                    hi, _ = weight_chunk(f, k, HI)
                    src = chunk_shape(wtmp[:, c % 2, :], f, k)
                    pool.wait_ge(s_whi, c + 1)
                    pool.tensor_tensor(dst, src, hi.bitcast(F32), ALU.subtract).then_inc(s_wlo, 1)

        def weight_chunk(f, k, part):
            w = width(f)
            if k < 4:
                return wgu[:, f, part, k // 2, 2 * (k % 2):2 * (k % 2) + 2, 0:w], P
            return wd[0:w, f, part, (k - 4) * 256:(k - 3) * 256], w

        def chunk_shape(ap, f, k):
            w = width(f)
            if k < 4:
                return ap.rearrange("p (t n) -> p t n", t=2)[:, :, 0:w]
            return ap[0:w, :]

        def zero_scale(f, k, which):
            b, w = f_z[(CHUNKS * f + k) % 2], width(f)
            if k < 4:
                return b[:, :].rearrange("p (t z n) -> p t z n", t=2, z=2)[:, :, which, 0:w]
            return b[0:w, which * 256:(which + 1) * 256]

        def pe_ffn(pe):
            for p in range(HP):
                x2_transposes(pe, p)

            def spread(f, ks):
                w = width(f)
                for k in ks:
                    c = CHUNKS * f + k
                    b = f_z[c % 2]
                    if c >= 2:
                        pe.wait_ge(s_wt, c - 1)
                    if k < 4:
                        at = (GATE, UP)[k // 2] + f * P
                        for t in range(2):
                            kt = 2 * (k % 2) + t
                            mm = pe.matmul(b[:, t * 256:(t + 1) * 256].rearrange("p (z n) -> p z n", z=2)[:, :, 0:w],
                                           oh_gu[:, k // 2, kt * P:(kt + 1) * P], zs[:, :, at:at + w],
                                           start=True, stop=True)
                    else:
                        at = DOWN + (k - 4) * 256
                        mm = pe.matmul(b[0:w, :].rearrange("p (z n) -> p z n", z=2), oh_d[:, f * P:f * P + w],
                                       zs[:, :, at:at + 256], start=True, stop=True)
                    mm.then_inc(s_zs, 1)

            def down(n):
                half, f = divmod(n, FT)
                w = width(f)
                if half == 0:
                    pe.wait_ge(s_wlo, CHUNKS * (f + 1))
                pe.wait_ge(s_hlo, n + 1)
                for t in range(HP):
                    if f == 0 and half == 1:
                        pe.wait_ge(s_y2, t + 1)
                    for k, (l, r) in enumerate(PASSES):
                        mm = pe.matmul(f_d[t][:, :], hT[0:w, l, t * P:(t + 1) * P], wd[0:w, f, r, :],
                                       start=(f == 0 and k == 0), stop=(f == FT - 1 and k == 2))
                mm.then_inc(s_d, 1)

            def inner(n, m, b):
                f = n % FT
                w = width(f)
                for kt in range(KT):
                    for k, (l, r) in enumerate(PASSES):
                        mm = pe.matmul(b[0:w, :], wgu[:, f, l, m, kt, 0:w], x2T[:, r, kt, :],
                                       start=(kt == 0 and k == 0), stop=(kt == KT - 1 and k == 2))
                return mm

            pe.wait_ge(s_idx_v, 7)
            pe.wait_ge(s_scale_v, 5)
            pe.wait_ge(s_zero_v, 18)
            pe.wait_ge(s_x2lo, HP)
            spread(0, range(CHUNKS))
            for n in range(2 * FT):
                half, f = divmod(n, FT)
                if half == 1 and f == 0:
                    pe.wait_ge(s_wt, CHUNKS * FT)
                    for p in range(HP, PAIRS):
                        x2_transposes(pe, p)
                    down(n - 1)
                    pe.wait_ge(s_x2lo, PAIRS)
                if half == 0:
                    pe.wait_ge(s_wlo, CHUNKS * f + 2)
                if n >= 1:
                    pe.wait_ge(s_gact, n)
                inner(n, 0, f_g).then_inc(s_g, 1)
                if n + 1 < FT:
                    spread(f + 1, (0, 1))
                if half == 0:
                    pe.wait_ge(s_wlo, CHUNKS * f + 4)
                if n >= 1:
                    pe.wait_ge(s_hval, n)
                inner(n, 1, f_u).then_inc(s_u, 1)
                if n + 1 < FT:
                    spread(f + 1, (2, 3))
                if f >= 1:
                    down(n - 1)
                if n + 1 < FT:
                    spread(f + 1, (4, 5))
            down(2 * FT - 1)

        def x2_transposes(pe, p):
            pe.wait_ge(s_xn, X2 * PAIRS + p + 1)
            if p == HP:
                pe.wait_ge(s_u, FT)
            if p >= 2:
                pe.wait_ge(s_x2lo, p - 1)
            for kt in range(KT):
                mm = pe.transpose(f_z[p % 2][:, kt * P:(kt + 1) * P], xn2[:, p % 2, kt * P:(kt + 1) * P], ident[:, :])
            mm.then_inc(s_tx2, 1)

        def x2_tile(part, p):
            return x2T[:, part, :, p % HP * P:(p % HP + 1) * P]

        def tiles(b):
            return b[:, :].rearrange("p (k t) -> p k t", k=KT)

        def act_ffn(act):
            act.wait_ge(s_acc, UNITS)

            def x2_hi(p):
                act.wait_ge(s_tx2, p + 1)
                act.activation(x2_tile(HI, p), tiles(f_z[p % 2]), ACT.Copy).then_inc(s_x2hi, 1)

            def w_hi(f, ks):
                for k in ks:
                    c = CHUNKS * f + k
                    dst, _ = weight_chunk(f, k, HI)
                    act.wait_ge(s_wt, c + 1)
                    act.activation(dst, chunk_shape(wtmp[:, c % 2, :], f, k), ACT.Copy).then_inc(s_whi, 1)

            for p in range(HP):
                x2_hi(p)
            w_hi(0, range(CHUNKS))
            for n in range(2 * FT):
                half, f = divmod(n, FT)
                w = width(f)
                if n == FT:
                    for p in range(HP, PAIRS):
                        x2_hi(p)
                act.wait_ge(s_g, n + 1)
                if n >= 1:
                    act.wait_ge(s_hval, n)
                act.activation(gact[0:w, :], f_g[0:w, :], ACT.Silu).then_inc(s_gact, 1)
                if n + 1 < FT:
                    w_hi(f + 1, (0, 1))
                act.wait_ge(s_hval, n + 1)
                if n >= 1:
                    act.wait_ge(s_d, n)
                act.activation(hT[0:w, HI, :], hval[0:w, :], ACT.Copy).then_inc(s_hhi, 1)
                if n + 1 < FT:
                    w_hi(f + 1, (2, 3, 4, 5))

        def dve_ffn(dve):
            dve.wait_ge(s_acc, UNITS)

            for p in range(PAIRS):
                ln_stats(dve, X2, p)
                if p >= 1 and p < 3:
                    ln_apply(dve, X2, p - 1, xn2[:, (p - 1) % 2, :], 0)
                if p >= 3 and p < HP + 1:
                    dve.wait_ge(s_x2hi, p - 2)
                    x2_lo(dve, p - 3)
                    ln_apply(dve, X2, p - 1, xn2[:, (p - 1) % 2, :], 0)
                if p == HP:
                    break
            for p in range(HP - 2, HP):
                dve.wait_ge(s_x2hi, p + 1)
                x2_lo(dve, p)
            for p in range(HP + 1, PAIRS):
                ln_stats(dve, X2, p)

            dve.wait_ge(s_pid, 1)
            dve.tensor_scalar(shift[:, :], pid[:, :], 7, 2, ALU.bitwise_and, ALU.logical_shift_left).then_inc(s_col, 1)
            dve.tensor_scalar(grp_i[:, :], pid[:, :], 31, None, ALU.bitwise_and).then_inc(s_col, 1)
            dve.wait_ge(s_col, 2)
            dve.tensor_copy(grp[:, :], grp_i[:, :]).then_inc(s_col, 1)
            dve.wait_ge(s_idx, 48)
            dve.tensor_copy(idx_f[:, :], idx_raw[:, :]).then_inc(s_idx_v, 1)
            dve.wait_ge(s_idx_v, 1)
            for cols, g in ((slice(0, 2 * D), GG), (slice(2 * D, 2 * D + F), GD)):
                dve.tensor_scalar(idx_n[:, cols], idx_f[:, cols], 0.0, float(g), ALU.is_lt, ALU.mult).then_inc(s_idx_v, 1)
            dve.wait_ge(s_idx_v, 3)
            dve.tensor_tensor(idx_f[:, :], idx_f[:, :], idx_n[:, :], ALU.add).then_inc(s_idx_v, 1)
            dve.wait_ge(s_idx_v, 4)
            for cols, g in ((slice(0, 2 * D), GG), (slice(2 * D, 2 * D + F), GD)):
                dve.tensor_scalar(idx_n[:, cols], idx_f[:, cols], float(g - 1), 0.0, ALU.min, ALU.max).then_inc(s_idx_v, 1)
            dve.wait_ge(s_idx_v, 6)
            dve.wait_ge(s_col, 3)
            dve.tensor_scalar(oh_gu[:, :, :].rearrange("p m k -> p (m k)"), idx_n[:, 0:2 * D], grp[:, 0:1], None,
                              ALU.is_equal)
            dve.tensor_scalar(oh_d[:, :], idx_n[:, 2 * D:2 * D + F], grp[:, 0:1], None, ALU.is_equal).then_inc(s_idx_v, 1)

            dve.wait_ge(s_zraw, 48)
            for j in range(8):
                for g, lo, hi in ((GG, GATE, UP + F), (GD, DOWN, DOWN + D)):
                    dve.tensor_scalar(z_int[0:g, lo // 8:hi // 8, j], z_raw[0:g, lo // 8:hi // 8], 4 * j, 15,
                                      ALU.logical_shift_right, ALU.bitwise_and).then_inc(s_zero_v, 1)
            dve.wait_ge(s_zero_v, 16)
            dve.wait_ge(s_zero, 2)
            for g, lo, hi in ((GG, GATE, UP + F), (GD, DOWN, DOWN + D)):
                dve.tensor_scalar(zs[0:g, 0, lo:hi], z_int[0:g, lo // 8:hi // 8, :].rearrange("p c j -> p (c j)"), 1, None,
                                  ALU.add).then_inc(s_zero_v, 1)
            dve.wait_ge(s_sraw, 16 * 9)
            dve.tensor_copy(zs[:, 1, :], s_raw[:, :]).then_inc(s_scale_v, 1)
            dve.wait_ge(s_scale_v, 1)
            dve.tensor_tensor(s_raw[64:P, :], s_raw[64:P, :], zs[64:P, 1, :], ALU.subtract).then_inc(s_scale_v, 1)
            dve.wait_ge(s_scale_v, 2)
            dve.tensor_copy(zs[64:P, 1, :], s_raw[64:P, :]).then_inc(s_scale_v, 1)
            dve.wait_ge(s_scale_v, 3)
            dve.tensor_tensor(s_raw[96:P, :], s_raw[96:P, :], zs[96:P, 1, :], ALU.subtract).then_inc(s_scale_v, 1)
            dve.wait_ge(s_scale_v, 4)
            dve.tensor_copy(zs[96:P, 1, :], s_raw[96:P, :]).then_inc(s_scale_v, 1)

            def dequant(f, ks):
                w = width(f)
                for k in ks:
                    c = CHUNKS * f + k
                    kind = k // 2
                    if k % 2 == 0:
                        dve.wait_ge(s_packed[kind], (64, 64, 16)[kind] * (f + 1))
                    if c >= 1:
                        dve.wait_ge(s_nib, 2 * c)
                    raw = chunk_shape(packed[:, kind, (k % 2) * 256:(k % 2 + 1) * 256], f, k)
                    n_, i_, t_ = (chunk_shape(v, f, k) for v in (nib[:, :], wint[:, :], wtmp[:, c % 2, :]))
                    rows = P if k < 4 else w
                    dve.tensor_scalar(n_, raw, shift[0:rows, 0:1], 15, ALU.logical_shift_right,
                                      ALU.bitwise_and).then_inc(s_nib, 1)
                    dve.wait_ge(s_nib, 2 * c + 1)
                    dve.wait_ge(s_zs, c + 1)
                    if c >= 1:
                        dve.wait_ge(s_wt, c)
                    dve.tensor_tensor(i_, n_, zero_scale(f, k, 0), ALU.subtract).then_inc(s_nib, 1)
                    dve.wait_ge(s_nib, 2 * c + 2)
                    if c >= 2:
                        dve.wait_ge(s_wlo, c - 1)
                    dve.tensor_tensor(t_, i_, zero_scale(f, k, 1), ALU.mult).then_inc(s_wt, 1)

            dequant(0, range(CHUNKS))
            for n in range(2 * FT):
                half, f = divmod(n, FT)
                w = width(f)
                if n == FT - 1:
                    for p in (HP, HP + 1):
                        ln_apply(dve, X2, p, xn2[:, p % 2, :], 0)
                if n == FT:
                    for p in range(HP, PAIRS):
                        dve.wait_ge(s_x2hi, p + 1)
                        x2_lo(dve, p)
                        if p + 2 < PAIRS:
                            ln_apply(dve, X2, p + 2, xn2[:, p % 2, :], 0)
                    add_down(dve, 0)
                if n + 1 < FT:
                    dequant(f + 1, (0, 1))
                dve.wait_ge(s_gact, n + 1)
                dve.wait_ge(s_u, n + 1)
                if n >= 1:
                    dve.wait_ge(s_hlo, n)
                dve.tensor_tensor(hval[0:w, :], gact[0:w, :], f_u[0:w, :], ALU.mult).then_inc(s_hval, 1)
                dve.wait_ge(s_hhi, n + 1)
                dve.tensor_tensor(hT[0:w, LO, :], hval[0:w, :], hT[0:w, HI, :].bitcast(F32), ALU.subtract).then_inc(s_hlo, 1)
                if n + 1 < FT:
                    dequant(f + 1, (2, 3, 4, 5))
            add_down(dve, 1)

        def x2_lo(dve, p):
            dve.tensor_tensor(x2_tile(LO, p), tiles(f_z[p % 2]), x2_tile(HI, p).bitcast(F32), ALU.subtract).then_inc(s_x2lo, 1)

        def add_down(dve, half):
            dve.wait_ge(s_d, FT * (half + 1))
            for t in range(HP):
                p = half * HP + t
                dve.tensor_tensor(acc[:, p, :], f_d[t][:, :], acc[:, p, :], ALU.add).then_inc(s_y2, 1)

        c_s = (bank[0], bank[1], bank[2], bank[7])
        c_t = bank[3:5]
        c_v, c_c = bank[5], bank[6]
        TILES = B * KT
        HEAD1 = PERIOD1 = 4 * KT
        ROUNDS1 = 2
        LT, LV, LY = 6, 8, 9
        STEPS1 = TILES + LY
        PT_ = 2 * KT
        s_cx = sems("s_cx", 2)
        (s_bn3, s_st3, s_rs3, s_xn3, s_cR, s_cRl, s_qR, s_qRl, s_ct, s_vT, s_vTl, s_vz) = (
            sem(f"s_{n}") for n in ("bn3", "st3", "rs3", "xn3", "cR", "cRl", "qR", "qRl", "ct", "vT", "vTl", "vz"))
        (s_s1, s_m1, s_e1, s_r1, s_n1, s_n1p, s_t1, s_p1, s_p1l, s_v1, s_y3) = (
            sem(f"s_{n}") for n in ("s1", "m1", "e1", "r1", "n1", "n1p", "t1", "p1", "p1l", "v1", "y3"))

        def acc_at(p):
            if isinstance(p, int):
                return acc[:, p, :]
            return acc[:, bass.ds(p, 1), :].rearrange("p o d -> p (o d)")

        def prepared(st):
            q = st.j // PT_ + 1
            if isinstance(st.i, int) and q >= PAIRS:
                return None
            return q + st.i * (PERIOD1 // PT_), q % 2

        def current(st):
            q = st.j // PT_
            return q + st.i * (PERIOD1 // PT_), q % 2

        def sp_l1x(sp):
            sp.wait_ge(s_y2, PAIRS)
            for q in range(PAIRS):
                if q >= 2:
                    sp.wait_ge(s_ct, q - 1)
                    sp.wait_ge(s_cRl, q - 1)
                sp.dma_start(cx[:, q % 2, :], ctx_t[q]).then_inc(s_cx[q % 2], 16)

        def arrived(eng, q, par):
            eng.wait_ge(s_cx[par], 8 * (q - par) + 16)

        def dve_stats(dve, q):
            dve.bn_stats(st3[:, :], acc_at(q)).then_inc(s_bn3, 1)

        def dve_aggregate(dve, q, par):
            dve.bn_aggr(mv3[:, par, :], st3[:, :]).then_inc(s_bn3, 1)
            dve.wait_ge(s_bn3, 2 * q + 2)
            dve.tensor_scalar(mv3[:, par, 1:2], mv3[:, par, 1:2], LN_EPS, None, ALU.add).then_inc(s_st3, 1)

        def pool_norm(pool, q, par):
            pool.wait_ge(s_st3, q + 1)
            pool.tensor_tensor(rs3[:, par, 0:1], mv3[:, par, 1:2], half_neg[:, 0:1], ALU.pow).then_inc(s_rs3, 1)
            pool.wait_ge(s_rs3, 2 * q + 1)
            pool.tensor_tensor(rs3[:, par, 1:2], rs3[:, par, 0:1], inv_sqrt_t[:, :], ALU.mult).then_inc(s_rs3, 1)

        def dve_queries(dve, q, par):
            dve.wait_ge(s_rs3, 2 * q + 2)
            wait(dve, s_qRl, q - 1)
            dve.tensor_scalar(xn3[:, par, :], acc_at(q), mv3[:, par, 0:1], rs3[:, par, 1:2],
                              ALU.subtract, ALU.mult).then_inc(s_xn3, 1)

        def act_context(act, q, par):
            arrived(act, q, par)
            wait(act, s_s1, PT_ * (q - 1))
            act.activation(cR[:, par, HI, :], cx[:, par, :], ACT.Copy).then_inc(s_cR, 1)

        def pool_context(pool, q, par):
            pool.wait_ge(s_cR, q + 1)
            pool.tensor_tensor(cR[:, par, LO, :], cx[:, par, :], cR[:, par, HI, :].bitcast(F32),
                               ALU.subtract).then_inc(s_cRl, 1)

        def act_queries(act, q, par):
            act.wait_ge(s_xn3, q + 1)
            wait(act, s_s1, PT_ * (q - 1))
            act.activation(qR[:, par, HI, :], xn3[:, par, :], ACT.Copy).then_inc(s_qR, 1)

        def pool_queries(pool, q, par):
            pool.wait_ge(s_qR, q + 1)
            pool.tensor_tensor(qR[:, par, LO, :], xn3[:, par, :], qR[:, par, HI, :].bitcast(F32),
                               ALU.subtract).then_inc(s_qRl, 1)

        def pe_context(pe, q, par):
            arrived(pe, q, par)
            wait(pe, s_vTl, q)
            for t in range(KT):
                mm = pe.transpose(c_c[:, t * P:(t + 1) * P], cx[:, par, t * P:(t + 1) * P], ident[:, :])
            mm.then_inc(s_ct, 1)

        def vT_of(par, part):
            return vTz[:, par, :, part, :].rearrange("p t (x c) -> p t x c", x=3)[:, :, 0::2, :]

        def c_view():
            return c_c[:, :].rearrange("p (t b c) -> p t b c", t=KT, b=2)

        def act_values(act, q, par):
            act.wait_ge(s_ct, q + 1)
            wait(act, s_v1, PT_ * (q - 1))
            act.activation(vT_of(par, HI), c_view(), ACT.Copy).then_inc(s_vT, 1)

        def dve_values(dve, q, par):
            dve.wait_ge(s_vT, q + 1)
            dve.tensor_tensor(vT_of(par, LO), c_view(), vT_of(par, HI).bitcast(F32), ALU.subtract).then_inc(s_vTl, 1)

        def pe_l1x(pe):
            pe.wait_ge(s_y2, PAIRS)
            run_steps(pe, pe_step1, HEAD1, PERIOD1, ROUNDS1, STEPS1)

        def pe_step1(st):
            pe = nc.tensor
            if st.has(0, TILES):
                t = st.j
                par, r0, n = t // PT_ % 2, t // KT % 2 * T, t % KT
                if t % PT_ == 0:
                    pe.wait_ge(s_cRl, st.i * 2 + t // PT_ + 1)
                    pe.wait_ge(s_qRl, st.i * 2 + t // PT_ + 1)
                wait(pe, s_e1, st.done(4))
                for k, (l, r) in enumerate(PASSES):
                    mm = pe.matmul(c_s[t % 4][:, :], cR[r0:r0 + T, par, l, n * P:(n + 1) * P],
                                   qR[r0:r0 + T, par, r, :], start=(k == 0), stop=(k == 2))
                mm.then_inc(s_s1, 1)
            if st.has(LT, TILES):
                t = st.j - LT
                b, m = t // KT % 4, t % KT
                if m == 0:
                    pe.wait_ge(s_n1, 2 * (t // KT + 1) + st.i * 8)
                    pe.wait_ge(s_n1p, 2 * (t // KT + 1) + st.i * 8)
                wait(pe, s_p1l, st.done(LT + 2))
                for n in range(KT):
                    mm = pe.transpose(c_t[t % 2][:, n * P:(n + 1) * P], pr[:, b, n, m * P:(m + 1) * P], ident[:, :])
                mm.then_inc(s_t1, 1)
            if st.has(LV, TILES):
                t = st.j - LV
                par, b, m = t // PT_ % 2, t // KT % 2, t % KT
                if t % PT_ == 0:
                    pe.wait_ge(s_vz, 1)
                    pe.wait_ge(s_vTl, st.i * 2 + t // PT_ + 1)
                    wait(pe, s_y3, st.i * 2 + t // PT_)
                pe.wait_ge(s_p1l, st.done(LV))
                for k, (l, r) in enumerate(PASSES):
                    mm = pe.matmul(c_v[:, :], vTz[:, par, m, l, b * T:b * T + P], pmT[:, t % 4, r, :],
                                   start=(t % PT_ == 0 and k == 0), stop=(t % PT_ == PT_ - 1 and k == 2))
                mm.then_inc(s_v1, 1)
            if st.j % PT_ == 1 and st.has(0, TILES):
                pe_context(pe, *current(st))

        def act_l1x(act):
            act.wait_ge(s_y2, PAIRS)
            act_context(act, 0, 0)
            act_queries(act, 0, 0)
            run_steps(act, act_step1, HEAD1, PERIOD1, ROUNDS1, STEPS1)

        def act_step1(st):
            act = nc.scalar
            if st.has(LT, TILES):
                t = st.j - LT
                act.wait_ge(s_t1, st.done(LT))
                wait(act, s_v1, st.done(LT + 4))
                act.activation(pmT[:, t % 4, HI, :], c_t[t % 2][:, :], ACT.Copy).then_inc(s_p1, 1)
            if st.has(0, TILES):
                t = st.j
                act.wait_ge(s_m1, st.done(0))
                if t % KT == 0:
                    wait(act, s_t1, st.done(0) - 1 - 3 * KT)
                wait(act, s_r1, st.done(4))
                act.activation(pr[:, t // KT % 4, t % KT, :], c_s[t % 4][:, :], ACT.Exp, bias=nm1[:, t % 4:t % 4 + 1],
                               accum_out=sm1[:, t % 4:t % 4 + 1]).then_inc(s_e1, 1)
            if prepared(st):
                if st.j % PT_ == 1:
                    act_context(act, *prepared(st))
                if st.j % PT_ == 5:
                    act_queries(act, *prepared(st))
            if st.j % PT_ == 2 and st.has(0, TILES):
                act_values(act, *current(st))

        def dve_l1x(dve):
            dve.wait_ge(s_y2, PAIRS)
            dve.memset(vTz[:, :, :, :, T:2 * T].bitcast(F32), 0.0).then_inc(s_vz, 1)
            dve_stats(dve, 0)
            dve.wait_ge(s_bn3, 1)
            dve_aggregate(dve, 0, 0)
            dve_queries(dve, 0, 0)
            run_steps(dve, dve_step1, HEAD1, PERIOD1, ROUNDS1, STEPS1)

        def dve_step1(st):
            dve = nc.vector
            norm = prepared(st) if st.j % PT_ == 0 else None
            if norm:
                dve_stats(dve, norm[0])
            if st.has(0, TILES):
                t = st.j
                dve.wait_ge(s_s1, st.done(0))
                wait(dve, s_e1, st.done(4))
                if norm:
                    dve.wait_ge(s_bn3, 2 * norm[0] + 1)
                dve.tensor_reduce(nm1[:, t % 4:t % 4 + 1], c_s[t % 4][:, :], AX, ALU.max, negate=True).then_inc(s_m1, 1)
            if norm:
                dve_aggregate(dve, *norm)
            if st.has(LT, TILES):
                t = st.j - LT
                dve.wait_ge(s_p1, st.done(LT))
                dve.tensor_tensor(pmT[:, t % 4, LO, :], c_t[t % 2][:, :], pmT[:, t % 4, HI, :].bitcast(F32),
                                  ALU.subtract).then_inc(s_p1l, 1)
            if st.has(1, TILES):
                t = st.j - 1
                dve.wait_ge(s_e1, st.done(1))
                if t % 2:
                    wait(dve, s_n1p, pool_normed(st, 1, t) - 2)
                else:
                    wait(dve, s_n1, pool_normed(st, 1, t) - 2)
                dve.reciprocal(rc1[:, t % 4:t % 4 + 1], sm1[:, t % 4:t % 4 + 1]).then_inc(s_r1, 1)
                if t % 2 == 0:
                    dve.wait_ge(s_r1, st.done(1))
                    dve.tensor_scalar(pr[:, t // KT % 4, t % KT, :], pr[:, t // KT % 4, t % KT, :],
                                      rc1[:, t % 4:t % 4 + 1], None, ALU.mult).then_inc(s_n1, 1)
            if st.has(LY, TILES) and (st.j - LY) % PT_ == PT_ - 1:
                q = (st.j - LY) // PT_ + st.i * 2
                dve.wait_ge(s_v1, st.done(LY))
                dve.tensor_tensor(acc_at(q), c_v[:, :], acc_at(q), ALU.add).then_inc(s_y3, 1)
            if prepared(st):
                if st.j % PT_ == 3:
                    dve_queries(dve, *prepared(st))
            if st.j % PT_ == 4 and st.has(0, TILES):
                dve_values(dve, *current(st))

        def pool_normed(st, lag, t):
            return t // 2 + 1 + st.i * (PERIOD1 // 2)

        def pool_l1x(pool):
            pool.wait_ge(s_y2, PAIRS)
            pool_norm(pool, 0, 0)
            pool_context(pool, 0, 0)
            pool_queries(pool, 0, 0)
            run_steps(pool, pool_step1, HEAD1, PERIOD1, ROUNDS1, STEPS1)

        def pool_step1(st):
            pool = nc.gpsimd
            if st.has(1, TILES) and (st.j - 1) % 2 == 1:
                t = st.j - 1
                pool.wait_ge(s_r1, st.done(1))
                pool.tensor_tensor(pr[:, t // KT % 4, t % KT, :], pr[:, t // KT % 4, t % KT, :],
                                   rc1[:, t % 4:t % 4 + 1].to_broadcast([P, D]), ALU.mult).then_inc(s_n1p, 1)
            if prepared(st):
                if st.j % PT_ == 1:
                    pool_norm(pool, *prepared(st))
                if st.j % PT_ == 3:
                    pool_context(pool, *prepared(st))
                if st.j % PT_ == 6:
                    pool_queries(pool, *prepared(st))

        s_ld_o, s_ld_q, s_ld_u = sem("s_ld_o"), sem("s_ld_q"), sem("s_ld_u")
        s_ld_d = sems("s_ld_d", KT)
        (s_wot, s_woh, s_wol, s_sm, s_smc, s_dnh, s_dnl, s_uph, s_upl, s_tx4, s_x4h, s_x4l, s_mean) = (
            sem(f"s_{n}") for n in ("wot", "woh", "wol", "sm", "smc", "dnh", "dnl", "uph", "upl", "tx4", "x4h", "x4l", "mean"))
        (s_h4, s_hv4, s_hh4, s_hl4, s_o4, s_y4, s_cv, s_ce) = (
            sem(f"s_{n}") for n in ("h4", "hv4", "hh4", "hl4", "o4", "y4", "cv", "ce"))
        m_x = bank[4:6]
        m_h = bank[6:8]
        m_o = bank[0:4]
        X4 = 2
        W_LATE = HP

        def sp_l1f(sp):
            sp.wait_ge(s_y3, PAIRS)
            sp.dma_start(worg[:, :, :], a["L1_ffn_W_org"].rearrange("(t p) i -> p t i", p=P)).then_inc(s_ld_o, 16)
            sp.dma_start(wq1[:, :], a["L1_ffn_Wq"]).then_inc(s_ld_q, 16)
            sp.dma_start(keys[:, :], a["L1_ffn_lora_keys"]).then_inc(s_ld_q, 16)
            down_t = a["L1_ffn_lora_down"].rearrange("e (t p) r -> t p e r", p=P)
            for t in range(KT):
                sp.dma_start(draw[:, t, :].rearrange("p (e r) -> p e r", e=EXP), down_t[t]).then_inc(s_ld_d[t], 16)
            sp.dma_start(uraw[:, :, :], a["L1_ffn_lora_up"].rearrange("e r o -> (e r) o")
                         .rearrange("(t p) o -> p t o", p=P)).then_inc(s_ld_u, 16)
            for p in range(PAIRS):
                sp.wait_ge(s_y4, p + 1)
                sp.dma_start(out_t[p], acc[:, p, :]).then_inc(s_out, 16)
            sp.wait_ge(s_out, 16 * PAIRS)

        def pool_l1f(pool):
            pool.wait_ge(s_y3, PAIRS)
            for p in range(PAIRS):
                ln_power(pool, X4, p)
            for t in range(KT):
                pool.wait_ge(s_dnh, t + 1)
                pool.tensor_tensor(dn[:, LO, t, :], draw[:, t, :], dn[:, HI, t, :].bitcast(F32), ALU.subtract).then_inc(s_dnl, 1)
            for t in range(KT):
                pool.wait_ge(s_uph, t + 1)
                pool.tensor_tensor(up[:, LO, t, :], uraw[:, t, :], up[:, HI, t, :].bitcast(F32), ALU.subtract).then_inc(s_upl, 1)
            for n in range(2 * KT):
                half, t = divmod(n, KT)
                cols = slice(half * HALF, (half + 1) * HALF)
                pool.wait_ge(s_hh4, n + 1)
                pool.tensor_tensor(hs[:, LO, t, cols], hval4[:, n % 2, :], hs[:, HI, t, cols].bitcast(F32),
                                   ALU.subtract).then_inc(s_hl4, 1)

        def pe_l1f(pe):
            pe.wait_ge(s_y3, PAIRS)

            def x_tile(p):
                pe.wait_ge(s_xn, 2 * PAIRS + p + 1)
                if p >= 2:
                    pe.wait_ge(s_x4l, p - 1)
                    pe.wait_ge(s_mean, p - 1)
                for kt in range(KT):
                    mm = pe.transpose(m_x[p % 2][:, kt * P:(kt + 1) * P], xn4[:, p % 2, kt * P:(kt + 1) * P], ident[:, :])
                mm.then_inc(s_tx4, 1)

            def base(p):
                pe.wait_ge(s_x4l, p + 1)
                if p >= HP:
                    pe.wait_ge(s_y4, p - HP + 1)
                for kt in range(KT):
                    for k, (l, r) in enumerate(PASSES):
                        pe.matmul(m_o[p % HP][:, :], x4T[:, l, kt, p * P:(p + 1) * P], woT[:, r, kt, :],
                                  start=(kt == 0 and k == 0), stop=False)

            def delta(p):
                pe.wait_ge(s_hl4, KT * (p // HP + 1))
                pe.wait_ge(s_upl, KT)
                for t in range(KT):
                    for k, (l, r) in enumerate(PASSES):
                        mm = pe.matmul(m_o[p % HP][:, :], hs[:, l, t, p * P:(p + 1) * P], up[:, r, t, :],
                                       start=False, stop=(t == KT - 1 and k == 2))
                mm.then_inc(s_o4, 1)

            def low_rank(n):
                half, j = divmod(n, KT)
                if n >= 2:
                    pe.wait_ge(s_hv4, n - 1)
                pe.wait_ge(s_dnl, KT)
                for kt in range(KT):
                    for k, (l, r) in enumerate(PASSES):
                        mm = pe.matmul(m_h[n % 2][:, :], dn[:, l, kt, j * P:(j + 1) * P],
                                       x4T[:, r, kt, half * HALF:(half + 1) * HALF],
                                       start=(kt == 0 and k == 0), stop=(kt == KT - 1 and k == 2))
                mm.then_inc(s_h4, 1)

            x_tile(0)
            x_tile(1)
            pe.wait_ge(s_ld_q, 32)
            for kt in range(KT):
                pe.transpose(m_h[0][:, kt * P:(kt + 1) * P], wq1[:, kt * P:(kt + 1) * P], ident[:, :])
            pe.transpose(m_h[1][:, 0:EXP], keys[:, :], ident[0:EXP, 0:EXP]).then_inc(s_sm, 1)
            pe.wait_ge(s_ld_o, 16)
            for it in range(KT):
                for ot in range(KT):
                    mm = pe.transpose(m_o[it][:, ot * P:(ot + 1) * P], worg[:, ot, it * P:(it + 1) * P], ident[:, :])
                mm.then_inc(s_wot, 1)
            x_tile(2)
            x_tile(3)
            pe.wait_ge(s_wol, KT)
            for p in range(HP):
                base(p)
                x_tile(HP + p)
            pe.wait_ge(s_mean, PAIRS)
            pe.wait_ge(s_smc, 2)
            for kt in range(KT):
                mm = pe.matmul(m_h[0][:, 0:B], wq1T[:, kt, :], meanT[:, kt, :], start=(kt == 0), stop=(kt == KT - 1))
            mm.then_inc(s_sm, 1)
            pe.wait_ge(s_smc, 3)
            pe.matmul(m_h[1][0:B, 0:EXP], q1T[:, :], keysT[:, :], start=True, stop=True).then_inc(s_sm, 1)
            pe.wait_ge(s_cv, 5)
            for t in range(KT):
                mm = pe.transpose(m_h[0][:, t * B:(t + 1) * B],
                                  cexp[:, :, :].rearrange("b e r -> b (e r)")[:, t * P:(t + 1) * P], ident[0:B, 0:B])
            mm.then_inc(s_sm, 1)
            pe.wait_ge(s_smc, 4)
            for n in range(KT):
                low_rank(n)
            for n in range(KT):
                low_rank(KT + n)
                delta(n)
            for p in range(HP, PAIRS):
                base(p)
                delta(p)

        def act_l1f(act):
            act.wait_ge(s_y3, PAIRS)

            def x_hi(p):
                act.wait_ge(s_tx4, p + 1)
                act.activation(x4T[:, HI, :, p * P:(p + 1) * P], tiles(m_x[p % 2]), ACT.Copy).then_inc(s_x4h, 1)

            x_hi(0)
            x_hi(1)
            act.wait_ge(s_sm, 1)
            act.activation(wq1T[:, :, :].rearrange("p t k -> p (t k)"), m_h[0][:, :], ACT.Copy).then_inc(s_smc, 1)
            act.activation(keysT[:, :], m_h[1][:, 0:EXP], ACT.Copy).then_inc(s_smc, 1)
            for t in range(KT):
                act.wait_ge(s_wot, t + 1)
                act.activation(woT[:, HI, t, :], m_o[t][:, :], ACT.Copy).then_inc(s_woh, 1)
            for p in range(2, PAIRS):
                x_hi(p)
                if p < 2 + KT:
                    act.wait_ge(s_ld_d[p - 2], 16)
                    act.activation(dn[:, HI, p - 2, :], draw[:, p - 2, :], ACT.Copy).then_inc(s_dnh, 1)
            act.wait_ge(s_ld_u, 16)
            for t in range(KT):
                act.activation(up[:, HI, t, :], uraw[:, t, :], ACT.Copy).then_inc(s_uph, 1)
            act.wait_ge(s_sm, 2)
            act.activation(q1T[:, :], m_h[0][:, 0:B], ACT.Copy, scale=1.0 / T).then_inc(s_smc, 1)
            act.wait_ge(s_cv, 2)
            act.activation(cf[:, :], lg[:, :], ACT.Exp, bias=cstat[:, 0:1], accum_out=cstat[:, 1:2]).then_inc(s_ce, 1)
            act.wait_ge(s_sm, 4)
            act.activation(cT[:, :, :].rearrange("p t b -> p (t b)"), m_h[0][:, 0:KT * B], ACT.Copy).then_inc(s_smc, 1)
            for n in range(2 * KT):
                half, t = divmod(n, KT)
                act.wait_ge(s_hv4, n + 1)
                act.activation(hs[:, HI, t, half * HALF:(half + 1) * HALF], hval4[:, n % 2, :], ACT.Copy).then_inc(s_hh4, 1)

        def dve_l1f(dve):
            dve.wait_ge(s_y3, PAIRS)

            def x_lo(p):
                dve.wait_ge(s_x4h, p + 1)
                dve.tensor_tensor(x4T[:, LO, :, p * P:(p + 1) * P], tiles(m_x[p % 2]),
                                  x4T[:, HI, :, p * P:(p + 1) * P].bitcast(F32), ALU.subtract).then_inc(s_x4l, 1)
                dve.tensor_reduce(meanT[:, :, 2 * p:2 * p + 2], m_x[p % 2][:, :].rearrange("p (k b t) -> p k b t", k=KT, b=2),
                                  AX, ALU.add).then_inc(s_mean, 1)

            for p in range(PAIRS + 1):
                if p < PAIRS:
                    ln_stats(dve, X4, p)
                if p >= 1:
                    if p >= 3:
                        dve.wait_ge(s_tx4, p - 2)
                    ln_apply(dve, X4, p - 1, xn4[:, (p - 1) % 2, :], 0)
                if p == 3:
                    for t in range(KT):
                        dve.wait_ge(s_woh, t + 1)
                        dve.tensor_tensor(woT[:, LO, t, :], m_o[t][:, :], woT[:, HI, t, :].bitcast(F32),
                                          ALU.subtract).then_inc(s_wol, 1)
                if p >= 2:
                    x_lo(p - 2)
            x_lo(PAIRS - 1)
            dve.wait_ge(s_sm, 3)
            dve.tensor_scalar(lg[:, :], m_h[1][0:B, 0:EXP], float(KD) ** -0.5, None, ALU.mult).then_inc(s_cv, 1)
            dve.wait_ge(s_cv, 1)
            dve.tensor_reduce(cstat[:, 0:1], lg[:, :], AX, ALU.max, negate=True).then_inc(s_cv, 1)
            dve.wait_ge(s_ce, 1)
            dve.reciprocal(cstat[:, 2:3], cstat[:, 1:2]).then_inc(s_cv, 1)
            dve.wait_ge(s_cv, 3)
            dve.tensor_scalar(lg[:, :], cf[:, :], cstat[:, 2:3], None, ALU.mult).then_inc(s_cv, 1)
            dve.wait_ge(s_cv, 4)
            dve.tensor_copy(cexp[:, :, :], lg[:, :].unsqueeze(2).to_broadcast([B, EXP, RANK])).then_inc(s_cv, 1)
            dve.wait_ge(s_smc, 4)

            def add_out(p):
                dve.wait_ge(s_o4, p + 1)
                dve.tensor_tensor(acc[:, p, :], m_o[p % HP][:, :], acc[:, p, :], ALU.add).then_inc(s_y4, 1)

            for n in range(2 * KT):
                half, t = divmod(n, KT)
                dve.wait_ge(s_h4, n + 1)
                if n >= 2:
                    dve.wait_ge(s_hl4, n - 1)
                dve.tensor_tensor(hval4[:, n % 2, :].rearrange("p (b t) -> p b t", t=T),
                                  m_h[n % 2][:, :].rearrange("p (b t) -> p b t", t=T),
                                  cT[:, t, half * B // 2:(half + 1) * B // 2].unsqueeze(2).to_broadcast([P, B // 2, T]),
                                  ALU.mult).then_inc(s_hv4, 1)
                if n > KT:
                    add_out(n - KT - 1)
            for p in range(HP - 1, PAIRS):
                add_out(p)


        s_out = sem("s_out")

        @block.sync
        def _(sp):
            sp_first(sp)
            sp_ffn(sp)
            sp_l1x(sp)
            sp_l1f(sp)

        @block.gpsimd
        def _(pool):
            pool.memset(ident[:, :], 0.0).then_inc(s_const, 1)
            pool.memset(half_neg[:, :], -0.5).then_inc(s_const, 1)
            pool.memset(inv_sqrt_t[:, :], float(T) ** -0.5).then_inc(s_const, 1)
            pool.wait_ge(s_const, 3)
            pool.affine_select(out=ident[:, :], in_=ident[:, :], compare_op=ALU.not_equal, fill=1.0, base=0,
                               pattern=[[-1, P]], channel_multiplier=1).then_inc(s_const, 1)
            pool_first(pool)
            pool_ffn(pool)
            pool_l1x(pool)
            pool_l1f(pool)

        @block.tensor
        def _(pe):
            pe_first(pe)
            pe_ffn(pe)
            pe_l1x(pe)
            pe_l1f(pe)

        @block.scalar
        def _(act):
            act_first(act)
            act_ffn(act)
            act_l1x(act)
            act_l1f(act)

        @block.vector
        def _(dve):
            dve_first(dve)
            dve_ffn(dve)
            dve_l1x(dve)
            dve_l1f(dve)


def kernel(**inputs):
    import numpy as _np
    import concourse.bacc as _bacc
    from concourse.bass_utils import run_bass_kernel_spmd as _run

    nc = _bacc.Bacc("TRN2", target_bir_lowering=False, num_devices=1)
    arrays, aps = {}, {}
    for name, value in inputs.items():
        v = _np.ascontiguousarray(value)
        arrays[f"in_{name}_dram"] = v
        aps[name] = nc.dram_tensor(f"in_{name}_dram", v.shape, mybir.dt.from_np(v.dtype), kind="ExternalInput").ap()
    out = nc.dram_tensor("out_0_dram", inputs["x"].shape, F32, kind="ExternalOutput").ap()
    block_kernel(nc, aps, out)
    r = _run(nc, [arrays], core_ids=[0])
    return r.results[0]["out_0_dram"]
```

```python
from contextlib import ExitStack

import concourse.bass as bass
from concourse import mybir

F32 = mybir.dt.float32
F32R = mybir.dt.float32r
BF16 = mybir.dt.bfloat16
I32 = mybir.dt.int32
ALU = mybir.AluOpType
ACT = mybir.ActivationFunctionType
AX = mybir.AxisListType.X

P = 128
HI, LO = 0, 1
PASSES = ((HI, HI), (HI, LO), (LO, HI))


class Step:

    def __init__(self, i, j, period):
        self.i, self.j, self.period = i, j, period

    def done(self, lag=0, per=1):
        return per * self.period * self.i + per * (self.j - lag + 1)

    def has(self, lag, units):
        return not isinstance(self.i, int) or 0 <= self.j - lag < units


def wait(eng, sem, value):
    if not isinstance(value, int) or value > 0:
        eng.wait_ge(sem, value)


def run_steps(eng, step, head, period, rounds, total, after=None):
    for j in range(head):
        step(Step(0, j, period))
    with eng.Fori(0, rounds) as i:
        for j in range(head, head + period):
            step(Step(i, j, period))
    for j in range(head + period * rounds, total):
        step(Step(0, j, period))
        if after is not None:
            after(j)


def block_kernel(nc, a, out, stop=None):
    x, ctx_in = a["x"], a["ctx_4096"]
    Wq, Wk, Wv, Wo = (a[f"L0_xattn_{n}"] for n in ("Wq", "Wk", "Wv", "Wo"))
    B, T, D = x.shape
    HD = a["L0_xattn_q_norm_w"].shape[0]
    KVH = Wk.shape[1] // HD
    G = Wq.shape[1] // HD // KVH
    KT = D // P
    PAIRS = B * T // P
    UNITS = KVH * PAIRS
    QW = G * HD
    QKV = QW + 2 * HD
    RMS_EPS, LN_EPS = 1e-6, 1e-5
    F = a["L0_ffn_gate_qweight"].shape[1]
    GG = a["L0_ffn_gate_scales"].shape[0]
    GD = a["L0_ffn_down_scales"].shape[0]
    FT = -(-F // P)
    HALF = B * T // 2
    EXP = a["L1_ffn_lora_down"].shape[0]
    RANK = a["L1_ffn_lora_down"].shape[2]
    KD = a["L1_ffn_Wq"].shape[0]
    assert (T, D, HD, G, PAIRS, KVH, QW, EXP * RANK) == (64, 512, 128, 4, 8, 8, 512, 512)

    x_t = x.rearrange("(q b) t d -> q (b t) d", b=2)
    ctx_t = ctx_in.rearrange("(q b) t d -> q (b t) d", b=2)
    out_t = out.rearrange("(q b) t d -> q (b t) d", b=2)

    root = ExitStack()
    with root:
        def sb(name, shape, dt, scope=root):
            return scope.enter_context(nc.sbuf_tensor(name, shape, dt))

        def sem(name):
            return root.enter_context(nc.semaphore(name))

        def sems(name, n):
            return [sem(f"{name}{k}") for k in range(n)]

        bank = [root.enter_context(nc.psum_tensor(f"bank{k}", [P, 512], F32)) for k in range(8)]

        acc = sb("acc", [P, PAIRS, D], F32)
        ident = sb("ident", [P, P], F32)
        half_neg = sb("half_neg", [P, 8], F32)
        inv_sqrt_t = sb("inv_sqrt_t", [P, 1], F32)
        stat = sb("stat", [P, 16, 6], F32)
        mv = sb("mv", [P, 4, PAIRS, 2], F32)
        rstd = sb("rstd", [P, 4, PAIRS], F32)
        wqk = sb("wqk", [P, 4], F32)

        s0 = ExitStack()
        kvT = sb("kvT", [P, 2, KT, PAIRS, 4, T], F32R, s0)
        wqkv_raw = sb("wqkv_raw", [P, 2, QKV], F32, s0)
        wo_raw = sb("wo_raw", [P, 2, D], F32, s0)
        wqkv = sb("wqkv", [P, 2, 2, KT, QKV], F32R, s0)
        wo = sb("wo", [P, 2, 2, G, D], F32R, s0)
        s0a = ExitStack()
        ctx_raw = sb("ctx_raw", [P, 4, D], F32, s0a)
        xn0 = sb("xn0", [P, 2, D], F32, s0a)
        s0a.close()
        s0b = ExitStack()
        qsq = sb("qsq", [P, G, HD], F32, s0b)
        ksq = sb("ksq", [P, 2, HD], F32, s0b)
        qn = sb("qn", [P, G, HD], F32, s0b)
        kn = sb("kn", [P, 2, HD], F32, s0b)
        qT = sb("qT", [P, 2, G, T], F32, s0b)
        kT = sb("kT", [P, 2, P], F32, s0b)
        vv = sb("vv", [P, 2, 2, 2, HD], F32R, s0b)
        prob = sb("prob", [P, 2 * 2, P], F32, s0b)
        pT = sb("pT", [P, 2, 2, G * T], F32R, s0b)
        aoT = sb("aoT", [P, 2, G, 2, T], F32R, s0b)
        ssq = sb("ssq", [P, 6], F32, s0b)
        msq = sb("msq", [P, 6], F32, s0b)
        rms = sb("rms", [P, 6], F32, s0b)
        nmax = sb("nmax", [P, 4], F32, s0b)
        psum_row = sb("psum_row", [P, 4], F32, s0b)
        rsum = sb("rsum", [P, 4], F32, s0b)
        s_raw = sb("s_raw", [P, 2 * F + D], F32, s0b)
        s0b.close()
        s0.close()

        GATE, UP, DOWN = 0, F, 2 * F
        ZS = 2 * F + D
        s1 = ExitStack()
        wd = sb("wd", [P, FT, 2, D], F32R, s1)
        x2T = sb("x2T", [P, 2, KT, HALF], F32R, s1)
        hT = sb("hT", [P, 2, HALF], F32R, s1)
        zs = sb("zs", [P, 2, ZS], BF16, s1)
        oh_gu = sb("oh_gu", [P, 2, D], BF16, s1)
        oh_d = sb("oh_d", [P, F], BF16, s1)
        pid = sb("pid", [P, 1], I32, s1)
        shift = sb("shift", [P, 1], I32, s1)
        grp_i = sb("grp_i", [P, 1], I32, s1)
        grp = sb("grp", [P, 1], F32, s1)
        s1a = ExitStack()
        z_raw = sb("z_raw", [32, ZS // 8], I32, s1a)
        z_int = sb("z_int", [32, ZS // 8, 8], I32, s1a)
        s1a.close()
        s1c = ExitStack()
        below_wo = 2 * KT * PAIRS * 4 * T + 2 * QKV + 2 * D + 2 * 2 * KT * QKV
        so_far = FT * 2 * D + 2 * KT * HALF + 2 * HALF + ZS + D + F // 2 + 4
        sb("gap", [P, below_wo - so_far], F32, s1c)
        idx_raw = sb("idx_raw", [P, 2 * D + F], I32, s1c)
        idx_n = sb("idx_n", [P, F], F32, s1c)
        s1c.close()
        s1b = ExitStack()
        packed = sb("packed", [P, 3, 512], I32, s1b)
        nib = sb("nib", [P, 256], I32, s1b)
        wint = sb("wint", [P, 256], F32, s1b)
        wtmp = sb("wtmp", [P, 2, 256], F32, s1b)
        xn2 = sb("xn2", [P, 2, D], F32, s1b)
        wgu = sb("wgu", [P, FT, 2, 2, KT, P], F32R, s1b)
        gact = sb("gact", [P, HALF], F32, s1b)
        hval = sb("hval", [P, HALF], F32, s1b)
        s1b.close()
        s1.close()

        s2 = ExitStack()
        cx = sb("cx", [P, 2, D], F32, s2)
        cR = sb("cR", [P, 2, 2, D], F32R, s2)
        vTz = sb("vTz", [P, 2, KT, 2, 3 * T], F32R, s2)
        xn3 = sb("xn3", [P, 2, D], F32, s2)
        qR = sb("qR", [P, 2, 2, D], F32R, s2)
        pr = sb("pr", [P, 4, KT, D], F32, s2)
        pmT = sb("pmT", [P, 4, 2, D], F32R, s2)
        st3 = sb("st3", [P, 6], F32, s2)
        mv3 = sb("mv3", [P, 2, 2], F32, s2)
        rs3 = sb("rs3", [P, 2, 2], F32, s2)
        nm1 = sb("nm1", [P, 4], F32, s2)
        sm1 = sb("sm1", [P, 4], F32, s2)
        rc1 = sb("rc1", [P, 4], F32, s2)
        s2.close()

        s3 = ExitStack()
        x4T = sb("x4T", [P, 2, KT, B * T], F32R, s3)
        woT = sb("woT", [P, 2, KT, D], F32R, s3)
        dn = sb("dn", [P, 2, KT, EXP * RANK], F32R, s3)
        up = sb("up", [P, 2, KT, D], F32R, s3)
        hs = sb("hs", [P, 2, KT, B * T], F32R, s3)
        worg = sb("worg", [P, KT, D], F32, s3)
        draw = sb("draw", [P, KT, EXP * RANK], F32, s3)
        uraw = sb("uraw", [P, KT, D], F32, s3)
        wq1 = sb("wq1", [P, D], F32, s3)
        wq1T = sb("wq1T", [P, KT, KD], F32, s3)
        keys = sb("keys", [EXP, KD], F32, s3)
        keysT = sb("keysT", [P, EXP], F32, s3)
        xn4 = sb("xn4", [P, 2, D], F32, s3)
        meanT = sb("meanT", [P, KT, B], F32, s3)
        q1T = sb("q1T", [P, B], F32, s3)
        lg = sb("lg", [B, EXP], F32, s3)
        cf = sb("cf", [B, EXP], F32, s3)
        cstat = sb("cstat", [B, 4], F32, s3)
        cexp = sb("cexp", [B, EXP, RANK], F32, s3)
        cT = sb("cT", [P, KT, B], F32, s3)
        hval4 = sb("hval4", [P, 2, 512], F32, s3)
        s3.close()

        s_const = sem("s_const")
        s_stat, s_rstd, s_xn = sem("s_stat"), sem("s_rstd"), sem("s_xn")
        sx, sc = sems("s_x", PAIRS), sems("s_ctx", PAIRS)

        block = root.enter_context(nc.Block())

        s_nw = sem("s_nw")
        s_wqk = sem("s_wqk")
        s_wqkv_in, s_wo_in = sems("s_wqkv_in", 2), sems("s_wo_in", 2)
        s_wqkv_hi, s_wqkv = sem("s_wqkv_hi"), sem("s_wqkv")
        s_wo_hi, s_wo = sem("s_wo_hi"), sem("s_wo")
        s_tc, s_tx = sem("s_tc"), sem("s_tx")
        s_chi, s_clo, s_xhi, s_xlo = sem("s_chi"), sem("s_clo"), sem("s_xhi"), sem("s_xlo")
        s_q, s_kv, s_t, s_s, s_pt, s_pv, s_o = (sem(f"s_{n}") for n in ("q", "kv", "t", "s", "pt", "pv", "o"))
        s_qsq, s_ksq, s_qT, s_kT, s_vhi, s_exp, s_phi, s_aohi = (
            sem(f"s_{n}") for n in ("qsq", "ksq", "qT", "kT", "vhi", "exp", "phi", "aohi"))
        s_qms, s_kms, s_qn, s_kn, s_vlo, s_max, s_plo, s_pn, s_aolo, s_acc = (
            sem(f"s_{n}") for n in ("qms", "kms", "qn", "kn", "vlo", "max", "plo", "pn", "aolo", "acc"))
        s_red = sem("s_red")
        s_rq, s_rk = sem("s_rq"), sem("s_rk")
        s_rec = sem("s_rec")
        b_q, b_kv, b_tq, b_tk, b_s, b_pt, b_pv, b_o = bank

        HEAD, PERIOD = 8, 2 * PAIRS
        ROUNDS = (UNITS - HEAD) // PERIOD
        STEPS0 = UNITS + 4

        def unit(st, lag):
            u = st.j - lag
            return u % PAIRS, u // PAIRS % 2, u % 2

        def sp_first(sp):
            sp.dma_start(wqk[:, 0:1], a["L0_xattn_q_norm_w"].rearrange("(d o) -> d o", o=1)).then_inc(s_nw, 16)
            sp.dma_start(wqk[:, 1:2], a["L0_xattn_k_norm_w"].rearrange("(d o) -> d o", o=1)).then_inc(s_nw, 16)

            def qkv_piece(g, kt, freed):
                wait(sp, s_wqkv, freed)
                rows, slot = slice(kt * P, (kt + 1) * P), kt % 2
                sp.dma_start(wqkv_raw[:, slot, 0:QW], Wq[rows, bass.ds(g * QW, QW)]).then_inc(s_wqkv_in[slot], 16)
                sp.dma_start(wqkv_raw[:, slot, QW:QW + HD], Wk[rows, bass.ds(g * HD, HD)]).then_inc(s_wqkv_in[slot], 16)
                sp.dma_start(wqkv_raw[:, slot, QW + HD:QKV], Wv[rows, bass.ds(g * HD, HD)]).then_inc(s_wqkv_in[slot], 16)

            def wo_piece(g, h, freed):
                wait(sp, s_wo, freed)
                sp.dma_start(wo_raw[:, h % 2, :], Wo[bass.ds(g * QW + h * HD, HD), :]).then_inc(s_wo_in[h % 2], 16)

            def group(g):
                for n in range(4):
                    qkv_piece(g, n, 4 * g + n - 1)
                    if n == 0:
                        wo_piece(g - 1, 3, 4 * g - 2)
                    else:
                        wo_piece(g, n - 1, 4 * g + n - 2)

            for p in range(2):
                sp.dma_start(acc[:, p, :], x_t[p]).then_inc(sx[p], 16)
                sp.dma_start(ctx_raw[:, p, :], ctx_t[p]).then_inc(sc[p], 16)
            qkv_piece(0, 0, 0)
            qkv_piece(0, 1, 0)
            for p in range(2, 4):
                sp.dma_start(acc[:, p, :], x_t[p]).then_inc(sx[p], 16)
                sp.dma_start(ctx_raw[:, p, :], ctx_t[p]).then_inc(sc[p], 16)
            wo_piece(0, 0, 0)
            qkv_piece(0, 2, 1)
            wo_piece(0, 1, 0)
            for p in range(4, PAIRS):
                sp.dma_start(acc[:, p, :], x_t[p]).then_inc(sx[p], 16)
                sp.wait_ge(s_clo, p - 3)
                sp.dma_start(ctx_raw[:, p % 4, :], ctx_t[p]).then_inc(sc[p], 16)
            qkv_piece(0, 3, 2)
            wo_piece(0, 2, 1)
            sp_scales(sp)
            with sp.Fori(1, KVH) as g:
                group(g)
            wo_piece(KVH - 1, 3, 4 * KVH - 2)

        def pe_first(pe):
            pe.wait_ge(s_const, 4)
            for p in range(PAIRS + 1):
                if p < PAIRS:
                    b = bank[p % 2]
                    pe.wait_ge(sc[p], 16)
                    if p >= 2:
                        pe.wait_ge(s_clo, p - 1)
                    for kt in range(KT):
                        mm = pe.transpose(b[:, kt * P:(kt + 1) * P], ctx_raw[:, p % 4, kt * P:(kt + 1) * P], ident[:, :])
                    mm.then_inc(s_tc, 1)
                if p >= 1:
                    b = bank[2 + p % 2]
                    pe.wait_ge(s_xn, p)
                    if p >= 3:
                        pe.wait_ge(s_xlo, p - 2)
                    for kt in range(KT):
                        mm = pe.transpose(b[:, kt * P:(kt + 1) * P], xn0[:, (p - 1) % 2, kt * P:(kt + 1) * P], ident[:, :])
                    mm.then_inc(s_tx, 1)
            pe.wait_ge(s_clo, PAIRS)
            pe.wait_ge(s_xlo, PAIRS)
            run_steps(pe, pe_step0, HEAD, PERIOD, ROUNDS, STEPS0, pe_ahead)

        def group_count(st, lag):
            return 4 * ((st.j - lag) // PAIRS + 1) + st.i * 4 * (PERIOD // PAIRS)

        def pe_step0(st):
            pe = nc.tensor
            if st.has(0, UNITS):
                p, par, _ = unit(st, 0)
                if p == 0:
                    pe.wait_ge(s_wqkv, group_count(st, 0))
                wait(pe, s_qn, st.done(1))
                for kt in range(KT):
                    for n, (l, r) in enumerate(PASSES):
                        mm = pe.matmul(b_q[:, :], kvT[:, l, kt, p, 1:3, :], wqkv[:, par, r, kt, 0:QW],
                                       start=(kt == 0 and n == 0), stop=(kt == KT - 1 and n == 2))
                mm.then_inc(s_q, 1)
            if st.has(1, UNITS):
                pe.wait_ge(s_qn, st.done(1))
                wait(pe, s_qT, st.done(2))
                wait(pe, s_kT, st.done(2))
                for h in range(G):
                    pe.transpose(b_tq[:, h * P:(h + 1) * P], qn[:, h, :], ident[:, :])
                pe.wait_ge(s_kn, st.done(1))
                for b in range(2):
                    mm = pe.transpose(b_tk[:, b * P:(b + 1) * P], kn[:, b, :], ident[:, :])
                mm.then_inc(s_t, 1)
            if st.has(0, UNITS):
                p, par, _ = unit(st, 0)
                wait(pe, s_vlo, st.done(1))
                wait(pe, s_kn, st.done(1))
                for b in range(2):
                    for kt in range(KT):
                        for n, (l, r) in enumerate(PASSES):
                            mm = pe.matmul(b_kv[:, b * 256:(b + 1) * 256], kvT[:, l, kt, p, 2 * b:2 * b + 2, :],
                                           wqkv[:, par, r, kt, QW:QKV],
                                           start=(kt == 0 and n == 0), stop=(kt == KT - 1 and n == 2))
                mm.then_inc(s_kv, 1)
            if st.has(1, UNITS):
                pe.wait_ge(s_qT, st.done(1))
                pe.wait_ge(s_kT, st.done(1))
                wait(pe, s_exp, st.done(2, 4))
                for b in range(2):
                    for hp in range(2):
                        n = b * 2 + hp
                        mm = pe.matmul(b_s[:, n * P:(n + 1) * P], qT[:, b, 2 * hp:2 * hp + 2, :], kT[:, b, :],
                                       start=True, stop=True)
                mm.then_inc(s_s, 1)
            if st.has(2, UNITS):
                pe.wait_ge(s_pn, st.done(2))
                wait(pe, s_plo, st.done(3))
                for n in range(4):
                    mm = pe.transpose(b_pt[:, n * P:(n + 1) * P], prob[:, n, :], ident[:, :])
                mm.then_inc(s_pt, 1)
            if st.has(3, UNITS):
                p, par, _ = unit(st, 3)
                if p == 0:
                    pe.wait_ge(s_wo, group_count(st, 3))
                pe.wait_ge(s_aolo, st.done(3))
                wait(pe, s_acc, st.done(4))
                for h in range(G):
                    for n, (l, r) in enumerate(PASSES):
                        mm = pe.matmul(b_o[:, :], aoT[:, l, h, :, :], wo[:, par, r, h, :],
                                       start=(h == 0 and n == 0), stop=(h == G - 1 and n == 2))
                mm.then_inc(s_o, 1)
            if st.has(2, UNITS):
                _, _, par = unit(st, 2)
                pe.wait_ge(s_plo, st.done(2))
                pe.wait_ge(s_vlo, st.done(2))
                wait(pe, s_aolo, st.done(3))
                for b in range(2):
                    for n, (l, r) in enumerate(PASSES):
                        mm = pe.matmul(b_pv[:, b * 256:(b + 1) * 256], vv[:, par, l, b, :], pT[:, r, b, :],
                                       start=(n == 0), stop=(n == 2))
                mm.then_inc(s_pv, 1)

        def weight_piece(st):
            j = st.j % PAIRS
            return {0: ("qkv", 0, 1), 1: ("wo", 3, 0), 2: ("qkv", 1, 1), 3: ("wo", 0, 1),
                    4: ("qkv", 2, 1), 5: ("wo", 1, 1), 6: ("qkv", 3, 1), 7: ("wo", 2, 1)}[j]

        def piece_of(st):
            kind, n, ahead = weight_piece(st)
            gj = st.j // PAIRS + ahead
            exists = not isinstance(st.i, int) or gj < KVH
            g = gj + st.i * (PERIOD // PAIRS)
            return kind, n, g, gj, exists

        def hi_piece(act, st):
            kind, n, g, gj, exists = piece_of(st)
            if not exists:
                return
            par = gj % 2
            if kind == "qkv":
                act.wait_ge(s_wqkv_in[n % 2], 48 * (2 * g + n // 2 + 1))
                wait(act, s_kv, (8 * (g - 1)) if gj >= 2 else 0)
                act.activation(wqkv[:, par, HI, n, :], wqkv_raw[:, n % 2, :], ACT.Copy).then_inc(s_wqkv_hi, 1)
            else:
                act.wait_ge(s_wo_in[n % 2], 16 * (2 * g + n // 2 + 1))
                wait(act, s_o, (8 * (g - 1)) if gj >= 2 else 0)
                act.activation(wo[:, par, HI, n, :], wo_raw[:, n % 2, :], ACT.Copy).then_inc(s_wo_hi, 1)

        def lo_piece(pool, st):
            kind, n, g, gj, exists = piece_of(st)
            if not exists:
                return
            par = gj % 2
            if kind == "qkv":
                pool.wait_ge(s_wqkv_hi, 4 * g + n + 1)
                pool.tensor_tensor(wqkv[:, par, LO, n, :], wqkv_raw[:, n % 2, :],
                                   wqkv[:, par, HI, n, :].bitcast(F32), ALU.subtract).then_inc(s_wqkv, 1)
            else:
                pool.wait_ge(s_wo_hi, 4 * g + n + 1)
                pool.tensor_tensor(wo[:, par, LO, n, :], wo_raw[:, n % 2, :],
                                   wo[:, par, HI, n, :].bitcast(F32), ALU.subtract).then_inc(s_wo, 1)

        def kv_context(part, p):
            return kvT[:, part, :, p, 0::3, :]

        def kv_latents(part, p):
            return kvT[:, part, :, p, 1:3, :]

        def by_batch(b):
            return b[:, :].rearrange("p (k b t) -> p k b t", k=KT, b=2)

        def act_first(act):
            for p in range(PAIRS + 1):
                if p < PAIRS:
                    act.wait_ge(s_tc, p + 1)
                    act.activation(kv_context(HI, p), by_batch(bank[p % 2]), ACT.Copy).then_inc(s_chi, 1)
                if p >= 1:
                    act.wait_ge(s_tx, p)
                    act.activation(kv_latents(HI, p - 1), by_batch(bank[2 + p % 2]), ACT.Copy).then_inc(s_xhi, 1)
                if 1 <= p <= 4:
                    kt = p - 1
                    act.wait_ge(s_wqkv_in[kt % 2], 48 * (kt // 2 + 1))
                    act.activation(wqkv[:, 0, HI, kt, :], wqkv_raw[:, kt % 2, :], ACT.Copy).then_inc(s_wqkv_hi, 1)
                if 5 <= p <= 7:
                    h = p - 5
                    act.wait_ge(s_wo_in[h % 2], 16 * (h // 2 + 1))
                    act.activation(wo[:, 0, HI, h, :], wo_raw[:, h % 2, :], ACT.Copy).then_inc(s_wo_hi, 1)
            act.wait_ge(s_clo, PAIRS)
            act.wait_ge(s_tx, PAIRS)
            act.wait_ge(s_wqk, 2)
            run_steps(act, act_step0, HEAD, PERIOD, ROUNDS, STEPS0, act_ahead)

        def act_step0(st):
            act = nc.scalar
            if st.has(3, UNITS):
                act.wait_ge(s_pv, st.done(3))
                wait(act, s_o, st.done(4))
                act.activation(aoT[:, HI, :, :, :], b_pv[:, :].rearrange("p (b h t) -> p h b t", b=2, h=G),
                               ACT.Copy).then_inc(s_aohi, 1)
            if st.has(1, UNITS):
                _, _, par = unit(st, 1)
                act.wait_ge(s_kn, st.done(1))
                wait(act, s_pv, st.done(3))
                act.activation(vv[:, par, HI, :, :], b_kv[:, :].rearrange("p (b c) -> p b c", b=2)[:, :, HD:2 * HD],
                               ACT.Copy).then_inc(s_vhi, 1)
            if st.has(0, UNITS):
                act.wait_ge(s_q, st.done(0))
                wait(act, s_qms, st.done(1))
                act.activation(qsq[:, :, :], b_q[:, :].rearrange("p (h d) -> p h d", h=G), ACT.Square).then_inc(s_qsq, 1)
            if st.has(1, UNITS):
                act.wait_ge(s_t, st.done(1))
                wait(act, s_s, st.done(2))
                act.activation(qT[:, :, :, :].rearrange("p b h t -> p h b t"),
                               b_tq[:, :].rearrange("p (h b t) -> p h b t", h=G, b=2), ACT.Copy).then_inc(s_qT, 1)
                act.activation(kT[:, :, :], b_tk[:, 0:2 * P].rearrange("p (b k) -> p b k", b=2), ACT.Copy,
                               scale=wqk[:, 3:4]).then_inc(s_kT, 1)
            if st.has(0, UNITS):
                act.wait_ge(s_kv, st.done(0))
                wait(act, s_kms, st.done(1))
                act.activation(ksq[:, :, :], b_kv[:, :].rearrange("p (b c) -> p b c", b=2)[:, :, 0:HD],
                               ACT.Square).then_inc(s_ksq, 1)
            if st.has(2, UNITS):
                act.wait_ge(s_pt, st.done(2))
                wait(act, s_pv, st.done(3))
                act.activation(pT[:, HI, :, :], b_pt[:, :].rearrange("p (b q) -> p b q", b=2), ACT.Copy).then_inc(s_phi, 1)
            if st.has(1, UNITS):
                act.wait_ge(s_max, st.done(1))
                wait(act, s_pt, st.done(2))
                wait(act, s_rec, st.done(2))
                for n in range(4):
                    act.activation(prob[:, n, :], b_s[:, n * P:(n + 1) * P], ACT.Exp, bias=nmax[:, n:n + 1],
                                   accum_out=psum_row[:, n:n + 1]).then_inc(s_exp, 1)
            hi_piece(act, st)

        def dve_step0(st):
            dve = nc.vector
            if st.has(3, UNITS):
                dve.wait_ge(s_aohi, st.done(3))
                dve.tensor_tensor(aoT[:, LO, :, :, :], b_pv[:, :].rearrange("p (b h t) -> p h b t", b=2, h=G),
                                  aoT[:, HI, :, :, :].bitcast(F32), ALU.subtract).then_inc(s_aolo, 1)
            if st.has(4, UNITS):
                p, _, _ = unit(st, 4)
                dve.wait_ge(s_o, st.done(4))
                dve.tensor_tensor(acc[:, p, :], b_o[:, :], acc[:, p, :], ALU.add).then_inc(s_acc, 1)
            if st.has(1, UNITS):
                _, _, par = unit(st, 1)
                dve.wait_ge(s_vhi, st.done(1))
                dve.tensor_tensor(vv[:, par, LO, :, :], b_kv[:, :].rearrange("p (b c) -> p b c", b=2)[:, :, HD:2 * HD],
                                  vv[:, par, HI, :, :].bitcast(F32), ALU.subtract).then_inc(s_vlo, 1)
            if st.has(0, UNITS):
                dve.wait_ge(s_qsq, st.done(0))
                wait(dve, s_rq, st.done(1))
                dve.tensor_reduce(ssq[:, 0:4], qsq[:, :, :], AX, ALU.add).then_inc(s_red, 1)
                dve.wait_ge(s_red, st.done(0, 2) - 1)
                dve.tensor_scalar(msq[:, 0:4], ssq[:, 0:4], 1.0 / HD, RMS_EPS, ALU.mult, ALU.add).then_inc(s_qms, 1)
                dve.wait_ge(s_rq, st.done(0))
                wait(dve, s_t, st.done(1))
                dve.tensor_tensor(qn[:, :, :], b_q[:, :].rearrange("p (h d) -> p h d", h=G),
                                  rms[:, 0:4].unsqueeze(2).to_broadcast([P, G, HD]), ALU.mult).then_inc(s_qn, 1)
                dve.wait_ge(s_ksq, st.done(0))
                wait(dve, s_rk, st.done(1))
                dve.tensor_reduce(ssq[:, 4:6], ksq[:, :, :], AX, ALU.add).then_inc(s_red, 1)
                dve.wait_ge(s_red, st.done(0, 2))
                dve.tensor_scalar(msq[:, 4:6], ssq[:, 4:6], 1.0 / HD, RMS_EPS, ALU.mult, ALU.add).then_inc(s_kms, 1)
            if st.has(1, UNITS):
                dve.wait_ge(s_s, st.done(1))
                wait(dve, s_exp, st.done(2, 4))
                dve.tensor_reduce(nmax[:, :], b_s[:, :].rearrange("p (n k) -> p n k", n=4), AX, ALU.max,
                                  negate=True).then_inc(s_max, 1)
            if st.has(2, UNITS):
                dve.wait_ge(s_phi, st.done(2))
                dve.tensor_tensor(pT[:, LO, :, :].rearrange("p b q -> p (b q)"), b_pt[:, :],
                                  pT[:, HI, :, :].rearrange("p b q -> p (b q)").bitcast(F32),
                                  ALU.subtract).then_inc(s_plo, 1)
            if st.has(0, UNITS):
                dve.wait_ge(s_rk, st.done(0))
                wait(dve, s_t, st.done(1))
                dve.tensor_tensor(kn[:, :, :], b_kv[:, :].rearrange("p (b c) -> p b c", b=2)[:, :, 0:HD],
                                  rms[:, 4:6].unsqueeze(2).to_broadcast([P, 2, HD]), ALU.mult).then_inc(s_kn, 1)
            if st.has(1, UNITS):
                dve.wait_ge(s_exp, st.done(1, 4))
                wait(dve, s_pn, st.done(2))
                dve.reciprocal(rsum[:, :], psum_row[:, :]).then_inc(s_rec, 1)
                dve.wait_ge(s_rec, st.done(1))
                dve.tensor_tensor(prob[:, :, :], prob[:, :, :], rsum[:, :].unsqueeze(2).to_broadcast([P, 4, P]),
                                  ALU.mult).then_inc(s_pn, 1)

        def dve_first(dve):
            dve.wait_ge(s_nw, 32)
            dve.tensor_tensor(wqk[:, 2:3], wqk[:, 0:1], wqk[:, 1:2], ALU.mult).then_inc(s_wqk, 1)
            dve.wait_ge(s_wqk, 1)
            dve.tensor_scalar(wqk[:, 3:4], wqk[:, 2:3], float(HD) ** -0.5, None, ALU.mult).then_inc(s_wqk, 1)
            for p in range(PAIRS + 2):
                if p < PAIRS:
                    dve.wait_ge(sx[p], 16)
                    ln_stats(dve, 0, p)
                if 1 <= p <= PAIRS:
                    if p >= 3:
                        dve.wait_ge(s_tx, p - 2)
                    ln_apply(dve, 0, p - 1, xn0[:, (p - 1) % 2, :])
                if p < PAIRS:
                    dve.wait_ge(s_chi, p + 1)
                    dve.tensor_tensor(kv_context(LO, p), by_batch(bank[p % 2]), kv_context(HI, p).bitcast(F32),
                                      ALU.subtract).then_inc(s_clo, 1)
                if p >= 2:
                    dve.wait_ge(s_xhi, p - 1)
                    dve.tensor_tensor(kv_latents(LO, p - 2), by_batch(bank[2 + (p - 1) % 2]),
                                      kv_latents(HI, p - 2).bitcast(F32), ALU.subtract).then_inc(s_xlo, 1)
            run_steps(dve, dve_step0, HEAD, PERIOD, ROUNDS, STEPS0, dve_ahead)

        def pool_first(pool):
            pool.memset(s_raw[:, :], 0.0).then_inc(s_zero, 1)
            for p in range(PAIRS):
                ln_power(pool, 0, p)
                if p < 4:
                    pool.wait_ge(s_wqkv_hi, p + 1)
                    pool.tensor_tensor(wqkv[:, 0, LO, p, :], wqkv_raw[:, p % 2, :], wqkv[:, 0, HI, p, :].bitcast(F32),
                                       ALU.subtract).then_inc(s_wqkv, 1)
                if 4 <= p < 7:
                    h = p - 4
                    pool.wait_ge(s_wo_hi, h + 1)
                    pool.tensor_tensor(wo[:, 0, LO, h, :], wo_raw[:, h % 2, :], wo[:, 0, HI, h, :].bitcast(F32),
                                       ALU.subtract).then_inc(s_wo, 1)
            pool.wait_ge(s_clo, PAIRS)
            pool.wait_ge(s_tx, PAIRS)
            run_steps(pool, pool_step0, HEAD, PERIOD, ROUNDS, STEPS0, pool_ahead)

        def pool_step0(st):
            pool = nc.gpsimd
            if st.has(0, UNITS):
                pool.wait_ge(s_qms, st.done(0))
                wait(pool, s_qn, st.done(1))
                pool.tensor_tensor(rms[:, 0:4], msq[:, 0:4], half_neg[:, 0:4], ALU.pow).then_inc(s_rq, 1)
                pool.wait_ge(s_kms, st.done(0))
                wait(pool, s_kn, st.done(1))
                pool.tensor_tensor(rms[:, 4:6], msq[:, 4:6], half_neg[:, 4:6], ALU.pow).then_inc(s_rk, 1)
            lo_piece(pool, st)

        s_bn = sem("s_bn")

        def ln_stats(dve, which, p):
            n = which * PAIRS + p
            dve.bn_stats(stat[:, n % 16, :], acc[:, p, :]).then_inc(s_bn, 1)
            dve.wait_ge(s_bn, 2 * n + 1)
            dve.bn_aggr(mv[:, which, p, :], stat[:, n % 16, :]).then_inc(s_bn, 1)
            dve.wait_ge(s_bn, 2 * n + 2)
            dve.tensor_scalar(mv[:, which, p, 1:2], mv[:, which, p, 1:2], LN_EPS, None, ALU.add).then_inc(s_stat, 1)

        def ln_power(pool, which, p):
            pool.wait_ge(s_stat, which * PAIRS + p + 1)
            pool.tensor_tensor(rstd[:, which, p:p + 1], mv[:, which, p, 1:2], half_neg[:, 0:1], ALU.pow).then_inc(s_rstd, 1)

        def ln_apply(dve, which, p, to):
            dve.wait_ge(s_rstd, which * PAIRS + p + 1)
            dve.tensor_scalar(to, acc[:, p, :], mv[:, which, p, 0:1], rstd[:, which, p:p + 1],
                              ALU.subtract, ALU.mult).then_inc(s_xn, 1)

        s_pid, s_col, s_zero = sem("s_pid"), sem("s_col"), sem("s_zero")
        s_idx, s_sraw, s_zraw = sem("s_idx"), sem("s_sraw"), sem("s_zraw")
        s_idx_v, s_scale_v, s_zero_v = sem("s_idx_v"), sem("s_scale_v"), sem("s_zero_v")
        s_packed = sems("s_packed", 3)
        s_nib, s_zs, s_wt, s_whi, s_wlo = sem("s_nib"), sem("s_zs"), sem("s_wt"), sem("s_whi"), sem("s_wlo")
        s_tx2, s_x2hi, s_x2lo = sem("s_tx2"), sem("s_x2hi"), sem("s_x2lo")
        s_g, s_u, s_d, s_gact, s_hval, s_hhi, s_hlo, s_y2 = (
            sem(f"s_{n}") for n in ("g", "u", "d", "gact", "hval", "hhi", "hlo", "y2"))
        f_g, f_u = bank[0], bank[1]
        f_z = bank[2:4]
        f_d = bank[4:8]
        SCALE_ROWS = (0, 64, 96)
        TABLES = (("gate", GATE, F, GG), ("up", UP, F, GG), ("down", DOWN, D, GD))
        CHUNKS = 6
        HP = PAIRS // 2
        EVEN_DONE = UNITS - PAIRS
        s_rest = sem("s_rest")
        HALF_ZS, QUARTER_ZS = ZS // 2, ZS // 4
        X2 = 1

        def width(f):
            return min(P, F - f * P)

        def sp_scales(sp):
            sp.wait_ge(s_zero, 1)
            for m, at, n, g in TABLES:
                for row in SCALE_ROWS:
                    sp.dma_start(s_raw[row:row + g, at:at + n], a[f"L0_ffn_{m}_scales"]).then_inc(s_sraw, 16)

        def sp_ffn(sp):
            sp.wait_ge(s_q, EVEN_DONE)
            sp.wait_ge(s_kv, EVEN_DONE)
            for m, at, n, g in TABLES:
                sp.dma_start(z_raw[0:g, at // 8:(at + n) // 8], a[f"L0_ffn_{m}_qzeros"]).then_inc(s_zraw, 16)
            sp.wait_ge(s_o, EVEN_DONE)
            for n, (m, count) in enumerate((("gate", D), ("up", D), ("down", F))):
                sp.dma_start(idx_raw[:, n * D:n * D + count],
                             a[f"L0_ffn_{m}_g_idx"].rearrange("(o k) -> o k", o=1).to_broadcast([P, count])).then_inc(s_idx, 16)
            sp.wait_ge(s_zero_v, 18)
            for f in range(FT):
                w = width(f)
                for k, m in enumerate(("gate", "up")):
                    if f >= 1:
                        sp.wait_ge(s_nib, 2 * (CHUNKS * (f - 1) + 2 * k + 2) - 1)
                    rows = a[f"L0_ffn_{m}_qweight"].rearrange("(t r) n -> t r n", t=KT)
                    for kt in range(KT):
                        sp.dma_start(packed[:, k, kt * P:kt * P + w],
                                     rows[kt, :, f * P:f * P + w].unsqueeze(1).to_broadcast([P // 8, 8, w])
                                     ).then_inc(s_packed[k], 16)
                if f >= 1:
                    sp.wait_ge(s_nib, 2 * CHUNKS * f - 1)
                sp.dma_start(packed[0:w, 2, :],
                             a["L0_ffn_down_qweight"][f * P // 8:(f * P + w) // 8, :].unsqueeze(1)
                             .to_broadcast([w // 8, 8, D])).then_inc(s_packed[2], 16)

        def pool_ahead(j):
            pool = nc.gpsimd
            n = j - EVEN_DONE
            if n == 1:
                pool.wait_ge(s_kv, EVEN_DONE)
                pool.wait_ge(s_wo, 4 * KVH)
                pool.iota(pid[:, :], pattern=[[0, 1]], base=0, channel_multiplier=1).then_inc(s_pid, 1)
                pool.memset(zs[:, 0, :], 0.0).then_inc(s_zero, 1)
            if 2 <= n <= 5:
                half = n % 2
                pool.wait_ge(s_scale_v, n - 1)
                for q in (2 * half, 2 * half + 1):
                    cols = slice(q * QUARTER_ZS, (q + 1) * QUARTER_ZS)
                    pool.tensor_tensor(s_raw[:, cols], s_raw[:, cols], zs[:, 1, cols],
                                       ALU.subtract).then_inc(s_rest, 1)
            if 5 <= n <= 8:
                ln_power(pool, X2, n - 5)
            if 9 <= n <= 11:
                w_lo(pool, 0, (2 * (n - 9), 2 * (n - 9) + 1))

        def w_lo(pool, f, ks):
            for k in ks:
                c = CHUNKS * f + k
                dst, rows = weight_chunk(f, k, LO)
                hi, _ = weight_chunk(f, k, HI)
                pool.wait_ge(s_whi, c + 1)
                pool.tensor_tensor(dst, chunk_shape(wtmp[:, c % 2, :], f, k), hi.bitcast(F32),
                                   ALU.subtract).then_inc(s_wlo, 1)

        def pool_ffn(pool):
            for p in range(HP, PAIRS):
                ln_power(pool, X2, p)
            for f in range(1, FT):
                w_lo(pool, f, range(CHUNKS))

        def weight_chunk(f, k, part):
            w = width(f)
            if k < 4:
                return wgu[:, f, part, k // 2, 2 * (k % 2):2 * (k % 2) + 2, 0:w], P
            return wd[0:w, f, part, (k - 4) * 256:(k - 3) * 256], w

        def chunk_shape(ap, f, k):
            w = width(f)
            if k < 4:
                return ap.rearrange("p (t n) -> p t n", t=2)[:, :, 0:w]
            return ap[0:w, :]

        def zs_bank(f, k):
            c = CHUNKS * f + k
            return bank[c] if c < 2 else f_z[c % 2]

        def zero_scale(f, k, which):
            b, w = zs_bank(f, k), width(f)
            if k < 4:
                return b[:, :].rearrange("p (t z n) -> p t z n", t=2, z=2)[:, :, which, 0:w]
            return b[0:w, which * 256:(which + 1) * 256]

        def pe_ahead(j):
            pe = nc.tensor
            n = j - UNITS
            if n == 0:
                pe.wait_ge(s_qT, UNITS)
                pe.wait_ge(s_kT, UNITS)
                x2_transposes(pe, 0)
                x2_transposes(pe, 1)
                pe.wait_ge(s_idx_v, 8)
                pe.wait_ge(s_scale_v, 6)
                pe.wait_ge(s_zero_v, 18)
                pe.wait_ge(s_qn, UNITS)
                pe.wait_ge(s_vlo, UNITS)
                spread(pe, 0, (0, 1))
            if n == 1:
                x2_transposes(pe, 2)
                x2_transposes(pe, 3)
            if n == 2:
                spread(pe, 0, (2, 3))
                inner_product(pe, 0, 0)
            if n == 3:
                spread(pe, 0, (4, 5))

        def spread(pe, f, ks):
            w = width(f)
            for k in ks:
                c = CHUNKS * f + k
                b = zs_bank(f, k)
                if c >= 4:
                    pe.wait_ge(s_wt, c - 1)
                elif c >= 2:
                    pe.wait_ge(s_x2lo, HP)
                if k < 4:
                    at = (GATE, UP)[k // 2] + f * P
                    for t in range(2):
                        kt = 2 * (k % 2) + t
                        mm = pe.matmul(b[:, t * 256:(t + 1) * 256].rearrange("p (z n) -> p z n", z=2)[:, :, 0:w],
                                       oh_gu[:, k // 2, kt * P:(kt + 1) * P], zs[:, :, at:at + w],
                                       start=True, stop=True)
                else:
                    at = DOWN + (k - 4) * 256
                    mm = pe.matmul(b[0:w, :].rearrange("p (z n) -> p z n", z=2), oh_d[:, f * P:f * P + w],
                                   zs[:, :, at:at + 256], start=True, stop=True)
                mm.then_inc(s_zs, 1)

        def inner_product(pe, n, m):
            half, f = divmod(n, FT)
            w = width(f)
            b, used, done = ((f_g, s_gact, s_g), (f_u, s_hval, s_u))[m]
            if half == 0:
                pe.wait_ge(s_wlo, CHUNKS * f + 2 * m + 2)
            if n >= 1:
                pe.wait_ge(used, n)
            for kt in range(KT):
                for k, (l, r) in enumerate(PASSES):
                    mm = pe.matmul(b[0:w, :], wgu[:, f, l, m, kt, 0:w], x2T[:, r, kt, :],
                                   start=(kt == 0 and k == 0), stop=(kt == KT - 1 and k == 2))
            mm.then_inc(done, 1)

        def pe_ffn(pe):
            def down(n):
                half, f = divmod(n, FT)
                w = width(f)
                if half == 0:
                    pe.wait_ge(s_wlo, CHUNKS * (f + 1))
                if n == 0:
                    pe.wait_ge(s_acc, UNITS)
                pe.wait_ge(s_hlo, n + 1)
                for t in range(HP):
                    if f == 0 and half == 1:
                        pe.wait_ge(s_y2, t + 1)
                    for k, (l, r) in enumerate(PASSES):
                        mm = pe.matmul(f_d[t][:, :], hT[0:w, l, t * P:(t + 1) * P], wd[0:w, f, r, :],
                                       start=(f == 0 and k == 0), stop=(f == FT - 1 and k == 2))
                mm.then_inc(s_d, 1)

            for n in range(2 * FT):
                half, f = divmod(n, FT)
                if half == 1 and f == 0:
                    pe.wait_ge(s_wt, CHUNKS * FT)
                    for p in range(HP, PAIRS):
                        x2_transposes(pe, p)
                    down(n - 1)
                    pe.wait_ge(s_x2lo, PAIRS)
                if n >= 1:
                    inner_product(pe, n, 0)
                if n + 1 < FT:
                    spread(pe, f + 1, (0, 1))
                inner_product(pe, n, 1)
                if n + 1 < FT:
                    spread(pe, f + 1, (2, 3))
                if f >= 1:
                    down(n - 1)
                if n + 1 < FT:
                    spread(pe, f + 1, (4, 5))
            down(2 * FT - 1)

        def x2_transposes(pe, p):
            pe.wait_ge(s_xn, X2 * PAIRS + p + 1)
            if p == HP:
                pe.wait_ge(s_u, FT)
            if p >= 2:
                pe.wait_ge(s_x2lo, p - 1)
            for kt in range(KT):
                mm = pe.transpose(f_z[p % 2][:, kt * P:(kt + 1) * P], xn2[:, p % 2, kt * P:(kt + 1) * P], ident[:, :])
            mm.then_inc(s_tx2, 1)

        def x2_tile(part, p):
            return x2T[:, part, :, p % HP * P:(p % HP + 1) * P]

        def tiles(b):
            return b[:, :].rearrange("p (k t) -> p k t", k=KT)

        def act_ahead(j):
            act = nc.scalar
            n = j - EVEN_DONE
            if 1 <= n <= 6:
                part, half = divmod(n - 1, 2)
                row = SCALE_ROWS[part]
                cols = slice(half * HALF_ZS, (half + 1) * HALF_ZS)
                if n == 1:
                    act.wait_ge(s_sraw, 16 * 9)
                    act.wait_ge(s_wo, 4 * KVH)
                    act.wait_ge(s_kv, EVEN_DONE)
                if part >= 1:
                    act.wait_ge(s_rest, 2 * (n - 2))
                act.activation(zs[row:P, 1, cols], s_raw[row:P, cols], ACT.Copy).then_inc(s_scale_v, 1)
            if n == 8:
                x2_hi(act, 0)
                x2_hi(act, 1)
            if n == 9:
                x2_hi(act, 2)
                x2_hi(act, 3)
                w_hi(act, 0, (0, 1))
            if n == 10:
                w_hi(act, 0, (2, 3))
            if n == 11:
                w_hi(act, 0, (4, 5))

        def x2_hi(act, p):
            act.wait_ge(s_tx2, p + 1)
            act.activation(x2_tile(HI, p), tiles(f_z[p % 2]), ACT.Copy).then_inc(s_x2hi, 1)

        def w_hi(act, f, ks):
            for k in ks:
                c = CHUNKS * f + k
                dst, _ = weight_chunk(f, k, HI)
                act.wait_ge(s_wt, c + 1)
                act.activation(dst, chunk_shape(wtmp[:, c % 2, :], f, k), ACT.Copy).then_inc(s_whi, 1)

        def act_ffn(act):
            for n in range(2 * FT):
                half, f = divmod(n, FT)
                w = width(f)
                if n == FT:
                    for p in range(HP, PAIRS):
                        x2_hi(act, p)
                act.wait_ge(s_g, n + 1)
                if n >= 1:
                    act.wait_ge(s_hval, n)
                act.activation(gact[0:w, :], f_g[0:w, :], ACT.Silu).then_inc(s_gact, 1)
                if n + 1 < FT:
                    w_hi(act, f + 1, (0, 1))
                act.wait_ge(s_hval, n + 1)
                if n >= 1:
                    act.wait_ge(s_d, n)
                act.activation(hT[0:w, HI, :], hval[0:w, :], ACT.Copy).then_inc(s_hhi, 1)
                if n + 1 < FT:
                    w_hi(act, f + 1, (2, 3, 4, 5))

        def one_hot(dve, cols, g, to, count):
            raw, n = idx_raw[:, cols], idx_n[:, 0:cols.stop - cols.start]
            if count:
                dve.wait_ge(s_idx_v, count)
            dve.tensor_scalar(n, raw, 0.0, float(g), ALU.is_lt, ALU.mult).then_inc(s_idx_v, 1)
            dve.wait_ge(s_idx_v, count + 1)
            dve.tensor_tensor(n, raw, n, ALU.add).then_inc(s_idx_v, 1)
            dve.wait_ge(s_idx_v, count + 2)
            dve.tensor_scalar(n, n, float(g - 1), 0.0, ALU.min, ALU.max).then_inc(s_idx_v, 1)
            dve.wait_ge(s_idx_v, count + 3)
            dve.tensor_scalar(to, n, grp[:, 0:1], None, ALU.is_equal).then_inc(s_idx_v, 1)

        ZERO_TABLES = ((GG, GATE, UP + F), (GD, DOWN, DOWN + D))

        def dve_ahead(j):
            dve = nc.vector
            n = j - EVEN_DONE
            if n == 1 or n == 2:
                if n == 1:
                    dve.wait_ge(s_zraw, 48)
                for k in range(4 * (n - 1), 4 * n):
                    for g, lo, hi in ZERO_TABLES:
                        dve.tensor_scalar(z_int[0:g, lo // 8:hi // 8, k], z_raw[0:g, lo // 8:hi // 8], 4 * k, 15,
                                          ALU.logical_shift_right, ALU.bitwise_and).then_inc(s_zero_v, 1)
            if n == 2:
                dve.wait_ge(s_pid, 1)
                dve.tensor_scalar(shift[:, :], pid[:, :], 7, 2, ALU.bitwise_and, ALU.logical_shift_left).then_inc(s_col, 1)
                dve.tensor_scalar(grp_i[:, :], pid[:, :], 31, None, ALU.bitwise_and).then_inc(s_col, 1)
                dve.wait_ge(s_col, 2)
                dve.tensor_copy(grp[:, :], grp_i[:, :]).then_inc(s_col, 1)
            if n == 3:
                dve.wait_ge(s_zero_v, 16)
                dve.wait_ge(s_zero, 2)
                for g, lo, hi in ZERO_TABLES:
                    dve.tensor_scalar(zs[0:g, 0, lo:hi], z_int[0:g, lo // 8:hi // 8, :].rearrange("p c j -> p (c j)"), 1, None,
                                      ALU.add).then_inc(s_zero_v, 1)
            if n == 4:
                dve.wait_ge(s_col, 3)
                dve.wait_ge(s_idx, 48)
                one_hot(dve, slice(0, 2 * D), GG, oh_gu[:, :, :].rearrange("p m k -> p (m k)"), 0)
            if n == 5:
                one_hot(dve, slice(2 * D, 2 * D + F), GD, oh_d[:, :], 4)
            if n == 6 or n == 7:
                dve.wait_ge(s_zero_v, 18)
                ln_apply(dve, X2, n - 6, xn2[:, n - 6, :])
            if n == 9:
                for p in (2, 3):
                    dve.wait_ge(s_tx2, p - 1)
                    ln_apply(dve, X2, p, xn2[:, p % 2, :])
                for p in (0, 1):
                    dve.wait_ge(s_x2hi, p + 1)
                    x2_lo(dve, p)
                dequant(dve, 0, (0, 1))
            if n == 10:
                for p in (2, 3):
                    dve.wait_ge(s_x2hi, p + 1)
                    x2_lo(dve, p)
                dequant(dve, 0, (2, 3))
            if n == 11:
                dequant(dve, 0, (4, 5))
            if n >= 4:
                dve.wait_ge(s_acc, EVEN_DONE + n - 3)
                ln_stats(dve, X2, n - 4)

        def dequant(dve, f, ks):
            w = width(f)
            for k in ks:
                c = CHUNKS * f + k
                kind = k // 2
                if k % 2 == 0:
                    dve.wait_ge(s_packed[kind], (64, 64, 16)[kind] * (f + 1))
                if c >= 1:
                    dve.wait_ge(s_nib, 2 * c)
                raw = chunk_shape(packed[:, kind, (k % 2) * 256:(k % 2 + 1) * 256], f, k)
                n_, i_, t_ = (chunk_shape(v, f, k) for v in (nib[:, :], wint[:, :], wtmp[:, c % 2, :]))
                rows = P if k < 4 else w
                dve.tensor_scalar(n_, raw, shift[0:rows, 0:1], 15, ALU.logical_shift_right,
                                  ALU.bitwise_and).then_inc(s_nib, 1)
                dve.wait_ge(s_nib, 2 * c + 1)
                dve.wait_ge(s_zs, c + 1)
                if c >= 1:
                    dve.wait_ge(s_wt, c)
                dve.tensor_tensor(i_, n_, zero_scale(f, k, 0), ALU.subtract).then_inc(s_nib, 1)
                dve.wait_ge(s_nib, 2 * c + 2)
                if c >= 2:
                    dve.wait_ge(s_wlo, c - 1)
                dve.tensor_tensor(t_, i_, zero_scale(f, k, 1), ALU.mult).then_inc(s_wt, 1)

        def dve_ffn(dve):
            for n in range(2 * FT):
                half, f = divmod(n, FT)
                w = width(f)
                if n == FT - 1:
                    for p in (HP, HP + 1):
                        ln_apply(dve, X2, p, xn2[:, p % 2, :])
                if n == FT:
                    for p in range(HP, PAIRS):
                        dve.wait_ge(s_x2hi, p + 1)
                        x2_lo(dve, p)
                        if p + 2 < PAIRS:
                            ln_apply(dve, X2, p + 2, xn2[:, p % 2, :])
                    add_down(dve, 0)
                if n + 1 < FT:
                    dequant(dve, f + 1, (0, 1))
                dve.wait_ge(s_gact, n + 1)
                dve.wait_ge(s_u, n + 1)
                if n >= 1:
                    dve.wait_ge(s_hlo, n)
                dve.tensor_tensor(hval[0:w, :], gact[0:w, :], f_u[0:w, :], ALU.mult).then_inc(s_hval, 1)
                dve.wait_ge(s_hhi, n + 1)
                dve.tensor_tensor(hT[0:w, LO, :], hval[0:w, :], hT[0:w, HI, :].bitcast(F32), ALU.subtract).then_inc(s_hlo, 1)
                if n + 1 < FT:
                    dequant(dve, f + 1, (2, 3, 4, 5))
            add_down(dve, 1)

        def x2_lo(dve, p):
            dve.tensor_tensor(x2_tile(LO, p), tiles(f_z[p % 2]), x2_tile(HI, p).bitcast(F32), ALU.subtract).then_inc(s_x2lo, 1)

        def add_down(dve, half):
            dve.wait_ge(s_d, FT * (half + 1))
            for t in range(HP):
                p = half * HP + t
                dve.tensor_tensor(acc[:, p, :], f_d[t][:, :], acc[:, p, :], ALU.add).then_inc(s_y2, 1)

        c_s = (bank[0], bank[1], bank[6], bank[7])
        c_t = bank[3:5]
        c_v = (bank[2], bank[5])
        TILES = B * KT
        HEAD1 = PERIOD1 = 4 * KT
        ROUNDS1 = 2
        LT, LV, LY = 7, 9, 9
        STEPS1 = TILES + LY
        PT_ = 2 * KT
        s_cx = sems("s_cx", 2)
        (s_bn3, s_st3, s_rs3, s_xn3, s_cR, s_cRl, s_qR, s_qRl, s_ct, s_vT, s_vTl, s_vz) = (
            sem(f"s_{n}") for n in ("bn3", "st3", "rs3", "xn3", "cR", "cRl", "qR", "qRl", "ct", "vT", "vTl", "vz"))
        (s_s1, s_m1, s_e1, s_r1, s_n1, s_n1p, s_t1, s_p1, s_p1l, s_v1, s_y3) = (
            sem(f"s_{n}") for n in ("s1", "m1", "e1", "r1", "n1", "n1p", "t1", "p1", "p1l", "v1", "y3"))

        def acc_at(p):
            if isinstance(p, int):
                return acc[:, p, :]
            return acc[:, bass.ds(p, 1), :].rearrange("p o d -> p (o d)")

        def prepared(st):
            q = st.j // PT_ + 1
            if isinstance(st.i, int) and q >= PAIRS:
                return None
            return q + st.i * (PERIOD1 // PT_), q % 2

        def current(st):
            q = st.j // PT_
            return q + st.i * (PERIOD1 // PT_), q % 2

        def sp_l1x(sp):
            sp.wait_ge(s_y2, PAIRS)
            for q in range(PAIRS):
                if q >= 2:
                    sp.wait_ge(s_ct, q - 1)
                    sp.wait_ge(s_cRl, q - 1)
                sp.dma_start(cx[:, q % 2, :], ctx_t[q]).then_inc(s_cx[q % 2], 16)

        def arrived(eng, q, par):
            eng.wait_ge(s_cx[par], 8 * (q - par) + 16)

        def dve_stats(dve, q):
            dve.bn_stats(st3[:, :], acc_at(q)).then_inc(s_bn3, 1)

        def dve_aggregate(dve, q, par):
            dve.bn_aggr(mv3[:, par, :], st3[:, :]).then_inc(s_bn3, 1)
            dve.wait_ge(s_bn3, 2 * q + 2)
            dve.tensor_scalar(mv3[:, par, 1:2], mv3[:, par, 1:2], LN_EPS, None, ALU.add).then_inc(s_st3, 1)

        def pool_norm(pool, q, par):
            pool.wait_ge(s_st3, q + 1)
            pool.tensor_tensor(rs3[:, par, 0:1], mv3[:, par, 1:2], half_neg[:, 0:1], ALU.pow).then_inc(s_rs3, 1)
            pool.wait_ge(s_rs3, 2 * q + 1)
            pool.tensor_tensor(rs3[:, par, 1:2], rs3[:, par, 0:1], inv_sqrt_t[:, :], ALU.mult).then_inc(s_rs3, 1)

        def dve_queries(dve, q, par):
            dve.wait_ge(s_rs3, 2 * q + 2)
            wait(dve, s_qRl, q - 1)
            dve.tensor_scalar(xn3[:, par, :], acc_at(q), mv3[:, par, 0:1], rs3[:, par, 1:2],
                              ALU.subtract, ALU.mult).then_inc(s_xn3, 1)

        def act_context(act, q, par):
            arrived(act, q, par)
            wait(act, s_s1, PT_ * (q - 1))
            act.activation(cR[:, par, HI, :], cx[:, par, :], ACT.Copy).then_inc(s_cR, 1)

        def pool_context(pool, q, par):
            pool.wait_ge(s_cR, q + 1)
            pool.tensor_tensor(cR[:, par, LO, :], cx[:, par, :], cR[:, par, HI, :].bitcast(F32),
                               ALU.subtract).then_inc(s_cRl, 1)

        def act_queries(act, q, par):
            act.wait_ge(s_xn3, q + 1)
            wait(act, s_s1, PT_ * (q - 1))
            act.activation(qR[:, par, HI, :], xn3[:, par, :], ACT.Copy).then_inc(s_qR, 1)

        def pool_queries(pool, q, par):
            pool.wait_ge(s_qR, q + 1)
            pool.tensor_tensor(qR[:, par, LO, :], xn3[:, par, :], qR[:, par, HI, :].bitcast(F32),
                               ALU.subtract).then_inc(s_qRl, 1)

        def pe_context(pe, q, par):
            arrived(pe, q, par)
            wait(pe, s_y3, q - 1)
            for t in range(KT):
                mm = pe.transpose(c_v[par][:, t * P:(t + 1) * P], cx[:, par, t * P:(t + 1) * P], ident[:, :])
            mm.then_inc(s_ct, 1)

        def vT_of(par, part):
            return vTz[:, par, :, part, :].rearrange("p t (x c) -> p t x c", x=3)[:, :, 0::2, :]

        def c_view(par):
            return c_v[par][:, :].rearrange("p (t b c) -> p t b c", t=KT, b=2)

        def act_values(act, q, par):
            act.wait_ge(s_ct, q + 1)
            wait(act, s_v1, PT_ * (q - 1))
            act.activation(vT_of(par, HI), c_view(par), ACT.Copy).then_inc(s_vT, 1)

        def dve_values(dve, q, par):
            dve.wait_ge(s_vT, q + 1)
            dve.tensor_tensor(vT_of(par, LO), c_view(par), vT_of(par, HI).bitcast(F32), ALU.subtract).then_inc(s_vTl, 1)

        def pe_l1x(pe):
            pe.wait_ge(s_y2, PAIRS)
            run_steps(pe, pe_step1, HEAD1, PERIOD1, ROUNDS1, STEPS1)

        def pe_step1(st):
            pe = nc.tensor
            if st.has(0, TILES):
                t = st.j
                par, r0, n = t // PT_ % 2, t // KT % 2 * T, t % KT
                if t % PT_ == 0:
                    pe.wait_ge(s_cRl, st.i * 2 + t // PT_ + 1)
                    pe.wait_ge(s_qRl, st.i * 2 + t // PT_ + 1)
                wait(pe, s_e1, st.done(4))
                for k, (l, r) in enumerate(PASSES):
                    mm = pe.matmul(c_s[t % 4][:, :], cR[r0:r0 + T, par, l, n * P:(n + 1) * P],
                                   qR[r0:r0 + T, par, r, :], start=(k == 0), stop=(k == 2))
                mm.then_inc(s_s1, 1)
            if st.has(LT, TILES):
                t = st.j - LT
                b, m = t // KT % 4, t % KT
                if m == 0:
                    pe.wait_ge(s_n1, 2 * (t // KT + 1) + st.i * 8)
                    pe.wait_ge(s_n1p, 2 * (t // KT + 1) + st.i * 8)
                wait(pe, s_p1l, st.done(LT + 2))
                for n in range(KT):
                    mm = pe.transpose(c_t[t % 2][:, n * P:(n + 1) * P], pr[:, b, n, m * P:(m + 1) * P], ident[:, :])
                mm.then_inc(s_t1, 1)
            if st.has(LV, TILES):
                t = st.j - LV
                par, b, m = t // PT_ % 2, t // KT % 2, t % KT
                if t % PT_ == 0:
                    pe.wait_ge(s_vz, 1)
                    pe.wait_ge(s_vTl, st.i * 2 + t // PT_ + 1)
                pe.wait_ge(s_p1l, st.done(LV))
                for k, (l, r) in enumerate(PASSES):
                    mm = pe.matmul(c_v[par][:, :], vTz[:, par, m, l, b * T:b * T + P], pmT[:, t % 4, r, :],
                                   start=(t % PT_ == 0 and k == 0), stop=(t % PT_ == PT_ - 1 and k == 2))
                mm.then_inc(s_v1, 1)
            if st.j % PT_ == 1 and st.has(0, TILES):
                pe_context(pe, *current(st))

        def act_l1x(act):
            act.wait_ge(s_y2, PAIRS)
            act_context(act, 0, 0)
            act_queries(act, 0, 0)
            run_steps(act, act_step1, HEAD1, PERIOD1, ROUNDS1, STEPS1)

        def act_step1(st):
            act = nc.scalar
            if st.has(LT, TILES):
                t = st.j - LT
                act.wait_ge(s_t1, st.done(LT))
                wait(act, s_v1, st.done(LT + 4))
                act.activation(pmT[:, t % 4, HI, :], c_t[t % 2][:, :], ACT.Copy).then_inc(s_p1, 1)
            if st.has(0, TILES):
                t = st.j
                act.wait_ge(s_m1, st.done(0))
                if t % KT == 0:
                    wait(act, s_t1, st.done(0) - 1 - 3 * KT)
                wait(act, s_r1, st.done(4))
                act.activation(pr[:, t // KT % 4, t % KT, :], c_s[t % 4][:, :], ACT.Exp, bias=nm1[:, t % 4:t % 4 + 1],
                               accum_out=sm1[:, t % 4:t % 4 + 1]).then_inc(s_e1, 1)
            if prepared(st):
                if st.j % PT_ == 0:
                    act_context(act, *prepared(st))
                if st.j % PT_ == 2:
                    act_queries(act, *prepared(st))
            if st.j % PT_ == 2 and st.has(0, TILES):
                act_values(act, *current(st))

        def dve_l1x(dve):
            dve.wait_ge(s_y2, PAIRS)
            dve.memset(vTz[:, :, :, :, T:2 * T].bitcast(F32), 0.0).then_inc(s_vz, 1)
            dve_stats(dve, 0)
            dve.wait_ge(s_bn3, 1)
            dve_aggregate(dve, 0, 0)
            dve_queries(dve, 0, 0)
            run_steps(dve, dve_step1, HEAD1, PERIOD1, ROUNDS1, STEPS1)

        def dve_step1(st):
            dve = nc.vector
            norm = prepared(st) if st.j % PT_ == 0 else None
            if norm:
                dve_stats(dve, norm[0])
            if st.has(0, TILES):
                t = st.j
                dve.wait_ge(s_s1, st.done(0))
                wait(dve, s_e1, st.done(4))
                if norm:
                    dve.wait_ge(s_bn3, 2 * norm[0] + 1)
                dve.tensor_reduce(nm1[:, t % 4:t % 4 + 1], c_s[t % 4][:, :], AX, ALU.max, negate=True).then_inc(s_m1, 1)
            if norm:
                dve_aggregate(dve, *norm)
            if st.has(LT, TILES):
                t = st.j - LT
                dve.wait_ge(s_p1, st.done(LT))
                dve.tensor_tensor(pmT[:, t % 4, LO, :], c_t[t % 2][:, :], pmT[:, t % 4, HI, :].bitcast(F32),
                                  ALU.subtract).then_inc(s_p1l, 1)
            if st.has(1, TILES):
                t = st.j - 1
                dve.wait_ge(s_e1, st.done(1))
                if t % 2:
                    wait(dve, s_n1p, pool_normed(st, 1, t) - 2)
                else:
                    wait(dve, s_n1, pool_normed(st, 1, t) - 2)
                dve.reciprocal(rc1[:, t % 4:t % 4 + 1], sm1[:, t % 4:t % 4 + 1]).then_inc(s_r1, 1)
                if t % 2 == 0:
                    dve.wait_ge(s_r1, st.done(1))
                    dve.tensor_scalar(pr[:, t // KT % 4, t % KT, :], pr[:, t // KT % 4, t % KT, :],
                                      rc1[:, t % 4:t % 4 + 1], None, ALU.mult).then_inc(s_n1, 1)
            if st.has(LY, TILES) and (st.j - LY) % PT_ == PT_ - 1:
                q = (st.j - LY) // PT_ + st.i * 2
                dve.wait_ge(s_v1, st.done(LY))
                dve.tensor_tensor(acc_at(q), c_v[(st.j - LY) // PT_ % 2][:, :], acc_at(q), ALU.add).then_inc(s_y3, 1)
            if prepared(st):
                if st.j % PT_ == 1:
                    dve_queries(dve, *prepared(st))
            if st.j % PT_ == 4 and st.has(0, TILES):
                dve_values(dve, *current(st))

        def pool_normed(st, lag, t):
            return t // 2 + 1 + st.i * (PERIOD1 // 2)

        def pool_l1x(pool):
            pool.wait_ge(s_y2, PAIRS)
            pool_norm(pool, 0, 0)
            pool_context(pool, 0, 0)
            pool_queries(pool, 0, 0)
            run_steps(pool, pool_step1, HEAD1, PERIOD1, ROUNDS1, STEPS1)

        def pool_step1(st):
            pool = nc.gpsimd
            if st.has(1, TILES) and (st.j - 1) % 2 == 1:
                t = st.j - 1
                pool.wait_ge(s_r1, st.done(1))
                pool.tensor_tensor(pr[:, t // KT % 4, t % KT, :], pr[:, t // KT % 4, t % KT, :],
                                   rc1[:, t % 4:t % 4 + 1].to_broadcast([P, D]), ALU.mult).then_inc(s_n1p, 1)
            if prepared(st):
                if st.j % PT_ == 0:
                    pool_norm(pool, *prepared(st))
                if st.j % PT_ == 2:
                    pool_context(pool, *prepared(st))
                if st.j % PT_ == 4:
                    pool_queries(pool, *prepared(st))

        s_ld_o, s_ld_q, s_ld_u = sem("s_ld_o"), sem("s_ld_q"), sem("s_ld_u")
        s_ld_d = sems("s_ld_d", KT)
        (s_wot, s_woh, s_wol, s_sm, s_smc, s_dnh, s_dnl, s_uph, s_upl, s_tx4, s_x4h, s_x4l, s_mean) = (
            sem(f"s_{n}") for n in ("wot", "woh", "wol", "sm", "smc", "dnh", "dnl", "uph", "upl", "tx4", "x4h", "x4l", "mean"))
        (s_h4, s_hv4, s_hh4, s_hl4, s_o4, s_y4, s_cv, s_ce) = (
            sem(f"s_{n}") for n in ("h4", "hv4", "hh4", "hl4", "o4", "y4", "cv", "ce"))
        m_x = bank[4:6]
        m_h = bank[6:8]
        m_o = bank[0:4]
        X4 = 2
        W_LATE = HP

        def sp_l1f(sp):
            sp.wait_ge(s_y3, PAIRS)
            sp.dma_start(worg[:, :, :], a["L1_ffn_W_org"].rearrange("(t p) i -> p t i", p=P)).then_inc(s_ld_o, 16)
            sp.dma_start(wq1[:, :], a["L1_ffn_Wq"]).then_inc(s_ld_q, 16)
            sp.dma_start(keys[:, :], a["L1_ffn_lora_keys"]).then_inc(s_ld_q, 16)
            down_t = a["L1_ffn_lora_down"].rearrange("e (t p) r -> t p e r", p=P)
            for t in range(KT):
                sp.dma_start(draw[:, t, :].rearrange("p (e r) -> p e r", e=EXP), down_t[t]).then_inc(s_ld_d[t], 16)
            sp.dma_start(uraw[:, :, :], a["L1_ffn_lora_up"].rearrange("e r o -> (e r) o")
                         .rearrange("(t p) o -> p t o", p=P)).then_inc(s_ld_u, 16)
            for p in range(PAIRS):
                sp.wait_ge(s_y4, p + 1)
                sp.dma_start(out_t[p], acc[:, p, :]).then_inc(s_out, 16)
            sp.wait_ge(s_out, 16 * PAIRS)

        def pool_l1f(pool):
            pool.wait_ge(s_y3, PAIRS)
            for p in range(PAIRS):
                ln_power(pool, X4, p)
            for t in range(KT):
                pool.wait_ge(s_dnh, t + 1)
                pool.tensor_tensor(dn[:, LO, t, :], draw[:, t, :], dn[:, HI, t, :].bitcast(F32), ALU.subtract).then_inc(s_dnl, 1)
            for t in range(KT):
                pool.wait_ge(s_uph, t + 1)
                pool.tensor_tensor(up[:, LO, t, :], uraw[:, t, :], up[:, HI, t, :].bitcast(F32), ALU.subtract).then_inc(s_upl, 1)
            for n in range(2 * KT):
                half, t = divmod(n, KT)
                cols = slice(half * HALF, (half + 1) * HALF)
                pool.wait_ge(s_hh4, n + 1)
                pool.tensor_tensor(hs[:, LO, t, cols], hval4[:, n % 2, :], hs[:, HI, t, cols].bitcast(F32),
                                   ALU.subtract).then_inc(s_hl4, 1)

        def pe_l1f(pe):
            pe.wait_ge(s_y3, PAIRS)

            def x_tile(p):
                pe.wait_ge(s_xn, 2 * PAIRS + p + 1)
                if p >= 2:
                    pe.wait_ge(s_x4l, p - 1)
                    pe.wait_ge(s_mean, p - 1)
                for kt in range(KT):
                    mm = pe.transpose(m_x[p % 2][:, kt * P:(kt + 1) * P], xn4[:, p % 2, kt * P:(kt + 1) * P], ident[:, :])
                mm.then_inc(s_tx4, 1)

            def base(p):
                pe.wait_ge(s_x4l, p + 1)
                if p >= HP:
                    pe.wait_ge(s_y4, p - HP + 1)
                for kt in range(KT):
                    for k, (l, r) in enumerate(PASSES):
                        pe.matmul(m_o[p % HP][:, :], x4T[:, l, kt, p * P:(p + 1) * P], woT[:, r, kt, :],
                                  start=(kt == 0 and k == 0), stop=False)

            def delta(p):
                pe.wait_ge(s_hl4, KT * (p // HP + 1))
                pe.wait_ge(s_upl, KT)
                for t in range(KT):
                    for k, (l, r) in enumerate(PASSES):
                        mm = pe.matmul(m_o[p % HP][:, :], hs[:, l, t, p * P:(p + 1) * P], up[:, r, t, :],
                                       start=False, stop=(t == KT - 1 and k == 2))
                mm.then_inc(s_o4, 1)

            def low_rank(n):
                half, j = divmod(n, KT)
                if n >= 2:
                    pe.wait_ge(s_hv4, n - 1)
                pe.wait_ge(s_dnl, KT)
                for kt in range(KT):
                    for k, (l, r) in enumerate(PASSES):
                        mm = pe.matmul(m_h[n % 2][:, :], dn[:, l, kt, j * P:(j + 1) * P],
                                       x4T[:, r, kt, half * HALF:(half + 1) * HALF],
                                       start=(kt == 0 and k == 0), stop=(kt == KT - 1 and k == 2))
                mm.then_inc(s_h4, 1)

            x_tile(0)
            x_tile(1)
            pe.wait_ge(s_ld_q, 32)
            for kt in range(KT):
                pe.transpose(m_h[0][:, kt * P:(kt + 1) * P], wq1[:, kt * P:(kt + 1) * P], ident[:, :])
            pe.transpose(m_h[1][:, 0:EXP], keys[:, :], ident[0:EXP, 0:EXP]).then_inc(s_sm, 1)
            pe.wait_ge(s_ld_o, 16)
            for it in range(KT):
                for ot in range(KT):
                    mm = pe.transpose(m_o[it][:, ot * P:(ot + 1) * P], worg[:, ot, it * P:(it + 1) * P], ident[:, :])
                mm.then_inc(s_wot, 1)
            x_tile(2)
            x_tile(3)
            pe.wait_ge(s_wol, KT)
            for p in range(HP):
                base(p)
                x_tile(HP + p)
            pe.wait_ge(s_mean, PAIRS)
            pe.wait_ge(s_smc, 2)
            for kt in range(KT):
                mm = pe.matmul(m_h[0][:, 0:B], wq1T[:, kt, :], meanT[:, kt, :], start=(kt == 0), stop=(kt == KT - 1))
            mm.then_inc(s_sm, 1)
            pe.wait_ge(s_smc, 3)
            pe.matmul(m_h[1][0:B, 0:EXP], q1T[:, :], keysT[:, :], start=True, stop=True).then_inc(s_sm, 1)
            pe.wait_ge(s_cv, 5)
            for t in range(KT):
                mm = pe.transpose(m_h[0][:, t * B:(t + 1) * B],
                                  cexp[:, :, :].rearrange("b e r -> b (e r)")[:, t * P:(t + 1) * P], ident[0:B, 0:B])
            mm.then_inc(s_sm, 1)
            pe.wait_ge(s_smc, 4)
            for n in range(KT):
                low_rank(n)
            for n in range(KT):
                low_rank(KT + n)
                delta(n)
            for p in range(HP, PAIRS):
                base(p)
                delta(p)

        def act_l1f(act):
            act.wait_ge(s_y3, PAIRS)

            def x_hi(p):
                act.wait_ge(s_tx4, p + 1)
                act.activation(x4T[:, HI, :, p * P:(p + 1) * P], tiles(m_x[p % 2]), ACT.Copy).then_inc(s_x4h, 1)

            x_hi(0)
            x_hi(1)
            act.wait_ge(s_sm, 1)
            act.activation(wq1T[:, :, :].rearrange("p t k -> p (t k)"), m_h[0][:, :], ACT.Copy).then_inc(s_smc, 1)
            act.activation(keysT[:, :], m_h[1][:, 0:EXP], ACT.Copy).then_inc(s_smc, 1)
            for t in range(KT):
                act.wait_ge(s_wot, t + 1)
                act.activation(woT[:, HI, t, :], m_o[t][:, :], ACT.Copy).then_inc(s_woh, 1)
            for p in range(2, PAIRS):
                x_hi(p)
                if p < 2 + KT:
                    act.wait_ge(s_ld_d[p - 2], 16)
                    act.activation(dn[:, HI, p - 2, :], draw[:, p - 2, :], ACT.Copy).then_inc(s_dnh, 1)
            act.wait_ge(s_ld_u, 16)
            for t in range(KT):
                act.activation(up[:, HI, t, :], uraw[:, t, :], ACT.Copy).then_inc(s_uph, 1)
            act.wait_ge(s_sm, 2)
            act.activation(q1T[:, :], m_h[0][:, 0:B], ACT.Copy, scale=1.0 / T).then_inc(s_smc, 1)
            act.wait_ge(s_cv, 2)
            act.activation(cf[:, :], lg[:, :], ACT.Exp, bias=cstat[:, 0:1], accum_out=cstat[:, 1:2]).then_inc(s_ce, 1)
            act.wait_ge(s_sm, 4)
            act.activation(cT[:, :, :].rearrange("p t b -> p (t b)"), m_h[0][:, 0:KT * B], ACT.Copy).then_inc(s_smc, 1)
            for n in range(2 * KT):
                half, t = divmod(n, KT)
                act.wait_ge(s_hv4, n + 1)
                act.activation(hs[:, HI, t, half * HALF:(half + 1) * HALF], hval4[:, n % 2, :], ACT.Copy).then_inc(s_hh4, 1)

        def dve_l1f(dve):
            dve.wait_ge(s_y3, PAIRS)

            def x_lo(p):
                dve.wait_ge(s_x4h, p + 1)
                dve.tensor_tensor(x4T[:, LO, :, p * P:(p + 1) * P], tiles(m_x[p % 2]),
                                  x4T[:, HI, :, p * P:(p + 1) * P].bitcast(F32), ALU.subtract).then_inc(s_x4l, 1)
                dve.tensor_reduce(meanT[:, :, 2 * p:2 * p + 2], m_x[p % 2][:, :].rearrange("p (k b t) -> p k b t", k=KT, b=2),
                                  AX, ALU.add).then_inc(s_mean, 1)

            for p in range(PAIRS + 1):
                if p < PAIRS:
                    ln_stats(dve, X4, p)
                if p >= 1:
                    if p >= 3:
                        dve.wait_ge(s_tx4, p - 2)
                    ln_apply(dve, X4, p - 1, xn4[:, (p - 1) % 2, :])
                if p == 3:
                    for t in range(KT):
                        dve.wait_ge(s_woh, t + 1)
                        dve.tensor_tensor(woT[:, LO, t, :], m_o[t][:, :], woT[:, HI, t, :].bitcast(F32),
                                          ALU.subtract).then_inc(s_wol, 1)
                if p >= 2:
                    x_lo(p - 2)
            x_lo(PAIRS - 1)
            dve.wait_ge(s_sm, 3)
            dve.tensor_scalar(lg[:, :], m_h[1][0:B, 0:EXP], float(KD) ** -0.5, None, ALU.mult).then_inc(s_cv, 1)
            dve.wait_ge(s_cv, 1)
            dve.tensor_reduce(cstat[:, 0:1], lg[:, :], AX, ALU.max, negate=True).then_inc(s_cv, 1)
            dve.wait_ge(s_ce, 1)
            dve.reciprocal(cstat[:, 2:3], cstat[:, 1:2]).then_inc(s_cv, 1)
            dve.wait_ge(s_cv, 3)
            dve.tensor_scalar(lg[:, :], cf[:, :], cstat[:, 2:3], None, ALU.mult).then_inc(s_cv, 1)
            dve.wait_ge(s_cv, 4)
            dve.tensor_copy(cexp[:, :, :], lg[:, :].unsqueeze(2).to_broadcast([B, EXP, RANK])).then_inc(s_cv, 1)
            dve.wait_ge(s_smc, 4)

            def add_out(p):
                dve.wait_ge(s_o4, p + 1)
                dve.tensor_tensor(acc[:, p, :], m_o[p % HP][:, :], acc[:, p, :], ALU.add).then_inc(s_y4, 1)

            for n in range(2 * KT):
                half, t = divmod(n, KT)
                dve.wait_ge(s_h4, n + 1)
                if n >= 2:
                    dve.wait_ge(s_hl4, n - 1)
                dve.tensor_tensor(hval4[:, n % 2, :].rearrange("p (b t) -> p b t", t=T),
                                  m_h[n % 2][:, :].rearrange("p (b t) -> p b t", t=T),
                                  cT[:, t, half * B // 2:(half + 1) * B // 2].unsqueeze(2).to_broadcast([P, B // 2, T]),
                                  ALU.mult).then_inc(s_hv4, 1)
                if n > KT:
                    add_out(n - KT - 1)
            for p in range(HP - 1, PAIRS):
                add_out(p)


        s_out = sem("s_out")

        @block.sync
        def _(sp):
            sp_first(sp)
            sp_ffn(sp)
            sp_l1x(sp)
            sp_l1f(sp)

        @block.gpsimd
        def _(pool):
            pool.memset(ident[:, :], 0.0).then_inc(s_const, 1)
            pool.memset(half_neg[:, :], -0.5).then_inc(s_const, 1)
            pool.memset(inv_sqrt_t[:, :], float(T) ** -0.5).then_inc(s_const, 1)
            pool.wait_ge(s_const, 3)
            pool.affine_select(out=ident[:, :], in_=ident[:, :], compare_op=ALU.not_equal, fill=1.0, base=0,
                               pattern=[[-1, P]], channel_multiplier=1).then_inc(s_const, 1)
            pool_first(pool)
            pool_ffn(pool)
            pool_l1x(pool)
            pool_l1f(pool)

        @block.tensor
        def _(pe):
            pe_first(pe)
            pe_ffn(pe)
            pe_l1x(pe)
            pe_l1f(pe)

        @block.scalar
        def _(act):
            act_first(act)
            act_ffn(act)
            act_l1x(act)
            act_l1f(act)

        @block.vector
        def _(dve):
            dve_first(dve)
            dve_ffn(dve)
            dve_l1x(dve)
            dve_l1f(dve)


def kernel(**inputs):
    import numpy as _np
    import concourse.bacc as _bacc
    from concourse.bass_utils import run_bass_kernel_spmd as _run

    nc = _bacc.Bacc("TRN2", target_bir_lowering=False, num_devices=1)
    arrays, aps = {}, {}
    for name, value in inputs.items():
        v = _np.ascontiguousarray(value)
        arrays[f"in_{name}_dram"] = v
        aps[name] = nc.dram_tensor(f"in_{name}_dram", v.shape, mybir.dt.from_np(v.dtype), kind="ExternalInput").ap()
    out = nc.dram_tensor("out_0_dram", inputs["x"].shape, F32, kind="ExternalOutput").ap()
    block_kernel(nc, aps, out)
    r = _run(nc, [arrays], core_ids=[0])
    return r.results[0]["out_0_dram"]
```

```python
from contextlib import ExitStack

import concourse.bass as bass
from concourse import mybir

F32 = mybir.dt.float32
F32R = mybir.dt.float32r
BF16 = mybir.dt.bfloat16
I32 = mybir.dt.int32
ALU = mybir.AluOpType
ACT = mybir.ActivationFunctionType
AX = mybir.AxisListType.X

P = 128
HI, LO = 0, 1
PASSES = ((HI, HI), (HI, LO), (LO, HI))


class Step:

    def __init__(self, i, j, period):
        self.i, self.j, self.period = i, j, period

    def done(self, lag=0, per=1):
        return per * self.period * self.i + per * (self.j - lag + 1)

    def has(self, lag, units):
        return not isinstance(self.i, int) or 0 <= self.j - lag < units


def wait(eng, sem, value):
    if not isinstance(value, int) or value > 0:
        eng.wait_ge(sem, value)


def run_steps(eng, step, head, period, rounds, total, after=None):
    for j in range(head):
        step(Step(0, j, period))
        if after is not None:
            after(j)
    with eng.Fori(0, rounds) as i:
        for j in range(head, head + period):
            step(Step(i, j, period))
    for j in range(head + period * rounds, total):
        step(Step(0, j, period))
        if after is not None:
            after(j)


def block_kernel(nc, a, out, stop=None):
    x, ctx_in = a["x"], a["ctx_4096"]
    Wq, Wk, Wv, Wo = (a[f"L0_xattn_{n}"] for n in ("Wq", "Wk", "Wv", "Wo"))
    B, T, D = x.shape
    HD = a["L0_xattn_q_norm_w"].shape[0]
    KVH = Wk.shape[1] // HD
    G = Wq.shape[1] // HD // KVH
    KT = D // P
    PAIRS = B * T // P
    UNITS = KVH * PAIRS
    QW = G * HD
    QKV = QW + 2 * HD
    RMS_EPS, LN_EPS = 1e-6, 1e-5
    F = a["L0_ffn_gate_qweight"].shape[1]
    GG = a["L0_ffn_gate_scales"].shape[0]
    GD = a["L0_ffn_down_scales"].shape[0]
    FT = -(-F // P)
    HALF = B * T // 2
    EXP = a["L1_ffn_lora_down"].shape[0]
    RANK = a["L1_ffn_lora_down"].shape[2]
    KD = a["L1_ffn_Wq"].shape[0]
    assert (T, D, HD, G, PAIRS, KVH, QW, EXP * RANK) == (64, 512, 128, 4, 8, 8, 512, 512)

    x_t = x.rearrange("(q b) t d -> q (b t) d", b=2)
    ctx_t = ctx_in.rearrange("(q b) t d -> q (b t) d", b=2)
    out_t = out.rearrange("(q b) t d -> q (b t) d", b=2)

    root = ExitStack()
    with root:
        def sb(name, shape, dt, scope=root):
            return scope.enter_context(nc.sbuf_tensor(name, shape, dt))

        def sem(name):
            return root.enter_context(nc.semaphore(name))

        def sems(name, n):
            return [sem(f"{name}{k}") for k in range(n)]

        bank = [root.enter_context(nc.psum_tensor(f"bank{k}", [P, 512], F32)) for k in range(8)]

        acc = sb("acc", [P, PAIRS, D], F32)
        ident = sb("ident", [P, P], F32)
        half_neg = sb("half_neg", [P, 8], F32)
        inv_sqrt_t = sb("inv_sqrt_t", [P, 1], F32)
        stat = sb("stat", [P, 16, 6], F32)
        mv = sb("mv", [P, 4, PAIRS, 2], F32)
        rstd = sb("rstd", [P, 4, PAIRS], F32)
        wqk = sb("wqk", [P, 4], F32)

        s0 = ExitStack()
        kvT = sb("kvT", [P, 2, KT, PAIRS, 4, T], F32R, s0)
        wqkv_raw = sb("wqkv_raw", [P, 2, QKV], F32, s0)
        wo_raw = sb("wo_raw", [P, 2, D], F32, s0)
        wqkv = sb("wqkv", [P, 2, 2, KT, QKV], F32R, s0)
        s0a = ExitStack()
        sb("gap0", [P, 2 * G * D], F32, s0a)
        ctx_raw = sb("ctx_raw", [P, PAIRS, D], F32, s0a)
        s0a.close()
        wo = sb("wo", [P, 2, 2, G, D], F32R, s0)
        s0b = ExitStack()
        qsq = sb("qsq", [P, G, HD], F32, s0b)
        ksq = sb("ksq", [P, 2, HD], F32, s0b)
        qn = sb("qn", [P, G, HD], F32, s0b)
        kn = sb("kn", [P, 2, HD], F32, s0b)
        qT = sb("qT", [P, 2, G, T], F32, s0b)
        kT = sb("kT", [P, 2, P], F32, s0b)
        vv = sb("vv", [P, 2, 2, 2, HD], F32R, s0b)
        prob = sb("prob", [P, 2 * 2, P], F32, s0b)
        pT = sb("pT", [P, 2, 2, G * T], F32R, s0b)
        aoT = sb("aoT", [P, 2, G, 2, T], F32R, s0b)
        ssq = sb("ssq", [P, 6], F32, s0b)
        msq = sb("msq", [P, 6], F32, s0b)
        rms = sb("rms", [P, 6], F32, s0b)
        nmax = sb("nmax", [P, 4], F32, s0b)
        psum_row = sb("psum_row", [P, 4], F32, s0b)
        rsum = sb("rsum", [P, 4], F32, s0b)
        s0c = ExitStack()
        xn0 = sb("xn0", [P, 2, D], F32, s0c)
        s0c.close()
        s_raw = sb("s_raw", [P, 2 * F + D], F32, s0b)
        s0b.close()
        s0.close()

        GATE, UP, DOWN = 0, F, 2 * F
        ZS = 2 * F + D
        s1 = ExitStack()
        wd = sb("wd", [P, FT, 2, D], F32R, s1)
        x2T = sb("x2T", [P, 2, KT, HALF], F32R, s1)
        hT = sb("hT", [P, 2, HALF], F32R, s1)
        zs = sb("zs", [P, 2, ZS], BF16, s1)
        oh_gu = sb("oh_gu", [P, 2, D], BF16, s1)
        oh_d = sb("oh_d", [P, F], BF16, s1)
        pid = sb("pid", [P, 1], I32, s1)
        shift = sb("shift", [P, 1], I32, s1)
        grp_i = sb("grp_i", [P, 1], I32, s1)
        grp = sb("grp", [P, 1], F32, s1)
        s1a = ExitStack()
        z_raw = sb("z_raw", [32, ZS // 8], I32, s1a)
        z_int = sb("z_int", [32, ZS // 8, 8], I32, s1a)
        s1a.close()
        s1c = ExitStack()
        below_wo = 2 * KT * PAIRS * 4 * T + 2 * QKV + 2 * D + 2 * 2 * KT * QKV
        so_far = FT * 2 * D + 2 * KT * HALF + 2 * HALF + ZS + D + F // 2 + 4
        sb("gap", [P, below_wo - so_far], F32, s1c)
        idx_raw = sb("idx_raw", [P, 2 * D + F], I32, s1c)
        idx_n = sb("idx_n", [P, F], F32, s1c)
        s1c.close()
        s1b = ExitStack()
        packed = sb("packed", [P, 3, 512], I32, s1b)
        nib = sb("nib", [P, 256], I32, s1b)
        wint = sb("wint", [P, 256], F32, s1b)
        wtmp = sb("wtmp", [P, 2, 256], F32, s1b)
        xn2 = sb("xn2", [P, 2, D], F32, s1b)
        wgu = sb("wgu", [P, FT, 2, 2, KT, P], F32R, s1b)
        gact = sb("gact", [P, HALF], F32, s1b)
        hval = sb("hval", [P, HALF], F32, s1b)
        s1b.close()
        s1.close()

        s2 = ExitStack()
        sb("gap2", [P, FT * 2 * D + 2 * KT * HALF + 2 * HALF], F32, s2)
        cx = sb("cx", [P, 2, D], F32, s2)
        cR = sb("cR", [P, 2, 2, D], F32R, s2)
        xn3 = sb("xn3", [P, 2, D], F32, s2)
        qR = sb("qR", [P, 2, 2, D], F32R, s2)
        st3 = sb("st3", [P, 6], F32, s2)
        mv3 = sb("mv3", [P, 2, 2], F32, s2)
        rs3 = sb("rs3", [P, 2, 2], F32, s2)
        nm1 = sb("nm1", [P, 4], F32, s2)
        sm1 = sb("sm1", [P, 4], F32, s2)
        rc1 = sb("rc1", [P, 4], F32, s2)
        vTz = sb("vTz", [P, 2, KT, 2, 3 * T], F32R, s2)
        pr = sb("pr", [P, 4, KT, D], F32, s2)
        pmT = sb("pmT", [P, 4, 2, D], F32R, s2)
        s2.close()

        s3 = ExitStack()
        dn = sb("dn", [P, 2, KT, EXP * RANK], F32R, s3)
        up = sb("up", [P, 2, KT, D], F32R, s3)
        worg = sb("worg", [P, KT, D], F32, s3)
        draw = sb("draw", [P, KT, EXP * RANK], F32, s3)
        uraw = sb("uraw", [P, KT, D], F32, s3)
        wq1 = sb("wq1", [P, D], F32, s3)
        wq1T = sb("wq1T", [P, KT, KD], F32, s3)
        xn4 = sb("xn4", [P, 2, D], F32, s3)
        x4b = sb("x4b", [P, 2, KT, HALF], F32R, s3)
        hs = sb("hs", [P, 2, KT, B * T], F32R, s3)
        channel = 2 * D + 4 * D + 2 * D + 4 * D + 64 + 2 * KT * 2 * 3 * T + 4 * KT * D + 4 * 2 * D
        sb("gap3", [P, channel - 2 * KT * HALF - 2 * KT * B * T], F32, s3)
        x4a = sb("x4a", [P, 2, KT, HALF], F32R, s3)
        woT = sb("woT", [P, 2, KT, D], F32R, s3)
        hval4 = sb("hval4", [P, 2, 512], F32, s3)
        keys = sb("keys", [EXP, KD], F32, s3)
        keysT = sb("keysT", [P, EXP], F32, s3)
        meanT = sb("meanT", [P, KT, B], F32, s3)
        q1T = sb("q1T", [P, B], F32, s3)
        lg = sb("lg", [B, EXP], F32, s3)
        cf = sb("cf", [B, EXP], F32, s3)
        cstat = sb("cstat", [B, 4], F32, s3)
        cexp = sb("cexp", [B, EXP, RANK], F32, s3)
        cT = sb("cT", [P, KT, B], F32, s3)
        s3.close()

        s_const = sem("s_const")
        s_stat, s_rstd, s_xn = sem("s_stat"), sem("s_rstd"), sem("s_xn")
        sx, sc = sems("s_x", PAIRS), sems("s_ctx", PAIRS)

        block = root.enter_context(nc.Block())

        s_nw = sem("s_nw")
        s_wqk = sem("s_wqk")
        s_wqkv_in, s_wo_in = sems("s_wqkv_in", 2), sems("s_wo_in", 2)
        s_wqkv_hi, s_wqkv = sem("s_wqkv_hi"), sem("s_wqkv")
        s_wo_hi, s_wo = sem("s_wo_hi"), sem("s_wo")
        s_tc, s_tx = sem("s_tc"), sem("s_tx")
        s_chi, s_clo, s_xhi, s_xlo = sem("s_chi"), sem("s_clo"), sem("s_xhi"), sem("s_xlo")
        s_q, s_kv, s_t, s_s, s_pt, s_pv, s_o = (sem(f"s_{n}") for n in ("q", "kv", "t", "s", "pt", "pv", "o"))
        s_qsq, s_ksq, s_qT, s_kT, s_vhi, s_exp, s_phi, s_aohi = (
            sem(f"s_{n}") for n in ("qsq", "ksq", "qT", "kT", "vhi", "exp", "phi", "aohi"))
        s_qms, s_kms, s_qn, s_kn, s_vlo, s_max, s_plo, s_pn, s_aolo, s_acc = (
            sem(f"s_{n}") for n in ("qms", "kms", "qn", "kn", "vlo", "max", "plo", "pn", "aolo", "acc"))
        s_red = sem("s_red")
        s_rq, s_rk = sem("s_rq"), sem("s_rk")
        s_rec = sem("s_rec")
        b_q, b_kv, b_tq, b_tk, b_s, b_pt, b_pv, b_o = bank

        HEAD, PERIOD = 8, 2 * PAIRS
        ROUNDS = (UNITS - HEAD) // PERIOD
        STEPS0 = UNITS + 4

        def unit(st, lag):
            u = st.j - lag
            return u % PAIRS, u // PAIRS % 2, u % 2

        def sp_first(sp):
            sp.dma_start(wqk[:, 0:1], a["L0_xattn_q_norm_w"].rearrange("(d o) -> d o", o=1)).then_inc(s_nw, 16)
            sp.dma_start(wqk[:, 1:2], a["L0_xattn_k_norm_w"].rearrange("(d o) -> d o", o=1)).then_inc(s_nw, 16)

            def qkv_piece(g, kt, freed):
                wait(sp, s_wqkv, freed)
                rows, slot = slice(kt * P, (kt + 1) * P), kt % 2
                sp.dma_start(wqkv_raw[:, slot, 0:QW], Wq[rows, bass.ds(g * QW, QW)]).then_inc(s_wqkv_in[slot], 16)
                sp.dma_start(wqkv_raw[:, slot, QW:QW + HD], Wk[rows, bass.ds(g * HD, HD)]).then_inc(s_wqkv_in[slot], 16)
                sp.dma_start(wqkv_raw[:, slot, QW + HD:QKV], Wv[rows, bass.ds(g * HD, HD)]).then_inc(s_wqkv_in[slot], 16)

            def wo_piece(g, h, freed):
                wait(sp, s_wo, freed)
                sp.dma_start(wo_raw[:, h % 2, :], Wo[bass.ds(g * QW + h * HD, HD), :]).then_inc(s_wo_in[h % 2], 16)

            def group(g):
                for n in range(4):
                    qkv_piece(g, n, 4 * g + n - 1)
                    if n == 0:
                        wo_piece(g - 1, 3, 4 * g - 2)
                    else:
                        wo_piece(g, n - 1, 4 * g + n - 2)

            for p in range(PAIRS):
                sp.dma_start(acc[:, p, :], x_t[p]).then_inc(sx[p], 16)
                sp.dma_start(ctx_raw[:, p, :], ctx_t[p]).then_inc(sc[p], 16)
                if p == 3:
                    qkv_piece(0, 0, 0)
                if p == 5:
                    qkv_piece(0, 1, 0)
            wo_piece(0, 0, 0)
            wo_piece(0, 1, 0)
            qkv_piece(0, 2, 1)
            qkv_piece(0, 3, 2)
            wo_piece(0, 2, 1)
            with sp.Fori(1, KVH) as g:
                group(g)
            sp_scales(sp)
            wo_piece(KVH - 1, 3, 4 * KVH - 2)

        CTX_BANK = (0, 1, 0, 1, 5, 6, 5, 6)
        X_BANK = (2, 3, 2, 3, 7, 4, 7, 5)

        def pe_tokens(pe, p):
            if p < PAIRS:
                b = bank[CTX_BANK[p]]
                pe.wait_ge(sc[p], 16)
                if p in (2, 3, 6, 7):
                    pe.wait_ge(s_clo, p - 1)
                for kt in range(KT):
                    mm = pe.transpose(b[:, kt * P:(kt + 1) * P], ctx_raw[:, p, kt * P:(kt + 1) * P], ident[:, :])
                mm.then_inc(s_tc, 1)
            if p >= 1:
                q = p - 1
                b = bank[X_BANK[q]]
                pe.wait_ge(s_xn, q + 1)
                if q in (2, 3, 6):
                    pe.wait_ge(s_xlo, q - 1)
                if q == 7:
                    pe.wait_ge(s_clo, q)
                for kt in range(KT):
                    mm = pe.transpose(b[:, kt * P:(kt + 1) * P], xn0[:, q % 2, kt * P:(kt + 1) * P], ident[:, :])
                mm.then_inc(s_tx, 1)

        def pe_first(pe):
            pe.wait_ge(s_const, 4)
            first = Step(0, 0, PERIOD)
            for p in range(PAIRS + 1):
                pe_tokens(pe, p)
                if p == 7:
                    pe.wait_ge(s_clo, 3)
                    pe.wait_ge(s_xlo, 1)
                    query_projection(pe, first)
                if p == 8:
                    pe.wait_ge(s_clo, 4)
                    key_projection(pe, first)
            pe.wait_ge(s_clo, PAIRS)
            pe.wait_ge(s_xlo, PAIRS)
            run_steps(pe, pe_step0, HEAD, PERIOD, ROUNDS, STEPS0, pe_ahead)

        def group_count(st, lag):
            return 4 * ((st.j - lag) // PAIRS + 1) + st.i * 4 * (PERIOD // PAIRS)

        def is_first(st):
            return isinstance(st.i, int) and st.j == 0

        def query_projection(pe, st):
            p, par, _ = unit(st, 0)
            if p == 0:
                pe.wait_ge(s_wqkv, group_count(st, 0))
            wait(pe, s_qn, st.done(1))
            for kt in range(KT):
                for n, (l, r) in enumerate(PASSES):
                    mm = pe.matmul(b_q[:, :], kvT[:, l, kt, p, 1:3, :], wqkv[:, par, r, kt, 0:QW],
                                   start=(kt == 0 and n == 0), stop=(kt == KT - 1 and n == 2))
            mm.then_inc(s_q, 1)

        def key_projection(pe, st):
            p, par, _ = unit(st, 0)
            wait(pe, s_vlo, st.done(1))
            wait(pe, s_kn, st.done(1))
            for b in range(2):
                for kt in range(KT):
                    for n, (l, r) in enumerate(PASSES):
                        mm = pe.matmul(b_kv[:, b * 256:(b + 1) * 256], kvT[:, l, kt, p, 2 * b:2 * b + 2, :],
                                       wqkv[:, par, r, kt, QW:QKV],
                                       start=(kt == 0 and n == 0), stop=(kt == KT - 1 and n == 2))
            mm.then_inc(s_kv, 1)

        def pe_step0(st):
            pe = nc.tensor
            if st.has(0, UNITS) and not is_first(st):
                query_projection(pe, st)
            if st.has(1, UNITS):
                pe.wait_ge(s_qn, st.done(1))
                wait(pe, s_qT, st.done(2))
                wait(pe, s_kT, st.done(2))
                for h in range(G):
                    pe.transpose(b_tq[:, h * P:(h + 1) * P], qn[:, h, :], ident[:, :])
                pe.wait_ge(s_kn, st.done(1))
                for b in range(2):
                    mm = pe.transpose(b_tk[:, b * P:(b + 1) * P], kn[:, b, :], ident[:, :])
                mm.then_inc(s_t, 1)
            if st.has(0, UNITS) and not is_first(st):
                key_projection(pe, st)
            if st.has(1, UNITS):
                pe.wait_ge(s_qT, st.done(1))
                pe.wait_ge(s_kT, st.done(1))
                wait(pe, s_exp, st.done(2, 4))
                for b in range(2):
                    for hp in range(2):
                        n = b * 2 + hp
                        mm = pe.matmul(b_s[:, n * P:(n + 1) * P], qT[:, b, 2 * hp:2 * hp + 2, :], kT[:, b, :],
                                       start=True, stop=True)
                mm.then_inc(s_s, 1)
            if st.has(2, UNITS):
                pe.wait_ge(s_pn, st.done(2))
                wait(pe, s_plo, st.done(3))
                for n in range(4):
                    mm = pe.transpose(b_pt[:, n * P:(n + 1) * P], prob[:, n, :], ident[:, :])
                mm.then_inc(s_pt, 1)
            if st.has(3, UNITS):
                p, par, _ = unit(st, 3)
                if p == 0:
                    pe.wait_ge(s_wo, group_count(st, 3))
                pe.wait_ge(s_aolo, st.done(3))
                wait(pe, s_acc, st.done(4))
                for h in range(G):
                    for n, (l, r) in enumerate(PASSES):
                        mm = pe.matmul(b_o[:, :], aoT[:, l, h, :, :], wo[:, par, r, h, :],
                                       start=(h == 0 and n == 0), stop=(h == G - 1 and n == 2))
                mm.then_inc(s_o, 1)
            if st.has(2, UNITS):
                _, _, par = unit(st, 2)
                pe.wait_ge(s_plo, st.done(2))
                pe.wait_ge(s_vlo, st.done(2))
                wait(pe, s_aolo, st.done(3))
                for b in range(2):
                    for n, (l, r) in enumerate(PASSES):
                        mm = pe.matmul(b_pv[:, b * 256:(b + 1) * 256], vv[:, par, l, b, :], pT[:, r, b, :],
                                       start=(n == 0), stop=(n == 2))
                mm.then_inc(s_pv, 1)

        def weight_piece(st):
            j = st.j % PAIRS
            return {0: ("qkv", 0, 1), 1: ("wo", 3, 0), 2: ("qkv", 1, 1), 3: ("wo", 0, 1),
                    4: ("qkv", 2, 1), 5: ("wo", 1, 1), 6: ("qkv", 3, 1), 7: ("wo", 2, 1)}[j]

        def piece_of(st):
            kind, n, ahead = weight_piece(st)
            gj = st.j // PAIRS + ahead
            exists = not isinstance(st.i, int) or gj < KVH
            g = gj + st.i * (PERIOD // PAIRS)
            return kind, n, g, gj, exists

        def hi_piece(act, st):
            kind, n, g, gj, exists = piece_of(st)
            if not exists:
                return
            par = gj % 2
            if kind == "qkv":
                act.wait_ge(s_wqkv_in[n % 2], 48 * (2 * g + n // 2 + 1))
                wait(act, s_kv, (8 * (g - 1)) if gj >= 2 else 0)
                act.activation(wqkv[:, par, HI, n, :], wqkv_raw[:, n % 2, :], ACT.Copy).then_inc(s_wqkv_hi, 1)
            else:
                act.wait_ge(s_wo_in[n % 2], 16 * (2 * g + n // 2 + 1))
                wait(act, s_o, (8 * (g - 1)) if gj >= 2 else 0)
                act.activation(wo[:, par, HI, n, :], wo_raw[:, n % 2, :], ACT.Copy).then_inc(s_wo_hi, 1)

        def lo_piece(pool, st):
            kind, n, g, gj, exists = piece_of(st)
            if not exists:
                return
            par = gj % 2
            if kind == "qkv":
                pool.wait_ge(s_wqkv_hi, 4 * g + n + 1)
                pool.tensor_tensor(wqkv[:, par, LO, n, :], wqkv_raw[:, n % 2, :],
                                   wqkv[:, par, HI, n, :].bitcast(F32), ALU.subtract).then_inc(s_wqkv, 1)
            else:
                pool.wait_ge(s_wo_hi, 4 * g + n + 1)
                pool.tensor_tensor(wo[:, par, LO, n, :], wo_raw[:, n % 2, :],
                                   wo[:, par, HI, n, :].bitcast(F32), ALU.subtract).then_inc(s_wo, 1)

        def kv_context(part, p):
            return kvT[:, part, :, p, 0::3, :]

        def kv_latents(part, p):
            return kvT[:, part, :, p, 1:3, :]

        def by_batch(b):
            return b[:, :].rearrange("p (k b t) -> p k b t", k=KT, b=2)

        def act_tokens(act, p):
            if p < PAIRS:
                act.wait_ge(s_tc, p + 1)
                act.activation(kv_context(HI, p), by_batch(bank[CTX_BANK[p]]), ACT.Copy).then_inc(s_chi, 1)
            if p >= 1:
                act.wait_ge(s_tx, p)
                act.activation(kv_latents(HI, p - 1), by_batch(bank[X_BANK[p - 1]]), ACT.Copy).then_inc(s_xhi, 1)

        def first_wo_hi(act, h):
            act.wait_ge(s_wo_in[h % 2], 16 * (h // 2 + 1))
            act.activation(wo[:, 0, HI, h, :], wo_raw[:, h % 2, :], ACT.Copy).then_inc(s_wo_hi, 1)

        def act_first(act):
            for p in range(PAIRS + 1):
                act_tokens(act, p)
                kt = p - 2
                if kt >= KT:
                    first_wo_hi(act, kt - KT)
                elif kt >= 0:
                    act.wait_ge(s_wqkv_in[kt % 2], 48 * (kt // 2 + 1))
                    act.activation(wqkv[:, 0, HI, kt, :], wqkv_raw[:, kt % 2, :], ACT.Copy).then_inc(s_wqkv_hi, 1)
            act.wait_ge(s_wqk, 2)
            run_steps(act, act_step0, HEAD, PERIOD, ROUNDS, STEPS0, act_ahead)

        def act_step0(st):
            act = nc.scalar
            if st.has(3, UNITS):
                act.wait_ge(s_pv, st.done(3))
                wait(act, s_o, st.done(4))
                act.activation(aoT[:, HI, :, :, :], b_pv[:, :].rearrange("p (b h t) -> p h b t", b=2, h=G),
                               ACT.Copy).then_inc(s_aohi, 1)
            if st.has(1, UNITS):
                _, _, par = unit(st, 1)
                act.wait_ge(s_kn, st.done(1))
                wait(act, s_pv, st.done(3))
                act.activation(vv[:, par, HI, :, :], b_kv[:, :].rearrange("p (b c) -> p b c", b=2)[:, :, HD:2 * HD],
                               ACT.Copy).then_inc(s_vhi, 1)
            if st.has(0, UNITS):
                act.wait_ge(s_q, st.done(0))
                wait(act, s_qms, st.done(1))
                act.activation(qsq[:, :, :], b_q[:, :].rearrange("p (h d) -> p h d", h=G), ACT.Square).then_inc(s_qsq, 1)
            if st.has(1, UNITS):
                act.wait_ge(s_t, st.done(1))
                wait(act, s_s, st.done(2))
                act.activation(qT[:, :, :, :].rearrange("p b h t -> p h b t"),
                               b_tq[:, :].rearrange("p (h b t) -> p h b t", h=G, b=2), ACT.Copy).then_inc(s_qT, 1)
                act.activation(kT[:, :, :], b_tk[:, 0:2 * P].rearrange("p (b k) -> p b k", b=2), ACT.Copy,
                               scale=wqk[:, 3:4]).then_inc(s_kT, 1)
            if st.has(0, UNITS):
                act.wait_ge(s_kv, st.done(0))
                wait(act, s_kms, st.done(1))
                act.activation(ksq[:, :, :], b_kv[:, :].rearrange("p (b c) -> p b c", b=2)[:, :, 0:HD],
                               ACT.Square).then_inc(s_ksq, 1)
            if st.has(2, UNITS):
                act.wait_ge(s_pt, st.done(2))
                wait(act, s_pv, st.done(3))
                act.activation(pT[:, HI, :, :], b_pt[:, :].rearrange("p (b q) -> p b q", b=2), ACT.Copy).then_inc(s_phi, 1)
            if st.has(1, UNITS):
                act.wait_ge(s_max, st.done(1))
                wait(act, s_pt, st.done(2))
                wait(act, s_rec, st.done(2))
                for n in range(4):
                    act.activation(prob[:, n, :], b_s[:, n * P:(n + 1) * P], ACT.Exp, bias=nmax[:, n:n + 1],
                                   accum_out=psum_row[:, n:n + 1]).then_inc(s_exp, 1)
            hi_piece(act, st)

        def dve_step0(st):
            dve = nc.vector
            if st.has(3, UNITS):
                dve.wait_ge(s_aohi, st.done(3))
                dve.tensor_tensor(aoT[:, LO, :, :, :], b_pv[:, :].rearrange("p (b h t) -> p h b t", b=2, h=G),
                                  aoT[:, HI, :, :, :].bitcast(F32), ALU.subtract).then_inc(s_aolo, 1)
            if st.has(4, UNITS):
                p, _, _ = unit(st, 4)
                dve.wait_ge(s_o, st.done(4))
                dve.tensor_tensor(acc[:, p, :], b_o[:, :], acc[:, p, :], ALU.add).then_inc(s_acc, 1)
            if st.has(1, UNITS):
                _, _, par = unit(st, 1)
                dve.wait_ge(s_vhi, st.done(1))
                dve.tensor_tensor(vv[:, par, LO, :, :], b_kv[:, :].rearrange("p (b c) -> p b c", b=2)[:, :, HD:2 * HD],
                                  vv[:, par, HI, :, :].bitcast(F32), ALU.subtract).then_inc(s_vlo, 1)
            if st.has(0, UNITS):
                dve.wait_ge(s_qsq, st.done(0))
                wait(dve, s_rq, st.done(1))
                dve.tensor_reduce(ssq[:, 0:4], qsq[:, :, :], AX, ALU.add).then_inc(s_red, 1)
                dve.wait_ge(s_red, st.done(0, 2) - 1)
                dve.tensor_scalar(msq[:, 0:4], ssq[:, 0:4], 1.0 / HD, RMS_EPS, ALU.mult, ALU.add).then_inc(s_qms, 1)
                dve.wait_ge(s_rq, st.done(0))
                wait(dve, s_t, st.done(1))
                dve.tensor_tensor(qn[:, :, :], b_q[:, :].rearrange("p (h d) -> p h d", h=G),
                                  rms[:, 0:4].unsqueeze(2).to_broadcast([P, G, HD]), ALU.mult).then_inc(s_qn, 1)
                dve.wait_ge(s_ksq, st.done(0))
                wait(dve, s_rk, st.done(1))
                dve.tensor_reduce(ssq[:, 4:6], ksq[:, :, :], AX, ALU.add).then_inc(s_red, 1)
                dve.wait_ge(s_red, st.done(0, 2))
                dve.tensor_scalar(msq[:, 4:6], ssq[:, 4:6], 1.0 / HD, RMS_EPS, ALU.mult, ALU.add).then_inc(s_kms, 1)
            if st.has(1, UNITS):
                dve.wait_ge(s_s, st.done(1))
                wait(dve, s_exp, st.done(2, 4))
                dve.tensor_reduce(nmax[:, :], b_s[:, :].rearrange("p (n k) -> p n k", n=4), AX, ALU.max,
                                  negate=True).then_inc(s_max, 1)
            if st.has(2, UNITS):
                dve.wait_ge(s_phi, st.done(2))
                dve.tensor_tensor(pT[:, LO, :, :].rearrange("p b q -> p (b q)"), b_pt[:, :],
                                  pT[:, HI, :, :].rearrange("p b q -> p (b q)").bitcast(F32),
                                  ALU.subtract).then_inc(s_plo, 1)
            if st.has(0, UNITS):
                dve.wait_ge(s_rk, st.done(0))
                wait(dve, s_t, st.done(1))
                dve.tensor_tensor(kn[:, :, :], b_kv[:, :].rearrange("p (b c) -> p b c", b=2)[:, :, 0:HD],
                                  rms[:, 4:6].unsqueeze(2).to_broadcast([P, 2, HD]), ALU.mult).then_inc(s_kn, 1)
            if st.has(1, UNITS):
                dve.wait_ge(s_exp, st.done(1, 4))
                wait(dve, s_pn, st.done(2))
                dve.reciprocal(rsum[:, :], psum_row[:, :]).then_inc(s_rec, 1)
                dve.wait_ge(s_rec, st.done(1))
                dve.tensor_tensor(prob[:, :, :], prob[:, :, :], rsum[:, :].unsqueeze(2).to_broadcast([P, 4, P]),
                                  ALU.mult).then_inc(s_pn, 1)

        def dve_first(dve):
            dve.wait_ge(s_nw, 32)
            dve.tensor_tensor(wqk[:, 2:3], wqk[:, 0:1], wqk[:, 1:2], ALU.mult).then_inc(s_wqk, 1)
            dve.wait_ge(s_wqk, 1)
            dve.tensor_scalar(wqk[:, 3:4], wqk[:, 2:3], float(HD) ** -0.5, None, ALU.mult).then_inc(s_wqk, 1)
            for p in range(PAIRS + 2):
                dve_tokens(dve, p)
            run_steps(dve, dve_step0, HEAD, PERIOD, ROUNDS, STEPS0, dve_ahead)

        def dve_tokens(dve, p):
            if p < PAIRS:
                dve.wait_ge(sx[p], 16)
                ln_stats(dve, 0, p)
            if 1 <= p <= PAIRS:
                if p >= 3:
                    dve.wait_ge(s_tx, p - 2)
                ln_apply(dve, 0, p - 1, xn0[:, (p - 1) % 2, :])
            if p < PAIRS:
                dve.wait_ge(s_chi, p + 1)
                dve.tensor_tensor(kv_context(LO, p), by_batch(bank[CTX_BANK[p]]), kv_context(HI, p).bitcast(F32),
                                  ALU.subtract).then_inc(s_clo, 1)
            if p >= 2:
                dve.wait_ge(s_xhi, p - 1)
                dve.tensor_tensor(kv_latents(LO, p - 2), by_batch(bank[X_BANK[p - 2]]),
                                  kv_latents(HI, p - 2).bitcast(F32), ALU.subtract).then_inc(s_xlo, 1)

        def first_wo_lo(pool, h):
            pool.wait_ge(s_wo_hi, h + 1)
            pool.tensor_tensor(wo[:, 0, LO, h, :], wo_raw[:, h % 2, :], wo[:, 0, HI, h, :].bitcast(F32),
                               ALU.subtract).then_inc(s_wo, 1)

        def pool_first(pool):
            for p in range(PAIRS + 1):
                if p < PAIRS:
                    ln_power(pool, 0, p)
                n = p - 2
                if n >= KT:
                    first_wo_lo(pool, n - KT)
                elif n >= 0:
                    pool.wait_ge(s_wqkv_hi, n + 1)
                    pool.tensor_tensor(wqkv[:, 0, LO, n, :], wqkv_raw[:, n % 2, :], wqkv[:, 0, HI, n, :].bitcast(F32),
                                       ALU.subtract).then_inc(s_wqkv, 1)
            run_steps(pool, pool_step0, HEAD, PERIOD, ROUNDS, STEPS0, pool_after0)

        def pool_after0(j):
            pool = nc.gpsimd
            if j == 2:
                pool.wait_ge(s_tx, PAIRS)
                pool.memset(s_raw[:, :], 0.0).then_inc(s_zero, 1)
            pool_ahead(j)

        def pool_step0(st):
            pool = nc.gpsimd
            if st.has(0, UNITS):
                pool.wait_ge(s_qms, st.done(0))
                wait(pool, s_qn, st.done(1))
                pool.tensor_tensor(rms[:, 0:4], msq[:, 0:4], half_neg[:, 0:4], ALU.pow).then_inc(s_rq, 1)
                pool.wait_ge(s_kms, st.done(0))
                wait(pool, s_kn, st.done(1))
                pool.tensor_tensor(rms[:, 4:6], msq[:, 4:6], half_neg[:, 4:6], ALU.pow).then_inc(s_rk, 1)
            lo_piece(pool, st)

        s_bn = sem("s_bn")

        def ln_stats(dve, which, p):
            n = which * PAIRS + p
            dve.bn_stats(stat[:, n % 16, :], acc[:, p, :]).then_inc(s_bn, 1)
            dve.wait_ge(s_bn, 2 * n + 1)
            dve.bn_aggr(mv[:, which, p, :], stat[:, n % 16, :]).then_inc(s_bn, 1)
            dve.wait_ge(s_bn, 2 * n + 2)
            dve.tensor_scalar(mv[:, which, p, 1:2], mv[:, which, p, 1:2], LN_EPS, None, ALU.add).then_inc(s_stat, 1)

        def ln_power(pool, which, p):
            pool.wait_ge(s_stat, which * PAIRS + p + 1)
            pool.tensor_tensor(rstd[:, which, p:p + 1], mv[:, which, p, 1:2], half_neg[:, 0:1], ALU.pow).then_inc(s_rstd, 1)

        def ln_apply(dve, which, p, to):
            dve.wait_ge(s_rstd, which * PAIRS + p + 1)
            dve.tensor_scalar(to, acc[:, p, :], mv[:, which, p, 0:1], rstd[:, which, p:p + 1],
                              ALU.subtract, ALU.mult).then_inc(s_xn, 1)

        s_pid, s_col, s_zero = sem("s_pid"), sem("s_col"), sem("s_zero")
        s_idx, s_sraw, s_zraw = sem("s_idx"), sem("s_sraw"), sem("s_zraw")
        s_idx_v, s_scale_v, s_zero_v = sem("s_idx_v"), sem("s_scale_v"), sem("s_zero_v")
        s_packed = sems("s_packed", 3)
        s_nib, s_zs, s_wt, s_whi, s_wlo = sem("s_nib"), sem("s_zs"), sem("s_wt"), sem("s_whi"), sem("s_wlo")
        s_tx2, s_x2hi, s_x2lo = sem("s_tx2"), sem("s_x2hi"), sem("s_x2lo")
        s_g, s_u, s_d, s_gact, s_hval, s_hhi, s_hlo, s_y2 = (
            sem(f"s_{n}") for n in ("g", "u", "d", "gact", "hval", "hhi", "hlo", "y2"))
        f_g, f_u = bank[0], bank[1]
        f_z = bank[2:4]
        f_d = bank[4:8]
        SCALE_ROWS = (0, 64, 96)
        TABLES = (("gate", GATE, F, GG), ("up", UP, F, GG), ("down", DOWN, D, GD))
        CHUNKS = 6
        HP = PAIRS // 2
        AHEAD = 2 * FT - 6
        EVEN_DONE = UNITS - PAIRS
        s_rest = sem("s_rest")
        HALF_ZS, QUARTER_ZS = ZS // 2, ZS // 4
        X2 = 1

        def width(f):
            return min(P, F - f * P)

        def sp_scales(sp):
            sp.wait_ge(s_zero, 1)
            for m, at, n, g in TABLES:
                for row in SCALE_ROWS:
                    sp.dma_start(s_raw[row:row + g, at:at + n], a[f"L0_ffn_{m}_scales"]).then_inc(s_sraw, 16)

        def sp_ffn(sp):
            sp.wait_ge(s_q, EVEN_DONE)
            sp.wait_ge(s_kv, EVEN_DONE)
            for m, at, n, g in TABLES:
                sp.dma_start(z_raw[0:g, at // 8:(at + n) // 8], a[f"L0_ffn_{m}_qzeros"]).then_inc(s_zraw, 16)
            sp.wait_ge(s_o, EVEN_DONE)
            for n, (m, count) in enumerate((("gate", D), ("up", D), ("down", F))):
                sp.dma_start(idx_raw[:, n * D:n * D + count],
                             a[f"L0_ffn_{m}_g_idx"].rearrange("(o k) -> o k", o=1).to_broadcast([P, count])).then_inc(s_idx, 16)
            sp.wait_ge(s_zero_v, 18)
            for f in range(FT):
                w = width(f)
                for k, m in enumerate(("gate", "up")):
                    if f >= 1:
                        sp.wait_ge(s_nib, 2 * (CHUNKS * (f - 1) + 2 * k + 2) - 1)
                    rows = a[f"L0_ffn_{m}_qweight"].rearrange("(t r) n -> t r n", t=KT)
                    for kt in range(KT):
                        sp.dma_start(packed[:, k, kt * P:kt * P + w],
                                     rows[kt, :, f * P:f * P + w].unsqueeze(1).to_broadcast([P // 8, 8, w])
                                     ).then_inc(s_packed[k], 16)
                if f >= 1:
                    sp.wait_ge(s_nib, 2 * CHUNKS * f - 1)
                sp.dma_start(packed[0:w, 2, :],
                             a["L0_ffn_down_qweight"][f * P // 8:(f * P + w) // 8, :].unsqueeze(1)
                             .to_broadcast([w // 8, 8, D])).then_inc(s_packed[2], 16)

        def pool_ahead(j):
            pool = nc.gpsimd
            n = j - EVEN_DONE
            if n == 1:
                pool.wait_ge(s_kv, EVEN_DONE)
                pool.wait_ge(s_wo, 4 * KVH)
                pool.iota(pid[:, :], pattern=[[0, 1]], base=0, channel_multiplier=1).then_inc(s_pid, 1)
                pool.memset(zs[:, 0, :], 0.0).then_inc(s_zero, 1)
            if 2 <= n <= 5:
                half = n % 2
                pool.wait_ge(s_scale_v, n - 1)
                for q in (2 * half, 2 * half + 1):
                    cols = slice(q * QUARTER_ZS, (q + 1) * QUARTER_ZS)
                    pool.tensor_tensor(s_raw[:, cols], s_raw[:, cols], zs[:, 1, cols],
                                       ALU.subtract).then_inc(s_rest, 1)
            if 5 <= n <= 8:
                ln_power(pool, X2, n - 5)
            if 9 <= n <= 11:
                w_lo(pool, 0, (2 * (n - 9), 2 * (n - 9) + 1))

        def w_lo(pool, f, ks):
            for k in ks:
                c = CHUNKS * f + k
                dst, rows = weight_chunk(f, k, LO)
                hi, _ = weight_chunk(f, k, HI)
                pool.wait_ge(s_whi, c + 1)
                pool.tensor_tensor(dst, chunk_shape(wtmp[:, c % 2, :], f, k), hi.bitcast(F32),
                                   ALU.subtract).then_inc(s_wlo, 1)

        def pool_ffn(pool):
            for p in range(HP, PAIRS):
                ln_power(pool, X2, p)
            for f in range(1, FT):
                w_lo(pool, f, range(CHUNKS))

        def weight_chunk(f, k, part):
            w = width(f)
            if k < 4:
                return wgu[:, f, part, k // 2, 2 * (k % 2):2 * (k % 2) + 2, 0:w], P
            return wd[0:w, f, part, (k - 4) * 256:(k - 3) * 256], w

        def chunk_shape(ap, f, k):
            w = width(f)
            if k < 4:
                return ap.rearrange("p (t n) -> p t n", t=2)[:, :, 0:w]
            return ap[0:w, :]

        def zs_bank(f, k):
            c = CHUNKS * f + k
            return bank[c] if c < 2 else f_z[c % 2]

        def zero_scale(f, k, which):
            b, w = zs_bank(f, k), width(f)
            if k < 4:
                return b[:, :].rearrange("p (t z n) -> p t z n", t=2, z=2)[:, :, which, 0:w]
            return b[0:w, which * 256:(which + 1) * 256]

        def pe_ahead(j):
            pe = nc.tensor
            n = j - UNITS
            if n == 0:
                pe.wait_ge(s_qT, UNITS)
                pe.wait_ge(s_kT, UNITS)
                x2_transposes(pe, 0)
                x2_transposes(pe, 1)
                pe.wait_ge(s_idx_v, 8)
                pe.wait_ge(s_scale_v, 6)
                pe.wait_ge(s_zero_v, 18)
                pe.wait_ge(s_qn, UNITS)
                pe.wait_ge(s_vlo, UNITS)
                spread(pe, 0, (0, 1))
            if n == 1:
                x2_transposes(pe, 2)
                x2_transposes(pe, 3)
            if n == 2:
                spread(pe, 0, (2, 3))
                inner_product(pe, 0, 0)
            if n == 3:
                spread(pe, 0, (4, 5))

        def spread(pe, f, ks):
            w = width(f)
            for k in ks:
                c = CHUNKS * f + k
                b = zs_bank(f, k)
                if c >= 4:
                    pe.wait_ge(s_wt, c - 1)
                elif c >= 2:
                    pe.wait_ge(s_x2lo, HP)
                if k < 4:
                    at = (GATE, UP)[k // 2] + f * P
                    for t in range(2):
                        kt = 2 * (k % 2) + t
                        mm = pe.matmul(b[:, t * 256:(t + 1) * 256].rearrange("p (z n) -> p z n", z=2)[:, :, 0:w],
                                       oh_gu[:, k // 2, kt * P:(kt + 1) * P], zs[:, :, at:at + w],
                                       start=True, stop=True)
                else:
                    at = DOWN + (k - 4) * 256
                    mm = pe.matmul(b[0:w, :].rearrange("p (z n) -> p z n", z=2), oh_d[:, f * P:f * P + w],
                                   zs[:, :, at:at + 256], start=True, stop=True)
                mm.then_inc(s_zs, 1)

        def spread_next(pe, n, k):
            if n + 1 < FT:
                spread(pe, n + 1, (k,))

        def inner_product(pe, n, m):
            half, f = divmod(n, FT)
            w = width(f)
            b, used, done = ((f_g, s_gact, s_g), (f_u, s_hval, s_u))[m]
            if half == 0:
                pe.wait_ge(s_wlo, CHUNKS * f + 2 * m + 2)
            if n >= 1:
                pe.wait_ge(used, n)
            for kt in range(KT):
                for k, (l, r) in enumerate(PASSES):
                    mm = pe.matmul(b[0:w, :], wgu[:, f, l, m, kt, 0:w], x2T[:, r, kt, :],
                                   start=(kt == 0 and k == 0), stop=(kt == KT - 1 and k == 2))
                if kt == KT // 2 - 1 and n >= 1:
                    spread_next(pe, n, 2 * m)
            mm.then_inc(done, 1)
            if n >= 1:
                spread_next(pe, n, 2 * m + 1)

        def pe_ffn(pe):
            def down(n, now):
                half, f = divmod(n, FT)
                w = width(f)
                if half == 0:
                    pe.wait_ge(s_wlo, CHUNKS * (f + 1))
                if n == 0:
                    pe.wait_ge(s_acc, UNITS)
                pe.wait_ge(s_hlo, n + 1)
                for t in range(HP):
                    if f == 0 and half == 1:
                        pe.wait_ge(s_y2, t + 1)
                    for k, (l, r) in enumerate(PASSES):
                        mm = pe.matmul(f_d[t][:, :], hT[0:w, l, t * P:(t + 1) * P], wd[0:w, f, r, :],
                                       start=(f == 0 and k == 0), stop=(f == FT - 1 and k == 2))
                    if t == HP // 2 - 1:
                        spread_next(pe, now, 4)
                mm.then_inc(s_d, 1)
                spread_next(pe, now, 5)

            for n in range(2 * FT):
                half, f = divmod(n, FT)
                if half == 1 and f == 0:
                    pe.wait_ge(s_wt, CHUNKS * FT)
                    for p in range(HP, PAIRS):
                        x2_transposes(pe, p)
                    down(n - 1, n)
                    pe.wait_ge(s_x2lo, PAIRS)
                if n >= 1:
                    inner_product(pe, n, 0)
                else:
                    spread(pe, 1, (0, 1))
                inner_product(pe, n, 1)
                if f >= 1:
                    down(n - 1, n)
                elif n == 0:
                    spread(pe, 1, (2, 3, 4, 5))
            down(2 * FT - 1, 2 * FT)

        def x2_transposes(pe, p):
            pe.wait_ge(s_xn, X2 * PAIRS + p + 1)
            if p == HP:
                pe.wait_ge(s_u, FT)
            if p >= 2:
                pe.wait_ge(s_x2lo, p - 1)
            for kt in range(KT):
                mm = pe.transpose(f_z[p % 2][:, kt * P:(kt + 1) * P], xn2[:, p % 2, kt * P:(kt + 1) * P], ident[:, :])
            mm.then_inc(s_tx2, 1)

        def x2_tile(part, p):
            return x2T[:, part, :, p % HP * P:(p % HP + 1) * P]

        def tiles(b):
            return b[:, :].rearrange("p (k t) -> p k t", k=KT)

        def act_ahead(j):
            act = nc.scalar
            n = j - EVEN_DONE
            if 1 <= n <= 6:
                part, half = divmod(n - 1, 2)
                row = SCALE_ROWS[part]
                cols = slice(half * HALF_ZS, (half + 1) * HALF_ZS)
                if n == 1:
                    act.wait_ge(s_sraw, 16 * 9)
                    act.wait_ge(s_wo, 4 * KVH)
                    act.wait_ge(s_kv, EVEN_DONE)
                if part >= 1:
                    act.wait_ge(s_rest, 2 * (n - 2))
                act.activation(zs[row:P, 1, cols], s_raw[row:P, cols], ACT.Copy).then_inc(s_scale_v, 1)
            if n == 8:
                x2_hi(act, 0)
                x2_hi(act, 1)
            if n == 9:
                x2_hi(act, 2)
                x2_hi(act, 3)
                w_hi(act, 0, (0, 1))
            if n == 10:
                w_hi(act, 0, (2, 3))
            if n == 11:
                w_hi(act, 0, (4, 5))

        def x2_hi(act, p):
            act.wait_ge(s_tx2, p + 1)
            act.activation(x2_tile(HI, p), tiles(f_z[p % 2]), ACT.Copy).then_inc(s_x2hi, 1)

        def w_hi(act, f, ks):
            for k in ks:
                c = CHUNKS * f + k
                dst, _ = weight_chunk(f, k, HI)
                act.wait_ge(s_wt, c + 1)
                act.activation(dst, chunk_shape(wtmp[:, c % 2, :], f, k), ACT.Copy).then_inc(s_whi, 1)

        def act_ffn(act):
            for n in range(2 * FT):
                half, f = divmod(n, FT)
                w = width(f)
                if n == FT:
                    for p in range(HP, PAIRS):
                        x2_hi(act, p)
                if n == AHEAD:
                    act.wait_ge(s_zs, CHUNKS * FT)
                    act_context(act, 0, 0)
                if n == AHEAD + 2:
                    act_queries(act, 0, 0)
                act.wait_ge(s_g, n + 1)
                if n >= 1:
                    act.wait_ge(s_hval, n)
                act.activation(gact[0:w, :], f_g[0:w, :], ACT.Silu).then_inc(s_gact, 1)
                if n + 1 < FT:
                    w_hi(act, f + 1, (0, 1, 2, 3))
                act.wait_ge(s_hval, n + 1)
                if n >= 1:
                    act.wait_ge(s_d, n)
                act.activation(hT[0:w, HI, :], hval[0:w, :], ACT.Copy).then_inc(s_hhi, 1)
                if n + 1 < FT:
                    w_hi(act, f + 1, (4, 5))

        def one_hot(dve, part):
            cols, g, to = ((slice(0, 2 * D), GG, oh_gu[:, :, :].rearrange("p m k -> p (m k)")),
                           (slice(2 * D, 2 * D + F), GD, oh_d[:, :]))[part // 2]
            raw, n = idx_raw[:, cols], idx_n[:, 0:cols.stop - cols.start]
            if part:
                dve.wait_ge(s_idx_v, 2 * part)
            if part % 2 == 0:
                dve.tensor_scalar(n, raw, 0.0, float(g), ALU.is_lt, ALU.mult).then_inc(s_idx_v, 1)
                dve.wait_ge(s_idx_v, 2 * part + 1)
                dve.tensor_tensor(n, raw, n, ALU.add).then_inc(s_idx_v, 1)
            else:
                dve.tensor_scalar(n, n, float(g - 1), 0.0, ALU.min, ALU.max).then_inc(s_idx_v, 1)
                dve.wait_ge(s_idx_v, 2 * part + 1)
                dve.tensor_scalar(to, n, grp[:, 0:1], None, ALU.is_equal).then_inc(s_idx_v, 1)

        ZERO_TABLES = ((GG, GATE, UP + F), (GD, DOWN, DOWN + D))

        def dve_ahead(j):
            dve = nc.vector
            n = j - EVEN_DONE
            if n == 1 or n == 2:
                if n == 1:
                    dve.wait_ge(s_zraw, 48)
                for k in range(4 * (n - 1), 4 * n):
                    for g, lo, hi in ZERO_TABLES:
                        dve.tensor_scalar(z_int[0:g, lo // 8:hi // 8, k], z_raw[0:g, lo // 8:hi // 8], 4 * k, 15,
                                          ALU.logical_shift_right, ALU.bitwise_and).then_inc(s_zero_v, 1)
            if n == 2:
                dve.wait_ge(s_pid, 1)
                dve.tensor_scalar(shift[:, :], pid[:, :], 7, 2, ALU.bitwise_and, ALU.logical_shift_left).then_inc(s_col, 1)
                dve.tensor_scalar(grp_i[:, :], pid[:, :], 31, None, ALU.bitwise_and).then_inc(s_col, 1)
                dve.wait_ge(s_col, 2)
                dve.tensor_copy(grp[:, :], grp_i[:, :]).then_inc(s_col, 1)
            if n == 3:
                dve.wait_ge(s_zero_v, 16)
                dve.wait_ge(s_zero, 2)
                for g, lo, hi in ZERO_TABLES:
                    dve.tensor_scalar(zs[0:g, 0, lo:hi], z_int[0:g, lo // 8:hi // 8, :].rearrange("p c j -> p (c j)"), 1, None,
                                      ALU.add).then_inc(s_zero_v, 1)
            if n == 4:
                dve.wait_ge(s_col, 3)
                dve.wait_ge(s_idx, 48)
            if 4 <= n <= 7:
                one_hot(dve, n - 4)
            if n == 6 or n == 7:
                dve.wait_ge(s_zero_v, 18)
                ln_apply(dve, X2, n - 6, xn2[:, n - 6, :])
            if n == 9:
                for p in (2, 3):
                    dve.wait_ge(s_tx2, p - 1)
                    ln_apply(dve, X2, p, xn2[:, p % 2, :])
            if n == 9 or n == 10:
                for p in (2 * (n - 9), 2 * (n - 9) + 1):
                    dve.wait_ge(s_x2hi, p + 1)
                    x2_lo(dve, p)
            if n == 9 or n == 10:
                dequant(dve, 0, (2 * (n - 9), 2 * (n - 9) + 1))
            if n == 11:
                dequant(dve, 0, (4, 5))
            if n >= 4:
                dve.wait_ge(s_acc, EVEN_DONE + n - 3)
                ln_stats(dve, X2, n - 4)

        def dequant(dve, f, ks):
            w = width(f)
            for k in ks:
                c = CHUNKS * f + k
                kind = k // 2
                if k % 2 == 0:
                    dve.wait_ge(s_packed[kind], (64, 64, 16)[kind] * (f + 1))
                if c >= 1:
                    dve.wait_ge(s_nib, 2 * c)
                raw = chunk_shape(packed[:, kind, (k % 2) * 256:(k % 2 + 1) * 256], f, k)
                n_, i_, t_ = (chunk_shape(v, f, k) for v in (nib[:, :], wint[:, :], wtmp[:, c % 2, :]))
                rows = P if k < 4 else w
                dve.tensor_scalar(n_, raw, shift[0:rows, 0:1], 15, ALU.logical_shift_right,
                                  ALU.bitwise_and).then_inc(s_nib, 1)
                dve.wait_ge(s_nib, 2 * c + 1)
                dve.wait_ge(s_zs, c + 1)
                if c >= 1:
                    dve.wait_ge(s_wt, c)
                dve.tensor_tensor(i_, n_, zero_scale(f, k, 0), ALU.subtract).then_inc(s_nib, 1)
                dve.wait_ge(s_nib, 2 * c + 2)
                if c >= 2:
                    dve.wait_ge(s_wlo, c - 1)
                dve.tensor_tensor(t_, i_, zero_scale(f, k, 1), ALU.mult).then_inc(s_wt, 1)

        def dve_ffn(dve):
            for n in range(2 * FT):
                half, f = divmod(n, FT)
                w = width(f)
                if n == AHEAD:
                    dve.wait_ge(s_u, FT + 1)
                    dve.memset(vTz[:, :, :, :, T:2 * T].bitcast(F32), 0.0).then_inc(s_vz, 1)
                    dve.wait_ge(s_y2, 1)
                    dve_stats(dve, 0)
                    dve.wait_ge(s_bn3, 1)
                    dve_aggregate(dve, 0, 0)
                if n == AHEAD + 1:
                    dve_queries(dve, 0, 0)
                if n == FT - 1:
                    for p in (HP, HP + 1):
                        ln_apply(dve, X2, p, xn2[:, p % 2, :])
                if n == FT:
                    for p in range(HP, PAIRS):
                        dve.wait_ge(s_x2hi, p + 1)
                        x2_lo(dve, p)
                        if p + 2 < PAIRS:
                            ln_apply(dve, X2, p + 2, xn2[:, p % 2, :])
                    add_down(dve, 0)
                if n + 1 < FT:
                    dequant(dve, f + 1, (0, 1, 2))
                dve.wait_ge(s_gact, n + 1)
                dve.wait_ge(s_u, n + 1)
                if n >= 1:
                    dve.wait_ge(s_hlo, n)
                dve.tensor_tensor(hval[0:w, :], gact[0:w, :], f_u[0:w, :], ALU.mult).then_inc(s_hval, 1)
                if n + 1 < FT:
                    dequant(dve, f + 1, (3, 4))
                dve.wait_ge(s_hhi, n + 1)
                dve.tensor_tensor(hT[0:w, LO, :], hval[0:w, :], hT[0:w, HI, :].bitcast(F32), ALU.subtract).then_inc(s_hlo, 1)
                if n + 1 < FT:
                    dequant(dve, f + 1, (5,))
            add_down(dve, 1)

        def x2_lo(dve, p):
            dve.tensor_tensor(x2_tile(LO, p), tiles(f_z[p % 2]), x2_tile(HI, p).bitcast(F32), ALU.subtract).then_inc(s_x2lo, 1)

        def add_down(dve, half):
            dve.wait_ge(s_d, FT * (half + 1))
            for t in range(HP):
                p = half * HP + t
                dve.tensor_tensor(acc[:, p, :], f_d[t][:, :], acc[:, p, :], ALU.add).then_inc(s_y2, 1)

        c_s = (bank[0], bank[1], bank[4], bank[5])
        c_t = (bank[3], bank[7])
        c_v = (bank[2], bank[6])
        TILES = B * KT
        HEAD1 = PERIOD1 = 4 * KT
        ROUNDS1 = 2
        LT, LV, LY = 7, 9, 9
        STEPS1 = TILES + LY
        PT_ = 2 * KT
        s_cx = sems("s_cx", 2)
        (s_bn3, s_st3, s_rs3, s_xn3, s_cR, s_cRl, s_qR, s_qRl, s_ct, s_vT, s_vTl, s_vz) = (
            sem(f"s_{n}") for n in ("bn3", "st3", "rs3", "xn3", "cR", "cRl", "qR", "qRl", "ct", "vT", "vTl", "vz"))
        (s_s1, s_m1, s_e1, s_r1, s_n1, s_n1p, s_t1, s_p1, s_p1l, s_v1, s_y3) = (
            sem(f"s_{n}") for n in ("s1", "m1", "e1", "r1", "n1", "n1p", "t1", "p1", "p1l", "v1", "y3"))

        def acc_at(p):
            if isinstance(p, int):
                return acc[:, p, :]
            return acc[:, bass.ds(p, 1), :].rearrange("p o d -> p (o d)")

        def prepared(st):
            q = st.j // PT_ + 1
            if isinstance(st.i, int) and q >= PAIRS:
                return None
            return q + st.i * (PERIOD1 // PT_), q % 2

        def current(st):
            q = st.j // PT_
            return q + st.i * (PERIOD1 // PT_), q % 2

        def sp_l1x(sp):
            sp.wait_ge(s_zs, CHUNKS * FT)
            for q in range(PAIRS):
                if q >= 2:
                    sp.wait_ge(s_ct, q - 1)
                    sp.wait_ge(s_cRl, q - 1)
                sp.dma_start(cx[:, q % 2, :], ctx_t[q]).then_inc(s_cx[q % 2], 16)
                if q == 2:
                    sp_loads4(sp)

        def arrived(eng, q, par):
            eng.wait_ge(s_cx[par], 8 * (q - par) + 16)

        def dve_stats(dve, q):
            dve.bn_stats(st3[:, :], acc_at(q)).then_inc(s_bn3, 1)

        def dve_aggregate(dve, q, par):
            dve.bn_aggr(mv3[:, par, :], st3[:, :]).then_inc(s_bn3, 1)
            dve.wait_ge(s_bn3, 2 * q + 2)
            dve.tensor_scalar(mv3[:, par, 1:2], mv3[:, par, 1:2], LN_EPS, None, ALU.add).then_inc(s_st3, 1)

        def pool_norm(pool, q, par):
            pool.wait_ge(s_st3, q + 1)
            pool.tensor_tensor(rs3[:, par, 0:1], mv3[:, par, 1:2], half_neg[:, 0:1], ALU.pow).then_inc(s_rs3, 1)
            pool.wait_ge(s_rs3, 2 * q + 1)
            pool.tensor_tensor(rs3[:, par, 1:2], rs3[:, par, 0:1], inv_sqrt_t[:, :], ALU.mult).then_inc(s_rs3, 1)

        def dve_queries(dve, q, par):
            dve.wait_ge(s_rs3, 2 * q + 2)
            wait(dve, s_qRl, q - 1)
            dve.tensor_scalar(xn3[:, par, :], acc_at(q), mv3[:, par, 0:1], rs3[:, par, 1:2],
                              ALU.subtract, ALU.mult).then_inc(s_xn3, 1)

        def act_context(act, q, par):
            arrived(act, q, par)
            wait(act, s_s1, PT_ * (q - 1))
            act.activation(cR[:, par, HI, :], cx[:, par, :], ACT.Copy).then_inc(s_cR, 1)

        def pool_context(pool, q, par):
            pool.wait_ge(s_cR, q + 1)
            pool.tensor_tensor(cR[:, par, LO, :], cx[:, par, :], cR[:, par, HI, :].bitcast(F32),
                               ALU.subtract).then_inc(s_cRl, 1)

        def act_queries(act, q, par):
            act.wait_ge(s_xn3, q + 1)
            wait(act, s_s1, PT_ * (q - 1))
            act.activation(qR[:, par, HI, :], xn3[:, par, :], ACT.Copy).then_inc(s_qR, 1)

        def pool_queries(pool, q, par):
            pool.wait_ge(s_qR, q + 1)
            pool.tensor_tensor(qR[:, par, LO, :], xn3[:, par, :], qR[:, par, HI, :].bitcast(F32),
                               ALU.subtract).then_inc(s_qRl, 1)

        def pe_context(pe, q, par):
            arrived(pe, q, par)
            wait(pe, s_y3, q - 1)
            for t in range(KT):
                mm = pe.transpose(c_v[par][:, t * P:(t + 1) * P], cx[:, par, t * P:(t + 1) * P], ident[:, :])
            mm.then_inc(s_ct, 1)

        def vT_of(par, part):
            return vTz[:, par, :, part, :].rearrange("p t (x c) -> p t x c", x=3)[:, :, 0::2, :]

        def c_view(par):
            return c_v[par][:, :].rearrange("p (t b c) -> p t b c", t=KT, b=2)

        def act_values(act, q, par):
            act.wait_ge(s_ct, q + 1)
            wait(act, s_v1, PT_ * (q - 1))
            act.activation(vT_of(par, HI), c_view(par), ACT.Copy).then_inc(s_vT, 1)

        def dve_values(dve, q, par):
            dve.wait_ge(s_vT, q + 1)
            dve.tensor_tensor(vT_of(par, LO), c_view(par), vT_of(par, HI).bitcast(F32), ALU.subtract).then_inc(s_vTl, 1)

        def pe_l1x(pe):
            run_steps(pe, pe_step1, HEAD1, PERIOD1, ROUNDS1, STEPS1, pe_ahead4)

        def pe_step1(st):
            pe = nc.tensor
            if st.has(0, TILES):
                t = st.j
                par, r0, n = t // PT_ % 2, t // KT % 2 * T, t % KT
                if t % PT_ == 0:
                    pe.wait_ge(s_cRl, st.i * 2 + t // PT_ + 1)
                    pe.wait_ge(s_qRl, st.i * 2 + t // PT_ + 1)
                wait(pe, s_e1, st.done(4))
                if isinstance(st.i, int) and t in (2, 3, 4):
                    pe.wait_ge(s_y2, (5, 6, 8)[t - 2])
                for k, (l, r) in enumerate(PASSES):
                    mm = pe.matmul(c_s[t % 4][:, :], cR[r0:r0 + T, par, l, n * P:(n + 1) * P],
                                   qR[r0:r0 + T, par, r, :], start=(k == 0), stop=(k == 2))
                mm.then_inc(s_s1, 1)
            if st.has(LT, TILES):
                t = st.j - LT
                b, m = t // KT % 4, t % KT
                if m == 0:
                    pe.wait_ge(s_n1, 2 * (t // KT + 1) + st.i * 8)
                    pe.wait_ge(s_n1p, 2 * (t // KT + 1) + st.i * 8)
                wait(pe, s_p1l, st.done(LT + 2))
                for n in range(KT):
                    mm = pe.transpose(c_t[t % 2][:, n * P:(n + 1) * P], pr[:, b, n, m * P:(m + 1) * P], ident[:, :])
                mm.then_inc(s_t1, 1)
            if st.has(LV, TILES):
                t = st.j - LV
                par, b, m = t // PT_ % 2, t // KT % 2, t % KT
                if t % PT_ == 0:
                    pe.wait_ge(s_vz, 1)
                    pe.wait_ge(s_vTl, st.i * 2 + t // PT_ + 1)
                pe.wait_ge(s_p1l, st.done(LV))
                for k, (l, r) in enumerate(PASSES):
                    mm = pe.matmul(c_v[par][:, :], vTz[:, par, m, l, b * T:b * T + P], pmT[:, t % 4, r, :],
                                   start=(t % PT_ == 0 and k == 0), stop=(t % PT_ == PT_ - 1 and k == 2))
                mm.then_inc(s_v1, 1)
            if st.j % PT_ == 1 and st.has(0, TILES):
                pe_context(pe, *current(st))

        def act_l1x(act):
            run_steps(act, act_step1, HEAD1, PERIOD1, ROUNDS1, STEPS1, act_ahead4)

        def act_step1(st):
            act = nc.scalar
            if st.has(LT, TILES):
                t = st.j - LT
                act.wait_ge(s_t1, st.done(LT))
                wait(act, s_v1, st.done(LT + 4))
                act.activation(pmT[:, t % 4, HI, :], c_t[t % 2][:, :], ACT.Copy).then_inc(s_p1, 1)
            if st.has(0, TILES):
                t = st.j
                act.wait_ge(s_m1, st.done(0))
                if t % KT == 0:
                    wait(act, s_t1, st.done(0) - 1 - 3 * KT)
                wait(act, s_r1, st.done(4))
                act.activation(pr[:, t // KT % 4, t % KT, :], c_s[t % 4][:, :], ACT.Exp, bias=nm1[:, t % 4:t % 4 + 1],
                               accum_out=sm1[:, t % 4:t % 4 + 1]).then_inc(s_e1, 1)
            if prepared(st):
                if st.j % PT_ == 0:
                    act_context(act, *prepared(st))
                if st.j % PT_ == 2:
                    act_queries(act, *prepared(st))
            if st.j % PT_ == 2 and st.has(0, TILES):
                act_values(act, *current(st))

        def dve_l1x(dve):
            run_steps(dve, dve_step1, HEAD1, PERIOD1, ROUNDS1, STEPS1, dve_ahead4)

        def dve_step1(st):
            dve = nc.vector
            norm = prepared(st) if st.j % PT_ == 0 else None
            if norm:
                dve_stats(dve, norm[0])
            if st.has(0, TILES):
                t = st.j
                dve.wait_ge(s_s1, st.done(0))
                wait(dve, s_e1, st.done(4))
                if norm:
                    dve.wait_ge(s_bn3, 2 * norm[0] + 1)
                dve.tensor_reduce(nm1[:, t % 4:t % 4 + 1], c_s[t % 4][:, :], AX, ALU.max, negate=True).then_inc(s_m1, 1)
            if norm:
                dve_aggregate(dve, *norm)
            if st.has(LT, TILES):
                t = st.j - LT
                dve.wait_ge(s_p1, st.done(LT))
                dve.tensor_tensor(pmT[:, t % 4, LO, :], c_t[t % 2][:, :], pmT[:, t % 4, HI, :].bitcast(F32),
                                  ALU.subtract).then_inc(s_p1l, 1)
            if st.has(1, TILES):
                t = st.j - 1
                dve.wait_ge(s_e1, st.done(1))
                if t % 2:
                    wait(dve, s_n1p, pool_normed(st, 1, t) - 2)
                else:
                    wait(dve, s_n1, pool_normed(st, 1, t) - 2)
                dve.reciprocal(rc1[:, t % 4:t % 4 + 1], sm1[:, t % 4:t % 4 + 1]).then_inc(s_r1, 1)
                if t % 2 == 0:
                    dve.wait_ge(s_r1, st.done(1))
                    dve.tensor_scalar(pr[:, t // KT % 4, t % KT, :], pr[:, t // KT % 4, t % KT, :],
                                      rc1[:, t % 4:t % 4 + 1], None, ALU.mult).then_inc(s_n1, 1)
            if st.has(LY, TILES) and (st.j - LY) % PT_ == PT_ - 1:
                q = (st.j - LY) // PT_ + st.i * 2
                dve.wait_ge(s_v1, st.done(LY))
                dve.tensor_tensor(acc_at(q), c_v[(st.j - LY) // PT_ % 2][:, :], acc_at(q), ALU.add).then_inc(s_y3, 1)
            if prepared(st):
                if st.j % PT_ == 1:
                    dve_queries(dve, *prepared(st))
            if st.j % PT_ == 4 and st.has(0, TILES):
                dve_values(dve, *current(st))

        def pool_normed(st, lag, t):
            return t // 2 + 1 + st.i * (PERIOD1 // 2)

        def pool_l1x(pool):
            pool_norm(pool, 0, 0)
            pool_context(pool, 0, 0)
            pool_queries(pool, 0, 0)
            run_steps(pool, pool_step1, HEAD1, PERIOD1, ROUNDS1, STEPS1, pool_ahead4)

        def pool_step1(st):
            pool = nc.gpsimd
            if st.has(1, TILES) and (st.j - 1) % 2 == 1:
                t = st.j - 1
                pool.wait_ge(s_r1, st.done(1))
                pool.tensor_tensor(pr[:, t // KT % 4, t % KT, :], pr[:, t // KT % 4, t % KT, :],
                                   rc1[:, t % 4:t % 4 + 1].to_broadcast([P, D]), ALU.mult).then_inc(s_n1p, 1)
            if prepared(st):
                if st.j % PT_ == 0:
                    pool_norm(pool, *prepared(st))
                if st.j % PT_ == 2:
                    pool_context(pool, *prepared(st))
                if st.j % PT_ == 4:
                    pool_queries(pool, *prepared(st))

        s_ld_o, s_ld_q, s_ld_u = sem("s_ld_o"), sem("s_ld_q"), sem("s_ld_u")
        s_ld_d = sems("s_ld_d", KT)
        (s_wot, s_woh, s_wol, s_sm, s_smc, s_dnh, s_dnl, s_uph, s_upl, s_tx4, s_x4h, s_x4l, s_mean) = (
            sem(f"s_{n}") for n in ("wot", "woh", "wol", "sm", "smc", "dnh", "dnl", "uph", "upl", "tx4", "x4h", "x4l", "mean"))
        (s_h4, s_hv4, s_hh4, s_hl4, s_o4, s_y4, s_cv, s_ce) = (
            sem(f"s_{n}") for n in ("h4", "hv4", "hh4", "hl4", "o4", "y4", "cv", "ce"))
        m_x = bank[4:6]
        m_c = bank[6:8]
        m_h = bank[4:8]
        m_o = bank[0:4]
        X4 = 2

        def x4_tile(part, p):
            return (x4a, x4b)[p // HP][:, part, :, p % HP * P:(p % HP + 1) * P]

        def sp_loads4(sp):
            sp.wait_ge(s_y2, PAIRS)
            down_t = a["L1_ffn_lora_down"].rearrange("e (t p) r -> t p e r", p=P)
            for t in range(KT):
                sp.dma_start(draw[:, t, :].rearrange("p (e r) -> p e r", e=EXP), down_t[t]).then_inc(s_ld_d[t], 16)
            sp.dma_start(uraw[:, :, :], a["L1_ffn_lora_up"].rearrange("e r o -> (e r) o")
                         .rearrange("(t p) o -> p t o", p=P)).then_inc(s_ld_u, 16)
            sp.dma_start(worg[:, :, :], a["L1_ffn_W_org"].rearrange("(t p) i -> p t i", p=P)).then_inc(s_ld_o, 16)
            sp.dma_start(wq1[:, :], a["L1_ffn_Wq"]).then_inc(s_ld_q, 16)
            sp.dma_start(keys[:, :], a["L1_ffn_lora_keys"]).then_inc(s_ld_q, 16)

        def sp_l1f(sp):
            for p in range(PAIRS):
                sp.wait_ge(s_y4, p + 1)
                sp.dma_start(out_t[p], acc[:, p, :]).then_inc(s_out, 16)
            sp.wait_ge(s_out, 16 * PAIRS)

        def pool_ahead4(j):
            pool = nc.gpsimd
            n = (j - 50) // 2
            if j % 2 == 0 and 0 <= n < 2 * KT:
                t = n % KT
                if n < KT:
                    pool.wait_ge(s_dnh, t + 1)
                    pool.tensor_tensor(dn[:, LO, t, :], draw[:, t, :], dn[:, HI, t, :].bitcast(F32),
                                       ALU.subtract).then_inc(s_dnl, 1)
                else:
                    pool.wait_ge(s_uph, t + 1)
                    pool.tensor_tensor(up[:, LO, t, :], uraw[:, t, :], up[:, HI, t, :].bitcast(F32),
                                       ALU.subtract).then_inc(s_upl, 1)
            for p in {64: (0, 1), 65: (2, 3), 70: (4, 5)}.get(j, ()):
                ln_power(pool, X4, p)

        def act_ahead4(j):
            act = nc.scalar
            n = (j - 48) // 2
            if j % 2 == 0 and 0 <= n < 2 * KT:
                t = n % KT
                if n < KT:
                    act.wait_ge(s_ld_d[t], 16)
                    act.activation(dn[:, HI, t, :], draw[:, t, :], ACT.Copy).then_inc(s_dnh, 1)
                else:
                    act.wait_ge(s_ld_u, 16)
                    act.activation(up[:, HI, t, :], uraw[:, t, :], ACT.Copy).then_inc(s_uph, 1)
            if j == 65:
                worg_hi(act, 0)
                worg_hi(act, 1)
            if j == 66:
                x4_hi(act, 0)
                x4_hi(act, 1)
            if j == 69:
                x4_hi(act, 2)
                x4_hi(act, 3)
            if j == 71:
                worg_hi(act, 2)
                worg_hi(act, 3)

        def pe_ahead4(j):
            pe = nc.tensor
            if j == 64:
                pe.wait_ge(s_ld_o, 16)
                pe.wait_ge(s_e1, TILES)
                worg_transposes(pe, 0)
                worg_transposes(pe, 1)
            if j == 66:
                x4_transposes(pe, 0)
                x4_transposes(pe, 1)
            if j == 68:
                x4_transposes(pe, 2)
                x4_transposes(pe, 3)
            if j == 71:
                pe.wait_ge(s_p1l, TILES - 1)
                pe.wait_ge(s_y3, PAIRS - 1)
                worg_transposes(pe, 2)
                worg_transposes(pe, 3)

        def dve_ahead4(j):
            dve = nc.vector
            for p in {63: (0, 1), 64: (2, 3), 69: (4,), 70: (5,)}.get(j, ()):
                dve.wait_ge(s_y3, p + 1)
                ln_stats(dve, X4, p)
            if j == 65:
                x4_apply(dve, 0)
                x4_apply(dve, 1)
            if j == 66:
                worg_lo(dve, 0)
                worg_lo(dve, 1)
            if j == 67:
                x4_lo(dve, 0)
                x4_lo(dve, 1)
            if j == 68:
                x4_apply(dve, 2)
                x4_apply(dve, 3)
            if j == 70:
                x4_lo(dve, 2)
                x4_lo(dve, 3)
            if j == 71:
                worg_lo(dve, 2)
                worg_lo(dve, 3)
                x4_apply(dve, 4)
                x4_apply(dve, 5)

        def worg_transposes(pe, it):
            for ot in range(KT):
                mm = pe.transpose(m_o[it][:, ot * P:(ot + 1) * P], worg[:, ot, it * P:(it + 1) * P], ident[:, :])
            mm.then_inc(s_wot, 1)

        def worg_hi(act, t):
            act.wait_ge(s_wot, t + 1)
            act.activation(woT[:, HI, t, :], m_o[t][:, :], ACT.Copy).then_inc(s_woh, 1)

        def worg_lo(dve, t):
            dve.wait_ge(s_woh, t + 1)
            dve.tensor_tensor(woT[:, LO, t, :], m_o[t][:, :], woT[:, HI, t, :].bitcast(F32), ALU.subtract).then_inc(s_wol, 1)

        def x4_apply(dve, p):
            if p >= 2:
                dve.wait_ge(s_tx4, p - 1)
            ln_apply(dve, X4, p, xn4[:, p % 2, :])

        def x4_transposes(pe, p):
            pe.wait_ge(s_xn, X4 * PAIRS + p + 1)
            if p >= 2:
                pe.wait_ge(s_x4l, p - 1)
                pe.wait_ge(s_mean, p - 1)
            for kt in range(KT):
                mm = pe.transpose(m_x[p % 2][:, kt * P:(kt + 1) * P], xn4[:, p % 2, kt * P:(kt + 1) * P], ident[:, :])
            mm.then_inc(s_tx4, 1)

        def x4_hi(act, p):
            act.wait_ge(s_tx4, p + 1)
            act.activation(x4_tile(HI, p), tiles(m_x[p % 2]), ACT.Copy).then_inc(s_x4h, 1)

        def x4_lo(dve, p):
            dve.wait_ge(s_x4h, p + 1)
            dve.tensor_tensor(x4_tile(LO, p), tiles(m_x[p % 2]), x4_tile(HI, p).bitcast(F32), ALU.subtract).then_inc(s_x4l, 1)
            dve.tensor_reduce(meanT[:, :, 2 * p:2 * p + 2], m_x[p % 2][:, :].rearrange("p (k b t) -> p k b t", k=KT, b=2),
                              AX, ALU.add).then_inc(s_mean, 1)

        def pool_l1f(pool):
            ln_power(pool, X4, PAIRS - 2)
            ln_power(pool, X4, PAIRS - 1)
            for n in range(2 * KT):
                half, t = divmod(n, KT)
                cols = slice(half * HALF, (half + 1) * HALF)
                pool.wait_ge(s_hh4, n + 1)
                pool.tensor_tensor(hs[:, LO, t, cols], hval4[:, n % 2, :], hs[:, HI, t, cols].bitcast(F32),
                                   ALU.subtract).then_inc(s_hl4, 1)

        def pe_l1f(pe):
            def base(p):
                pe.wait_ge(s_x4l, p + 1)
                if p >= HP:
                    pe.wait_ge(s_y4, p - HP + 1)
                for kt in range(KT):
                    for k, (l, r) in enumerate(PASSES):
                        pe.matmul(m_o[p % HP][:, :], x4_tile(l, p)[:, kt, :], woT[:, r, kt, :],
                                  start=(kt == 0 and k == 0), stop=False)

            def delta(p):
                pe.wait_ge(s_hl4, KT * (p // HP + 1))
                for t in range(KT):
                    for k, (l, r) in enumerate(PASSES):
                        mm = pe.matmul(m_o[p % HP][:, :], hs[:, l, t, p * P:(p + 1) * P], up[:, r, t, :],
                                       start=False, stop=(t == KT - 1 and k == 2))
                mm.then_inc(s_o4, 1)

            def low_rank(n):
                half, j = divmod(n, KT)
                if n >= 4:
                    pe.wait_ge(s_hv4, n - 3)
                for kt in range(KT):
                    for k, (l, r) in enumerate(PASSES):
                        mm = pe.matmul(m_h[n % 4][:, :], dn[:, l, kt, j * P:(j + 1) * P], (x4a, x4b)[half][:, r, kt, :],
                                       start=(kt == 0 and k == 0), stop=(kt == KT - 1 and k == 2))
                mm.then_inc(s_h4, 1)

            pe.wait_ge(s_wol, KT)
            for p in range(HP):
                base(p)
                if p == 0:
                    x4_transposes(pe, HP)
                if p == 1:
                    pe.wait_ge(s_ld_q, 32)
                    pe.wait_ge(s_y3, PAIRS)
                    for kt in range(KT):
                        pe.transpose(m_c[0][:, kt * P:(kt + 1) * P], wq1[:, kt * P:(kt + 1) * P], ident[:, :])
                    pe.transpose(m_c[1][:, 0:EXP], keys[:, :], ident[0:EXP, 0:EXP]).then_inc(s_sm, 1)
                if p + 1 < HP:
                    x4_transposes(pe, HP + p + 1)
            pe.wait_ge(s_mean, PAIRS)
            pe.wait_ge(s_x4l, PAIRS)
            pe.wait_ge(s_smc, 2)
            for kt in range(KT):
                mm = pe.matmul(m_c[0][:, 0:B], wq1T[:, kt, :], meanT[:, kt, :], start=(kt == 0), stop=(kt == KT - 1))
            mm.then_inc(s_sm, 1)
            pe.wait_ge(s_dnl, KT)
            low_rank(0)
            pe.wait_ge(s_smc, 3)
            pe.matmul(m_c[1][0:B, 0:EXP], q1T[:, :], keysT[:, :], start=True, stop=True).then_inc(s_sm, 1)
            low_rank(1)
            pe.wait_ge(s_cv, 5)
            for t in range(KT):
                mm = pe.transpose(m_c[0][:, t * B:(t + 1) * B],
                                  cexp[:, :, :].rearrange("b e r -> b (e r)")[:, t * P:(t + 1) * P], ident[0:B, 0:B])
            mm.then_inc(s_sm, 1)
            pe.wait_ge(s_smc, 4)
            low_rank(2)
            low_rank(3)
            pe.wait_ge(s_upl, KT)
            for n in range(KT):
                low_rank(KT + n)
                delta(n)
            for p in range(HP, PAIRS):
                base(p)
                delta(p)

        def act_l1f(act):
            for p in range(HP, PAIRS):
                x4_hi(act, p)
                if p == HP + 1:
                    act.wait_ge(s_sm, 1)
                    act.activation(wq1T[:, :, :].rearrange("p t k -> p (t k)"), m_c[0][:, :], ACT.Copy).then_inc(s_smc, 1)
                    act.activation(keysT[:, :], m_c[1][:, 0:EXP], ACT.Copy).then_inc(s_smc, 1)
            act.wait_ge(s_sm, 2)
            act.activation(q1T[:, :], m_c[0][:, 0:B], ACT.Copy, scale=1.0 / T).then_inc(s_smc, 1)
            act.wait_ge(s_cv, 2)
            act.activation(cf[:, :], lg[:, :], ACT.Exp, bias=cstat[:, 0:1], accum_out=cstat[:, 1:2]).then_inc(s_ce, 1)
            act.wait_ge(s_sm, 4)
            act.activation(cT[:, :, :].rearrange("p t b -> p (t b)"), m_c[0][:, 0:KT * B], ACT.Copy).then_inc(s_smc, 1)
            for n in range(2 * KT):
                half, t = divmod(n, KT)
                act.wait_ge(s_hv4, n + 1)
                act.activation(hs[:, HI, t, half * HALF:(half + 1) * HALF], hval4[:, n % 2, :], ACT.Copy).then_inc(s_hh4, 1)

        def dve_l1f(dve):
            dve.wait_ge(s_y3, PAIRS)
            ln_stats(dve, X4, PAIRS - 2)
            ln_stats(dve, X4, PAIRS - 1)
            for p in range(HP, PAIRS):
                x4_lo(dve, p)
                if p + 2 < PAIRS:
                    x4_apply(dve, p + 2)
            dve.wait_ge(s_sm, 3)
            dve.tensor_scalar(lg[:, :], m_c[1][0:B, 0:EXP], float(KD) ** -0.5, None, ALU.mult).then_inc(s_cv, 1)
            dve.wait_ge(s_cv, 1)
            dve.tensor_reduce(cstat[:, 0:1], lg[:, :], AX, ALU.max, negate=True).then_inc(s_cv, 1)
            dve.wait_ge(s_ce, 1)
            dve.reciprocal(cstat[:, 2:3], cstat[:, 1:2]).then_inc(s_cv, 1)
            dve.wait_ge(s_cv, 3)
            dve.tensor_scalar(lg[:, :], cf[:, :], cstat[:, 2:3], None, ALU.mult).then_inc(s_cv, 1)
            dve.wait_ge(s_cv, 4)
            dve.tensor_copy(cexp[:, :, :], lg[:, :].unsqueeze(2).to_broadcast([B, EXP, RANK])).then_inc(s_cv, 1)
            dve.wait_ge(s_smc, 4)

            def add_out(p):
                dve.wait_ge(s_o4, p + 1)
                dve.tensor_tensor(acc[:, p, :], m_o[p % HP][:, :], acc[:, p, :], ALU.add).then_inc(s_y4, 1)

            for n in range(2 * KT):
                half, t = divmod(n, KT)
                dve.wait_ge(s_h4, n + 1)
                if n >= 2:
                    dve.wait_ge(s_hl4, n - 1)
                dve.tensor_tensor(hval4[:, n % 2, :].rearrange("p (b t) -> p b t", t=T),
                                  m_h[n % 4][:, :].rearrange("p (b t) -> p b t", t=T),
                                  cT[:, t, half * B // 2:(half + 1) * B // 2].unsqueeze(2).to_broadcast([P, B // 2, T]),
                                  ALU.mult).then_inc(s_hv4, 1)
                if n > KT:
                    add_out(n - KT - 1)
            for p in range(HP - 1, PAIRS):
                add_out(p)


        s_out = sem("s_out")

        @block.sync
        def _(sp):
            sp_first(sp)
            sp_ffn(sp)
            sp_l1x(sp)
            sp_l1f(sp)

        @block.gpsimd
        def _(pool):
            pool.memset(ident[:, :], 0.0).then_inc(s_const, 1)
            pool.memset(half_neg[:, :], -0.5).then_inc(s_const, 1)
            pool.memset(inv_sqrt_t[:, :], float(T) ** -0.5).then_inc(s_const, 1)
            pool.wait_ge(s_const, 3)
            pool.affine_select(out=ident[:, :], in_=ident[:, :], compare_op=ALU.not_equal, fill=1.0, base=0,
                               pattern=[[-1, P]], channel_multiplier=1).then_inc(s_const, 1)
            pool_first(pool)
            pool_ffn(pool)
            pool_l1x(pool)
            pool_l1f(pool)

        @block.tensor
        def _(pe):
            pe_first(pe)
            pe_ffn(pe)
            pe_l1x(pe)
            pe_l1f(pe)

        @block.scalar
        def _(act):
            act_first(act)
            act_ffn(act)
            act_l1x(act)
            act_l1f(act)

        @block.vector
        def _(dve):
            dve_first(dve)
            dve_ffn(dve)
            dve_l1x(dve)
            dve_l1f(dve)


def kernel(**inputs):
    import numpy as _np
    import concourse.bacc as _bacc
    from concourse.bass_utils import run_bass_kernel_spmd as _run

    nc = _bacc.Bacc("TRN2", target_bir_lowering=False, num_devices=1)
    arrays, aps = {}, {}
    for name, value in inputs.items():
        v = _np.ascontiguousarray(value)
        arrays[f"in_{name}_dram"] = v
        aps[name] = nc.dram_tensor(f"in_{name}_dram", v.shape, mybir.dt.from_np(v.dtype), kind="ExternalInput").ap()
    out = nc.dram_tensor("out_0_dram", inputs["x"].shape, F32, kind="ExternalOutput").ap()
    block_kernel(nc, aps, out)
    r = _run(nc, [arrays], core_ids=[0])
    return r.results[0]["out_0_dram"]
```
